# Optimizing a Trainium2 kernel written in Bass

```python
import numpy as np
import jax
import jax.numpy as jnp

def _softmax(x, axis=-1):
    return jax.nn.softmax(x, axis=axis)

def _gelu(x):
    return jax.nn.gelu(x, approximate=True)

def _silu(x):
    return jax.nn.silu(x)

def _sigmoid(x):
    return jax.nn.sigmoid(x)

def _layernorm(x, axis=-1, eps=1e-05):
    m = jnp.mean(x, axis=axis, keepdims=True)
    v = jnp.var(x, axis=axis, keepdims=True)
    return (x - m) / jnp.sqrt(v + eps)

def _scatter_add(tgt, idx, src, axis=0):
    return tgt.at[idx].add(src)

def _segment_sum(src, seg, n):
    return jax.ops.segment_sum(src, seg, n)
kernel_name = 'mk_adaln_d2_jaxref_r8_9cff30'

def setup_inputs(seed: int=0):
    np.random.seed(seed)
    _w = jnp.asarray

    def _L0_attn_setup():
        import jax, jax.numpy as jnp
        import numpy as np
        D_MODEL = 128
        N_LAYERS = 2
        D_STATE = 16
        EXPAND = 2
        D_CONV = 4
        ED = EXPAND * D_MODEL
        DT_RANK = 64
        BATCH = 1
        SEQ = 256
        EPS = 1e-05

        def _scan_op(c1, c2):
            a1, b1 = c1
            a2, b2 = c2
            return (a1 * a2, a2 * b1 + b2)

        def _mamba_block(x, norm_w, Win, conv_w, conv_b, Wx, Wdt, bdt, A_log, Dp, Wout):
            xn = x * jax.lax.rsqrt(jnp.mean(x * x, axis=-1, keepdims=True) + EPS) * norm_w
            xz = jnp.einsum('bld,ed->ble', xn, Win)
            xc, z = jnp.split(xz, 2, axis=-1)
            h = jax.lax.conv_general_dilated(xc.transpose(0, 2, 1), conv_w[:, None, :], window_strides=(1,), padding=[(D_CONV - 1, 0)], dimension_numbers=('NCH', 'OIH', 'NCH'), feature_group_count=ED)
            xc = jax.nn.silu((h + conv_b[None, :, None]).transpose(0, 2, 1))
            dBC = jnp.einsum('ble,re->blr', xc, Wx)
            dt, Bm, Cm = jnp.split(dBC, [DT_RANK, DT_RANK + D_STATE], axis=-1)
            delta = jax.nn.softplus(jnp.einsum('blr,er->ble', dt, Wdt) + bdt)
            A = -jnp.exp(A_log)
            deltaA = jnp.exp(delta[..., None] * A)
            BX = (delta * xc)[..., None] * Bm[:, :, None, :]
            hs = jax.lax.associative_scan(_scan_op, (deltaA, BX), axis=1)[1]
            y = jnp.einsum('blen,bln->ble', hs, Cm) + Dp * xc
            out = jnp.einsum('ble,de->bld', y * jax.nn.silu(z), Wout)
            return out
        key = jax.random.key(seed)
        ks = jax.random.split(key, 8)
        rn = lambda k, shape, s: jax.random.normal(k, shape, dtype=jnp.float32) * s
        x = jax.random.normal(ks[0], (BATCH, SEQ, D_MODEL), dtype=jnp.float32)
        norm_w = jnp.ones((N_LAYERS, D_MODEL), jnp.float32)
        Win = rn(ks[1], (N_LAYERS, 2 * ED, D_MODEL), D_MODEL ** (-0.5))
        conv_w = rn(ks[2], (N_LAYERS, ED, D_CONV), D_CONV ** (-0.5))
        conv_b = jnp.zeros((N_LAYERS, ED), jnp.float32)
        Wx = rn(ks[3], (N_LAYERS, DT_RANK + 2 * D_STATE, ED), ED ** (-0.5))
        Wdt = rn(ks[4], (N_LAYERS, ED, DT_RANK), DT_RANK ** (-0.5))
        dt = jnp.exp(jax.random.uniform(ks[5], (N_LAYERS, ED)) * (np.log(0.1) - np.log(0.001)) + np.log(0.001))
        bdt = dt + jnp.log(-jnp.expm1(-dt))
        A_log = jnp.log(jnp.broadcast_to(jnp.arange(1, D_STATE + 1, dtype=jnp.float32), (N_LAYERS, ED, D_STATE)))
        Dp = jnp.ones((N_LAYERS, ED), jnp.float32)
        Wout = rn(ks[6], (N_LAYERS, D_MODEL, ED), ED ** (-0.5))
        return dict(x=x, norm_w=norm_w, Win=Win, conv_w=conv_w, conv_b=conv_b, Wx=Wx, Wdt=Wdt, bdt=bdt, A_log=A_log, Dp=Dp, Wout=Wout)
    _L0_attn_in = _L0_attn_setup()

    def _L0_ffn_setup():
        import jax, jax.numpy as jnp
        import numpy as np
        N_HEAD, N_ACTIVE, D_MODEL, D_ATTN = (16, 4, 128, 64)
        key = jax.random.key(seed)
        ks = jax.random.split(key, 12)
        s = 0.02
        B, S = (2, 512)
        return {'x': jax.random.normal(ks[0], (B, S, D_MODEL), dtype=jnp.float32), 'Wq': jax.random.normal(ks[1], (D_MODEL, N_HEAD * D_ATTN), dtype=jnp.float32) * s, 'bq': jnp.zeros((N_HEAD * D_ATTN,), dtype=jnp.float32), 'Wk': jax.random.normal(ks[2], (D_MODEL, N_HEAD * D_ATTN), dtype=jnp.float32) * s, 'bk': jnp.zeros((N_HEAD * D_ATTN,), dtype=jnp.float32), 'Wv': jax.random.normal(ks[3], (D_MODEL, N_HEAD * D_ATTN), dtype=jnp.float32) * s, 'bv': jnp.zeros((N_HEAD * D_ATTN,), dtype=jnp.float32), 'Wr': jax.random.normal(ks[4], (D_MODEL, N_HEAD), dtype=jnp.float32) * s, 'br': jnp.zeros((N_HEAD,), dtype=jnp.float32), 'Wo': jax.random.normal(ks[5], (N_ACTIVE * D_ATTN, D_MODEL), dtype=jnp.float32) * s, 'bo': jnp.zeros((D_MODEL,), dtype=jnp.float32)}
    _L0_ffn_in = _L0_ffn_setup()
    _L0_c = _w((lambda *s: np.random.randn(*s).astype(np.float32) * 0.05)(2, 128))
    _L0_wmod = _w((lambda *s: np.random.randn(*s).astype(np.float32) * 0.05)(128, 6 * 128) * 128 ** (-0.5))

    def _L1_attn_setup():
        import math
        import jax, jax.numpy as jnp
        import numpy as np
        HEADS = 16
        REL_WINDOW = 128
        key = jax.random.key(seed)
        k1, k2, k3, k4, k5 = jax.random.split(key, 5)
        b, s, d = (2, 256, 128)
        hd = d // HEADS
        R = 2 * REL_WINDOW + 1
        return {'x': jax.random.normal(k1, (b, s, d), dtype=jnp.float32), 'Wqkv': jax.random.normal(k2, (3 * d, d), dtype=jnp.float32) * (1.0 / math.sqrt(d)), 'bqkv': jax.random.normal(k3, (3 * d,), dtype=jnp.float32) * 0.02, 'Wr': jax.random.normal(k4, (R, hd), dtype=jnp.float32) * (1.0 / math.sqrt(hd)), 'br': jax.random.normal(k5, (R,), dtype=jnp.float32) * 0.02}
    _L1_attn_in = _L1_attn_setup()

    def _L1_ffn_setup():
        import jax, jax.numpy as jnp
        import numpy as np
        DIM = 128
        HIDDEN = 512
        E = 8
        B, S = (2, 512)
        key = jax.random.key(seed)
        ks = jax.random.split(key, 8)
        sd = 1.0 / np.sqrt(DIM)
        sh = 1.0 / np.sqrt(HIDDEN)
        return {'x': jax.random.normal(ks[0], (B, S, DIM), dtype=jnp.float32), 'router_w': jax.random.uniform(ks[1], (DIM, E), jnp.float32, -sd, sd), 'router_b': jax.random.uniform(ks[2], (E,), jnp.float32, -sd, sd), 'w1': jax.random.uniform(ks[3], (E, DIM, 2 * HIDDEN), jnp.float32, -sd, sd), 'b1': jax.random.uniform(ks[4], (E, 2 * HIDDEN), jnp.float32, -sd, sd), 'w2': jax.random.uniform(ks[5], (E, HIDDEN, DIM), jnp.float32, -sh, sh), 'b2': jax.random.uniform(ks[6], (E, DIM), jnp.float32, -sh, sh)}
    _L1_ffn_in = _L1_ffn_setup()
    _L1_c = _w((lambda *s: np.random.randn(*s).astype(np.float32) * 0.05)(2, 128))
    _L1_wmod = _w((lambda *s: np.random.randn(*s).astype(np.float32) * 0.05)(128, 6 * 128) * 128 ** (-0.5))
    _d = {'L0_attn_x': _L0_attn_in['x'], 'L0_attn_norm_w': _L0_attn_in['norm_w'], 'L0_attn_Win': _L0_attn_in['Win'], 'L0_attn_conv_w': _L0_attn_in['conv_w'], 'L0_attn_conv_b': _L0_attn_in['conv_b'], 'L0_attn_Wx': _L0_attn_in['Wx'], 'L0_attn_Wdt': _L0_attn_in['Wdt'], 'L0_attn_bdt': _L0_attn_in['bdt'], 'L0_attn_A_log': _L0_attn_in['A_log'], 'L0_attn_Dp': _L0_attn_in['Dp'], 'L0_attn_Wout': _L0_attn_in['Wout'], 'L0_ffn_Wq': _L0_ffn_in['Wq'], 'L0_ffn_bq': _L0_ffn_in['bq'], 'L0_ffn_Wk': _L0_ffn_in['Wk'], 'L0_ffn_bk': _L0_ffn_in['bk'], 'L0_ffn_Wv': _L0_ffn_in['Wv'], 'L0_ffn_bv': _L0_ffn_in['bv'], 'L0_ffn_Wr': _L0_ffn_in['Wr'], 'L0_ffn_br': _L0_ffn_in['br'], 'L0_ffn_Wo': _L0_ffn_in['Wo'], 'L0_ffn_bo': _L0_ffn_in['bo'], 'L0_c': _L0_c, 'L0_wmod': _L0_wmod, 'L1_attn_Wqkv': _L1_attn_in['Wqkv'], 'L1_attn_bqkv': _L1_attn_in['bqkv'], 'L1_attn_Wr': _L1_attn_in['Wr'], 'L1_attn_br': _L1_attn_in['br'], 'L1_ffn_router_w': _L1_ffn_in['router_w'], 'L1_ffn_router_b': _L1_ffn_in['router_b'], 'L1_ffn_w1': _L1_ffn_in['w1'], 'L1_ffn_b1': _L1_ffn_in['b1'], 'L1_ffn_w2': _L1_ffn_in['w2'], 'L1_ffn_b2': _L1_ffn_in['b2'], 'L1_c': _L1_c, 'L1_wmod': _L1_wmod}
    _x0 = _d['L0_attn_x']
    _d['L0_attn_x'] = jax.random.normal(jax.random.fold_in(jax.random.key(seed), 1), (2, 1024, 128), dtype=_x0.dtype)
    del _x0
    return _d

def reference(L0_attn_x, L0_attn_norm_w, L0_attn_Win, L0_attn_conv_w, L0_attn_conv_b, L0_attn_Wx, L0_attn_Wdt, L0_attn_bdt, L0_attn_A_log, L0_attn_Dp, L0_attn_Wout, L0_ffn_Wq, L0_ffn_bq, L0_ffn_Wk, L0_ffn_bk, L0_ffn_Wv, L0_ffn_bv, L0_ffn_Wr, L0_ffn_br, L0_ffn_Wo, L0_ffn_bo, L0_c, L0_wmod, L1_attn_Wqkv, L1_attn_bqkv, L1_attn_Wr, L1_attn_br, L1_ffn_router_w, L1_ffn_router_b, L1_ffn_w1, L1_ffn_b1, L1_ffn_w2, L1_ffn_b2, L1_c, L1_wmod):

    def _L0_attn_ref(x, norm_w, Win, conv_w, conv_b, Wx, Wdt, bdt, A_log, Dp, Wout):
        import jax, jax.numpy as jnp
        import numpy as np
        D_MODEL = 128
        N_LAYERS = 2
        D_STATE = 16
        EXPAND = 2
        D_CONV = 4
        ED = EXPAND * D_MODEL
        DT_RANK = 64
        BATCH = 1
        SEQ = 256
        EPS = 1e-05

        def _scan_op(c1, c2):
            a1, b1 = c1
            a2, b2 = c2
            return (a1 * a2, a2 * b1 + b2)

        def _mamba_block(x, norm_w, Win, conv_w, conv_b, Wx, Wdt, bdt, A_log, Dp, Wout):
            xn = x * jax.lax.rsqrt(jnp.mean(x * x, axis=-1, keepdims=True) + EPS) * norm_w
            xz = jnp.einsum('bld,ed->ble', xn, Win)
            xc, z = jnp.split(xz, 2, axis=-1)
            h = jax.lax.conv_general_dilated(xc.transpose(0, 2, 1), conv_w[:, None, :], window_strides=(1,), padding=[(D_CONV - 1, 0)], dimension_numbers=('NCH', 'OIH', 'NCH'), feature_group_count=ED)
            xc = jax.nn.silu((h + conv_b[None, :, None]).transpose(0, 2, 1))
            dBC = jnp.einsum('ble,re->blr', xc, Wx)
            dt, Bm, Cm = jnp.split(dBC, [DT_RANK, DT_RANK + D_STATE], axis=-1)
            delta = jax.nn.softplus(jnp.einsum('blr,er->ble', dt, Wdt) + bdt)
            A = -jnp.exp(A_log)
            deltaA = jnp.exp(delta[..., None] * A)
            BX = (delta * xc)[..., None] * Bm[:, :, None, :]
            hs = jax.lax.associative_scan(_scan_op, (deltaA, BX), axis=1)[1]
            y = jnp.einsum('blen,bln->ble', hs, Cm) + Dp * xc
            out = jnp.einsum('ble,de->bld', y * jax.nn.silu(z), Wout)
            return out
        for i in range(N_LAYERS):
            x = x + _mamba_block(x, norm_w[i], Win[i], conv_w[i], conv_b[i], Wx[i], Wdt[i], bdt[i], A_log[i], Dp[i], Wout[i])
        return x

    def _L0_ffn_ref(x, Wq, bq, Wk, bk, Wv, bv, Wr, br, Wo, bo):
        import jax, jax.numpy as jnp
        import numpy as np
        N_HEAD, N_ACTIVE, D_MODEL, D_ATTN = (16, 4, 128, 64)
        B, S, D = x.shape
        H, K, dh = (N_HEAD, N_ACTIVE, D_ATTN)
        dist = jax.nn.softmax(jnp.mean(x @ Wr + br, axis=1), axis=-1)
        top_vals, top_idx = jax.lax.top_k(dist, K)
        sparse = jnp.zeros_like(dist).at[jnp.arange(B)[:, None], top_idx].set(top_vals)
        gates_all = jax.nn.softmax(sparse, axis=1)
        g = jnp.take_along_axis(gates_all, top_idx, axis=1)[:, :, None, None]

        def proj(W, b):
            return (x @ W + b).reshape(B, S, H, dh).transpose(0, 2, 1, 3)
        Q, Kt, V = (proj(Wq, bq), proj(Wk, bk), proj(Wv, bv))
        idx = top_idx[:, :, None, None]
        Qk = jnp.take_along_axis(Q, idx, axis=1) * g
        Kk = jnp.take_along_axis(Kt, idx, axis=1) * g
        Vk = jnp.take_along_axis(V, idx, axis=1) * g
        scores = jnp.einsum('bksd,bktd->bkst', Qk, Kk) / jnp.sqrt(jnp.float32(dh))
        attn = jax.nn.softmax(scores, axis=-1)
        out = jnp.einsum('bkst,bktd->bksd', attn, Vk)
        out = out.transpose(0, 2, 1, 3).reshape(B, S, K * dh)
        return out @ Wo + bo

    def _L1_attn_ref(x, Wqkv, bqkv, Wr, br):
        import math
        import jax, jax.numpy as jnp
        import numpy as np
        HEADS = 16
        REL_WINDOW = 128
        b, s, d = x.shape
        h = HEADS
        hd = d // h
        w = REL_WINDOW
        scale = math.sqrt(d / h)
        qkv = (x @ Wqkv.T + bqkv).reshape(b, s, h, 3 * hd)
        q, k, v = jnp.split(qkv, 3, axis=-1)
        q = q.transpose(0, 2, 1, 3)
        k = k.transpose(0, 2, 1, 3)
        v = v.transpose(0, 2, 1, 3)
        content = jnp.einsum('bhik,bhjk->bhij', q, k) / scale
        idx = jnp.arange(s)
        offsets = jnp.clip(idx[None, :] - idx[:, None], -w, w) + w
        rp = jnp.einsum('bhik,rk->bhir', q, Wr) + br
        pos = jnp.take_along_axis(rp, jnp.broadcast_to(offsets, (b, h, s, s)), axis=-1)
        attn = jax.nn.softmax(content + pos, axis=-1)
        out = jnp.einsum('bhij,bhjk->bhik', attn, v)
        return out.transpose(0, 2, 1, 3).reshape(b, s, d)

    def _L1_ffn_ref(x, router_w, router_b, w1, b1, w2, b2):
        import jax, jax.numpy as jnp
        import numpy as np
        DIM = 128
        HIDDEN = 512
        E = 8
        B, S = (2, 512)
        logits = jnp.einsum('bsd,de->bse', x, router_w) + router_b
        probs = jax.nn.softmax(logits, axis=-1)
        top1 = jnp.argmax(probs, axis=-1)
        out = jnp.zeros_like(x)
        for i in range(E):
            h = jnp.einsum('bsd,df->bsf', x, w1[i]) + b1[i]
            a, g = jnp.split(h, 2, axis=-1)
            y = jnp.einsum('bsh,hd->bsd', a * jax.nn.sigmoid(g), w2[i]) + b2[i]
            out = out + jnp.where((top1 == i)[..., None], y, 0.0)
        return out
    x = L0_attn_x
    mod = (_silu(L0_c) @ L0_wmod).reshape(L0_c.shape[0], 6, 1, -1)
    sa, ca, ga, sb, cb, gb = (mod[:, 0], mod[:, 1], mod[:, 2], mod[:, 3], mod[:, 4], mod[:, 5])
    ga = (2 * (ga >= 0) - 1) * jnp.maximum(jnp.abs(ga), 0.25)
    gb = (2 * (gb >= 0) - 1) * jnp.maximum(jnp.abs(gb), 0.25)
    h = _layernorm(x, axis=-1) * (1 + ca) + sa
    x = x + ga * _L0_attn_ref(h, L0_attn_norm_w, L0_attn_Win, L0_attn_conv_w, L0_attn_conv_b, L0_attn_Wx, L0_attn_Wdt, L0_attn_bdt, L0_attn_A_log, L0_attn_Dp, L0_attn_Wout)
    h = _layernorm(x, axis=-1) * (1 + cb) + sb
    x = x + gb * _L0_ffn_ref(h, L0_ffn_Wq, L0_ffn_bq, L0_ffn_Wk, L0_ffn_bk, L0_ffn_Wv, L0_ffn_bv, L0_ffn_Wr, L0_ffn_br, L0_ffn_Wo, L0_ffn_bo)
    mod = (_silu(L1_c) @ L1_wmod).reshape(L1_c.shape[0], 6, 1, -1)
    sa, ca, ga, sb, cb, gb = (mod[:, 0], mod[:, 1], mod[:, 2], mod[:, 3], mod[:, 4], mod[:, 5])
    ga = (2 * (ga >= 0) - 1) * jnp.maximum(jnp.abs(ga), 0.25)
    gb = (2 * (gb >= 0) - 1) * jnp.maximum(jnp.abs(gb), 0.25)
    h = _layernorm(x, axis=-1) * (1 + ca) + sa
    x = x + ga * _L1_attn_ref(h, L1_attn_Wqkv, L1_attn_bqkv, L1_attn_Wr, L1_attn_br)
    h = _layernorm(x, axis=-1) * (1 + cb) + sb
    x = x + gb * _L1_ffn_ref(h, L1_ffn_router_w, L1_ffn_router_b, L1_ffn_w1, L1_ffn_b1, L1_ffn_w2, L1_ffn_b2)
    return x

_drawn_inputs = setup_inputs


def setup_inputs(seed=0):
    import zlib

    import numpy as np

    out = dict(_drawn_inputs(seed))
    spreads = {'L0_attn_norm_w': (1.0, 0.2),
     'L0_attn_conv_b': (0.0, 0.436),
     'L0_attn_Dp': (1.0, 0.2),
     'L0_ffn_bq': (0.0, 2.0),
     'L0_ffn_bk': (0.0, 2.0),
     'L0_ffn_bv': (0.0, 0.8),
     'L0_ffn_br': (0.0, 0.8),
     'L0_ffn_bo': (0.0, 0.317)}
    factors = {'L0_attn_Wdt': 11.563,
     'L0_attn_bdt': 14.984,
     'L0_attn_A_log': 10.013,
     'L0_ffn_Wq': 64.0,
     'L0_ffn_Wk': 64.0,
     'L0_ffn_Wv': 64.0,
     'L0_ffn_Wr': 32.883,
     'L0_ffn_Wo': 8.0,
     'L1_attn_bqkv': 8.0,
     'L1_attn_Wr': 2.762,
     'L1_attn_br': 42.404,
     'L1_ffn_router_b': 4.148,
     'L1_ffn_b1': 8.0,
     'L1_ffn_b2': 8.0}
    for name, (base, spread) in spreads.items():
        noise = np.random.default_rng([zlib.crc32(name.encode()), seed]).standard_normal(out[name].shape)
        drawn = base * np.exp(spread * noise) if base else spread * noise
        out[name] = jnp.asarray(drawn.astype(out[name].dtype))
    for name, factor in factors.items():
        out[name] = (out[name] * factor).astype(out[name].dtype)
    return out
```

```python
from contextlib import ExitStack
import concourse.bass as bass
from concourse import mybir

F32 = mybir.dt.float32
BF16 = mybir.dt.bfloat16
U32 = mybir.dt.uint32
ALU = mybir.AluOpType
ACT = mybir.ActivationFunctionType
AX = mybir.AxisListType

P = 128
NB = 2
SEQ = 1024
TOK = NB * SEQ
D = 128
CH = 512
NCH = TOK // CH
EPS = 1e-5
NL = 2
ED = 256
NH2 = ED // P
NS = 16
RK = 64
NCONV = 4
MOD_S, MOD_C, MOD_G = 0, 1, 2
E_MAMBA_ROWS = 2 * NS


class Core:

    def __init__(self, nc, whole):
        self.nc = nc
        self.whole = whole
        self.sems = []

    def sb(self, stack, name, shape, dt=F32):
        return stack.enter_context(self.nc.sbuf_tensor(name, shape, dt))

    def sem(self, name):
        handle = self.nc.alloc_semaphore(name=name)
        self.sems.append(handle)
        return handle

    def reuse_semaphores(self):
        self.nc.clear_and_free_semaphores(self.sems)
        self.nc.all_engine_barrier()
        self.sems = []


def chunk(c):
    return slice(c * CH, (c + 1) * CH)


def constants_and_modulation(nc, core, T, A):
    with ExitStack() as st:
        cT = core.sb(st, "cT", [P, 2, NB])
        silu_c = core.sb(st, "silu_c", [P, 2, NB])
        wmod = core.sb(st, "wmod", [P, 2, 6 * D])
        sign = core.sb(st, "gate_sign", [P, 2, 2, NB])
        size = core.sb(st, "gate_size", [P, 2, 2, NB])
        x_loaded, c_loaded, wmod_loaded = core.sem("x_loaded"), core.sem("c_loaded"), core.sem("wmod_loaded")
        silu_ready, mod_summed = core.sem("silu_c_ready"), core.sem("mod_summed")
        mod_step, const_ready = core.sem("mod_step"), core.sem("const_ready")
        block = st.enter_context(nc.Block())

        @block.sync
        def _(sp):
            for l in range(2):
                sp.dma_start(cT[:, l, :], A[f"c{l}"]).then_inc(c_loaded, 16)
                sp.dma_start(wmod[:, l, :], A[f"wmod{l}"]).then_inc(wmod_loaded, 16)
            sp.dma_start(T["xT"][:, :], A["xT"]).then_inc(x_loaded, 16)
            sp.wait_ge(x_loaded, 16)

        @block.gpsimd
        def _(pool):
            pool.memset(T["mean_w"][:, :], 1.0 / D).then_inc(const_ready, 1)
            pool.memset(T["ones_bf"][:, :], 1.0).then_inc(const_ready, 1)
            pool.memset(T["ones"][:, :], 1.0).then_inc(const_ready, 1)
            pool.memset(T["eps"][:, :], EPS).then_inc(const_ready, 1)
            pool.memset(T["ident"][:, :], 0.0).then_inc(const_ready, 1)
            pool.wait_ge(const_ready, 5)
            pool.affine_select(out=T["ident"][:, :], in_=T["ident"][:, :], compare_op=ALU.not_equal, fill=1.0,
                               base=0, pattern=[[-1, P]], channel_multiplier=1).then_inc(const_ready, 1)
            pool.wait_ge(const_ready, 6)
            pool.tensor_copy(T["ident_bf"][:, :], T["ident"][:, :]).then_inc(const_ready, 1)

        @block.scalar
        def _(act):
            act.wait_ge(c_loaded, 32)
            act.activation(silu_c[:, :, :], cT[:, :, :], ACT.Silu).then_inc(silu_ready, 1)

        @block.tensor
        def _(pe):
            pe.wait_ge(silu_ready, 1)
            pe.wait_ge(wmod_loaded, 32)
            for l in range(2):
                for j in range(6):
                    at = (l * 6 + j) * NB
                    mm = pe.matmul(T["ps"][:, 0, at:at + NB], wmod[:, l, j * D:(j + 1) * D], silu_c[:, l, :],
                                   start=True, stop=True)
            mm.then_inc(mod_summed, 1)

        @block.vector
        def _(dve):
            mod = T["mod"]
            dve.wait_ge(mod_summed, 1)
            dve.tensor_copy(mod[:, :, :, :].rearrange("p l j b -> p (l j b)"), T["ps"][:, 0, 0:2 * 6 * NB])\
               .then_inc(mod_step, 1)
            dve.wait_ge(mod_step, 1)
            scales = mod[:, :, 1::3, :]
            gates = mod[:, :, 2::3, :]
            dve.tensor_scalar(scales, scales, 1.0, None, ALU.add).then_inc(mod_step, 1)
            dve.tensor_scalar(sign[:, :, :, :], gates, 0.0, 2.0, ALU.is_ge, ALU.mult).then_inc(mod_step, 1)
            dve.scalar_tensor_tensor(out=size[:, :, :, :], in0=gates, scalar=-1.0, in1=gates,
                                     op0=ALU.mult, op1=ALU.max).then_inc(mod_step, 1)
            dve.wait_ge(mod_step, 4)
            dve.tensor_scalar(size[:, :, :, :], size[:, :, :, :], 0.25, None, ALU.max).then_inc(mod_step, 1)
            dve.wait_ge(mod_step, 5)
            dve.scalar_tensor_tensor(out=gates, in0=sign[:, :, :, :], scalar=-1.0, in1=size[:, :, :, :],
                                     op0=ALU.add, op1=ALU.mult).then_inc(mod_step, 1)


def column_means(pe, T, sq, c, bank, first_wait=None):
    for j in range(CH // P):
        t = c * (CH // P) + j
        mm = pe.matmul(T["ps"][:, bank, t:t + 1], sq[:, t * P:(t + 1) * P], T["mean_w"][:, 0:1], start=True, stop=True)
    return mm


def layernorm(nc, core, T, name, layer, part, dst, residual=None):
    x, ps, mod = T["xT"], T["ps"], T["mod"]
    NT = TOK // P
    TC = CH // P
    with ExitStack() as st:
        cen = core.sb(st, name + "_centred", [P, TOK])
        sq = core.sb(st, name + "_square", [P, TOK])
        diag = core.sb(st, name + "_diag", [P, TOK])
        rstd = core.sb(st, name + "_rstd", [P, NT])
        mean_ready, centred, squared = core.sem(name + "_mean"), core.sem(name + "_centred"), core.sem(name + "_squared")
        var_ready, std_ready, rstd_ready = core.sem(name + "_var"), core.sem(name + "_std"), core.sem(name + "_rstd")
        diag_ready, spread = core.sem(name + "_diag"), core.sem(name + "_spread")
        normed, done, x_added = core.sem(name + "_normed"), core.sem(name + "_done"), core.sem(name + "_residual")
        block = st.enter_context(nc.Block())

        @block.tensor
        def _(pe):
            for c in range(NCH):
                if residual is not None:
                    pe.wait_ge(x_added, c + 1)
                pe.matmul(ps[:, c, :], T["mean_w"][:, :], x[:, chunk(c)], start=True, stop=True).then_inc(mean_ready, 1)
            for c in range(NCH):
                pe.wait_ge(squared, c + 1)
                mm = column_means(pe, T, sq, c, 4)
            mm.then_inc(var_ready, 1)
            for c in range(NCH):
                pe.wait_ge(diag_ready, (c + 1) * TC)
                pe.matmul(ps[:, c, :], T["ones"][:, :], diag[:, chunk(c)], start=True, stop=True).then_inc(spread, 1)

        @block.scalar
        def _(act):
            for c in range(NCH):
                act.wait_ge(centred, c + 1)
                act.activation(sq[:, chunk(c)], cen[:, chunk(c)], ACT.Square).then_inc(squared, 1)
            act.wait_ge(var_ready, 1)
            act.activation(rstd[:, :], ps[:, 4, 0:NT], ACT.Sqrt, bias=T["eps"][:, 0:1]).then_inc(std_ready, 1)
            for c in range(NCH):
                b = c * CH // SEQ
                act.wait_ge(normed, c + 1)
                act.activation(dst[:, chunk(c)], cen[:, chunk(c)], ACT.Identity, bias=mod[:, layer, part, b:b + 1])\
                   .then_inc(done, 1)

        @block.vector
        def _(dve):
            if residual is not None:
                src, l, j = residual
                for c in range(NCH):
                    b = c * CH // SEQ
                    dve.scalar_tensor_tensor(out=x[:, chunk(c)], in0=src[:, chunk(c)], scalar=mod[:, l, j, b:b + 1],
                                             in1=x[:, chunk(c)], op0=ALU.mult, op1=ALU.add).then_inc(x_added, 1)
            for c in range(NCH):
                dve.wait_ge(mean_ready, c + 1)
                dve.tensor_tensor(cen[:, chunk(c)], x[:, chunk(c)], ps[:, c, :], ALU.subtract).then_inc(centred, 1)
            dve.wait_ge(std_ready, 1)
            dve.reciprocal(rstd[:, :], rstd[:, :]).then_inc(rstd_ready, 1)
            dve.wait_ge(rstd_ready, 1)
            for t in range(NT):
                dve.tensor_scalar(diag[:, t * P:(t + 1) * P], T["ident"][:, :], rstd[:, t:t + 1], None, ALU.mult)\
                   .then_inc(diag_ready, 1)
            dve.wait_ge(centred, NCH)
            for c in range(NCH):
                b = c * CH // SEQ
                dve.wait_ge(spread, c + 1)
                dve.scalar_tensor_tensor(out=cen[:, chunk(c)], in0=cen[:, chunk(c)],
                                         scalar=mod[:, layer, part + 1, b:b + 1], in1=ps[:, c, :],
                                         op0=ALU.mult, op1=ALU.mult).then_inc(normed, 1)


def log1p_factors(degree=8):
    import numpy as np
    f = lambda e: np.log1p(e) / e
    poly = np.polynomial.chebyshev.Chebyshev.interpolate(f, degree, domain=[0, 1])\
        .convert(kind=np.polynomial.Polynomial, domain=[-1, 1], window=[-1, 1])
    s = poly.coef[-1] ** (1 / degree)
    roots = [z for z in poly.roots() if z.imag > 0]
    assert len(roots) == degree // 2
    return float(s), [(float(-s * z.real), float((s * z.imag) ** 2)) for z in roots]


def mamba_layer(nc, core, T, A, L, bc_dram):
    h, ps = T["hT"], T["ps"]
    n = f"m{L}_"
    with ExitStack() as st:
        def sb(name, shape, dt=F32):
            return core.sb(st, n + name, shape, dt)

        def sem(name):
            return core.sem(n + name)

        win = sb("win", [P, 2 * ED])
        wx = sb("wx", [P, NH2, RK + 2 * NS])
        wdt = sb("wdt", [RK, ED])
        wout = sb("wout", [P, NH2, D])
        normw = sb("normw", [P, 1])
        chan = sb("chan", [P, NH2, NCONV + 3 + NS])
        TAP, CB, BDT, DP, AL = 0, NCONV, NCONV + 1, NCONV + 2, NCONV + 3
        rate = sb("rate", [P, NH2, NS])
        diag_d = sb("diag_d", [P, NH2, P])
        silu_z = sb("silu_z", [P, NH2, TOK])
        xs = sb("xs", [P, NH2, TOK])
        delta = sb("delta", [P, NH2, TOK])
        du = sb("du", [P, NH2, TOK])
        decay = sb("decay", [P, 2, NH2, SEQ])
        drive = sb("drive", [P, 2, NH2, SEQ])
        PADW = NCONV - 1 + SEQ
        work = sb("work", [P, NH2 * NB * PADW])
        pad = work[:, :].rearrange("p (m b t) -> p m b t", m=NH2, b=NB)
        prod = work[:, 0:2 * NH2 * SEQ].rearrange("p (s m t) -> p s m t", s=2, m=NH2)
        hs = sb("hs", [P, NH2, SEQ])
        bc = sb("bc", [P, 2, 2, SEQ])
        rows = sb("rows", [3, 2, 2, SEQ], BF16)
        xn = hs[:, :, :].rearrange("p m t -> p (m t)")
        rs = bc[:, 0, :, :].rearrange("p m t -> p (m t)")
        dtr = bc[0:RK, 1, :, :].rearrange("p m t -> p (m t)")
        parts = drive[:, 0, :, :].rearrange("p m t -> p (m t)").bitcast(BF16).rearrange("p (k t) -> p k t", k=2)
        part3 = drive[:, 1, 0, :].bitcast(BF16)
        rest = decay[:, 0, :, :].rearrange("p m t -> p (m t)")
        rest2 = decay[:, 1, :, :].rearrange("p m t -> p (m t)")
        BCR = slice(RK, RK + 2 * NS)
        flat = decay[:, :, :, :].rearrange("p s m t -> p (s m t)")
        flat2 = drive[:, :, :, :].rearrange("p s m t -> p (s m t)")

        rdiag = drive[:, 0, :, :].rearrange("p m t -> p (m t)")
        rstd = sb("rstd", [P, TOK // P])
        slope, factors = log1p_factors()
        shifts = sb("log_shifts", [P, len(factors)])

        loaded = sem("loaded")
        diag_ready, spread_ready = sem("diag"), sem("spread")
        vmax, sq_ready, log_step, delta_ready, du_ready = (sem(x) for x in ("vmax", "sq", "log", "delta", "du"))
        squared, ms_ready, std_ready, rstd_ready, normed = (sem(x) for x in ("squared", "ms", "std", "rstd", "normed"))
        proj_ready, z_ready, xc_copied = sem("proj"), sem("z"), sem("xc")
        pad_zero, conv_step, conv_done, xs_ready = sem("padzero"), sem("convstep"), sem("conv"), sem("xs")
        small = sem("small")
        neg = sem("neg")
        dbc_ready, dt_copied, split_step, bc_stored = sem("dbc"), sem("dt"), sem("split"), sem("bcstored")
        dl_ready, ab_ready, ex_ready = (sem(x) for x in ("dl", "abs", "exp"))
        rows_ready = [sem(f"rows{i}") for i in range(2)]
        bc_summed, bc_copied, decay_ready, drive_ready = (sem(x) for x in ("bcsum", "bccopy", "decay", "drive"))
        scanned, multiplied, y_summed = sem("scanned"), sem("multiplied"), sem("ysum")
        y_init, gated, out_ready, added = sem("yinit"), sem("gated"), sem("out"), sem("added")

        block = st.enter_context(nc.Block())
        GI = NS

        @block.sync
        def _(sp):
            sp.dma_start(win[:, :], A["win"][L]).then_inc(loaded, 16)
            sp.dma_start(normw[:, :], A["normw"][L]).then_inc(loaded, 16)
            sp.dma_start(chan[:, :, :], A["chan"][L].rearrange("(m p) k -> p m k", p=P)).then_inc(loaded, 16)
            sp.dma_start(wx[:, :, :], A["wx"][L].rearrange("(m p) r -> p m r", p=P)).then_inc(loaded, 16)
            sp.dma_start(wdt[:, :], A["wdt"][L]).then_inc(loaded, 16)
            sp.dma_start(wout[:, :, :], A["wout"][L].rearrange("(m p) d -> p m d", p=P)).then_inc(loaded, 16)
            sp.wait_ge(split_step, 4 * 5)
            for k in range(3):
                src = parts[BCR, k, :] if k < 2 else part3[BCR, :]
                sp.dma_start(bc_dram[k].rearrange("b v n t -> (v n) b t"), src.rearrange("n (b t) -> n b t", b=NB))\
                  .then_inc(bc_stored, 16)
            sp.wait_ge(bc_stored, 48)
            for b in range(NB):
                with sp.Fori(0, NS // 2) as i:
                    for s in range(2):
                        sp.wait_ge(bc_summed, b * GI + 2 * i + s + 1)
                        sp.dma_start(rows[:, s, :, :], bc_dram[:, b, :, bass.ds(2 * i + s, 1), :].rearrange('k v n t -> k (v n) t'))\
                          .then_inc(rows_ready[s], 16)

        @block.gpsimd
        def _(pool):
            for m in range(NH2):
                pool.memset(pad[:, m, :, 0:NCONV - 1], 0.0).then_inc(pad_zero, 1)
            pool.wait_ge(loaded, 96)
            for m in range(NH2):
                pool.tensor_scalar(diag_d[:, m, :], T["ident"][:, :], chan[:, m, DP:DP + 1], None, ALU.mult)\
                    .then_inc(small, 1)
            for i, (shift, _) in enumerate(factors):
                pool.memset(shifts[:, i:i + 1], shift).then_inc(small, 1)
            for u in range(4):
                b, m = divmod(u, NH2)
                t = slice(b * SEQ, (b + 1) * SEQ)
                pool.wait_ge(delta_ready, u + 1)
                pool.wait_ge(xs_ready, u + 1)
                pool.tensor_tensor(du[:, m, t], delta[:, m, t], xs[:, m, t], ALU.mult).then_inc(du_ready, 1)
            pool.wait_ge(du_ready, 4)
            pool.sem_inc(drive_ready, 2)
            for b in range(NB):
                with pool.Fori(0, NS // 2) as i:
                    for s in range(2):
                        g = b * GI + 2 * i + s
                        pool.wait_ge(bc_copied, g + 2)
                        pool.wait_ge(scanned, 2 * (g + 1))
                        pool.tensor_tensor(drive[:, s, :, :], du[:, :, b * SEQ:(b + 1) * SEQ],
                                           bc[:, s, 0:1, :].broadcast_to([P, NH2, SEQ]), ALU.mult).then_inc(drive_ready, 1)

        @block.tensor
        def _(pe):
            for c in range(NCH):
                pe.wait_ge(squared, c + 1)
                mm = column_means(pe, T, rs, c, 4)
            mm.then_inc(ms_ready, 1)
            for c in range(NCH):
                pe.wait_ge(diag_ready, (c + 1) * (CH // P))
                pe.matmul(ps[:, c, :], T["ones"][:, :], rdiag[:, chunk(c)], start=True, stop=True).then_inc(spread_ready, 1)
            pe.wait_ge(loaded, 96)
            for c in range(NCH):
                pe.wait_ge(normed, c + 1)
                for m in range(4):
                    if c == 0 and m == 0:
                        pe.wait_ge(normed, NCH)
                    if c >= 2:
                        pe.wait_ge(z_ready, 2 * (c - 1))
                        pe.wait_ge(xc_copied, 2 * (c - 1))
                    pe.matmul(ps[:, (c % 2) * 4 + m, :], win[:, m * P:(m + 1) * P], xn[:, chunk(c)],
                              start=True, stop=True).then_inc(proj_ready, 1)
            pe.wait_ge(z_ready, 8)
            pe.wait_ge(xc_copied, 8)
            for c in range(NCH):
                pe.wait_ge(xs_ready, 2 * (c // 2) + 2)
                for m in range(NH2):
                    mm = pe.matmul(ps[0:RK + 2 * NS, c, :], wx[:, m, :], xs[:, m, chunk(c)],
                                   start=(m == 0), stop=(m == NH2 - 1))
                mm.then_inc(dbc_ready, 1)
            for b in range(NB):
                for m in range(NH2):
                    u = b * NH2 + m
                    if u < 2:
                        pe.wait_ge(dt_copied, 2 * b + 2)
                    else:
                        pe.wait_ge(dt_copied, NCH)
                        pe.wait_ge(split_step, 4 * 5)
                    for c in range(2):
                        mm = pe.matmul(ps[:, (4 + 2 * u + c) % 8, :], wdt[:, m * P:(m + 1) * P],
                                       dtr[:, chunk(2 * b + c)], start=True, stop=True)
                    mm.then_inc(dl_ready, 1)
            pe.wait_ge(small, 2)
            pe.sem_inc(bc_summed, 2)
            pe.sem_inc(y_summed, 2)
            for b in range(NB):
                if b == 0:
                    pe.wait_ge(ab_ready, 4)
                    pe.wait_ge(vmax, 4)
                else:
                    pe.wait_ge(gated, 2)
                for m in range(NH2):
                    for c in range(2):
                        mm = pe.matmul(ps[:, 2 * m + c, :], diag_d[:, m, :], xs[:, m, chunk(2 * b + c)],
                                       start=True, stop=False, skip_group_check=True)
                if b:
                    pe.wait_ge(added, 2)
                mm.then_inc(y_init, 1)

                def spread(g, s, turn):
                    pe.wait_ge(rows_ready[s], turn)
                    pe.wait_ge(bc_copied, g + 1)
                    for k in range(2):
                        for c in range(2):
                            mm = pe.matmul(ps[:, 4 + 2 * k + c, :], T["ones_bf"][0:3, :],
                                           rows[:, s, k, c * CH:(c + 1) * CH], start=True, stop=True)
                    mm.then_inc(bc_summed, 1)

                def sum_states(g, s):
                    pe.wait_ge(multiplied, g + 3)
                    for m in range(NH2):
                        for c in range(2):
                            mm = pe.matmul(ps[:, 2 * m + c, :], T["ident"][:, :], prod[:, s, m, c * CH:(c + 1) * CH],
                                           start=False, stop=False, skip_group_check=True)
                    mm.then_inc(y_summed, 1)

                half = NS // 2
                spread(b * GI, 0, 16 * (b * half + 1))
                with pe.Fori(0, half - 1) as i:
                    g = b * GI + 2 * i
                    spread(g + 1, 1, 16 * (b * half + i + 1))
                    sum_states(g, 0)
                    spread(g + 2, 0, 16 * (b * half + i + 2))
                    sum_states(g + 1, 1)
                spread((b + 1) * GI - 1, 1, 16 * (b + 1) * half)
                sum_states((b + 1) * GI - 2, 0)
                sum_states((b + 1) * GI - 1, 1)
                pe.wait_ge(gated, 2 * (b + 1))
                for c in range(2):
                    for m in range(NH2):
                        mm = pe.matmul(ps[:, 4 + c, :], wout[:, m, :], hs[:, m, c * CH:(c + 1) * CH],
                                       start=(m == 0), stop=(m == NH2 - 1))
                    mm.then_inc(out_ready, 1)


        @block.scalar
        def _(act):
            for c in range(NCH):
                act.activation(rs[:, chunk(c)], h[:, chunk(c)], ACT.Square).then_inc(squared, 1)
            act.wait_ge(ms_ready, 1)
            act.activation(rstd[:, :], ps[:, 4, 0:TOK // P], ACT.Sqrt, bias=T["eps"][:, 0:1]).then_inc(std_ready, 1)
            for c in range(NCH):
                for m in range(NH2):
                    act.wait_ge(proj_ready, 4 * c + 3 + m)
                    act.activation(silu_z[:, m, chunk(c)], ps[:, (c % 2) * 4 + NH2 + m, :], ACT.Silu)\
                       .then_inc(z_ready, 1)
            act.wait_ge(loaded, 96)
            for b in range(NB):
                for m in range(NH2):
                    t = slice(b * SEQ, (b + 1) * SEQ)
                    act.wait_ge(conv_done, 2 * b + m + 1)
                    act.activation(xs[:, m, t], xs[:, m, t], ACT.Silu, bias=chan[:, m, CB:CB + 1]).then_inc(xs_ready, 1)
            act.activation(rate[:, :, :], chan[:, :, AL:AL + NS], ACT.Exp).then_inc(neg, 1)
            NF = len(factors)
            act.wait_ge(small, NH2 + NF)
            for u in range(4):
                b, m = divmod(u, NH2)
                q = slice(u * SEQ, (u + 1) * SEQ)
                bank = (4 + 2 * u) % 8
                act.wait_ge(dl_ready, u + 1)
                act.wait_ge(vmax, u + 1)
                act.wait_ge(split_step, 4 * 5)
                act.activation(flat[:, q].rearrange("p (a t) -> p a t", a=2), ps[:, bank:bank + 2, :], ACT.Abs,
                               bias=chan[:, m, BDT:BDT + 1]).then_inc(ab_ready, 1)
                act.wait_ge(ab_ready, u + 1)
                act.activation(flat[:, q], flat[:, q], ACT.Exp, scale=-1.0).then_inc(ex_ready, 1)
            for u in range(4):
                q = slice(u * SEQ, (u + 1) * SEQ)
                act.wait_ge(ex_ready, u + 1)
                for i in range(NF):
                    k = u * NF + i
                    if k >= 2:
                        act.wait_ge(log_step, k - 1)
                    act.activation(hs[:, k % 2, :], flat[:, q], ACT.Square, scale=slope, bias=shifts[:, i:i + 1])\
                       .then_inc(sq_ready, 1)
            act.wait_ge(neg, 2)
            act.wait_ge(delta_ready, 4)
            act.sem_inc(bc_copied, 1)
            for b in range(NB):
                with act.Fori(0, NS // 2) as i:
                    for s in range(2):
                        g = b * GI + 2 * i + s
                        act.wait_ge(bc_summed, g + 3)
                        act.wait_ge(drive_ready, g + 1)
                        act.wait_ge(multiplied, g + 1)
                        act.activation(bc[:, s, :, :].rearrange("p k (c t) -> p (k c) t", t=CH), ps[:, 4:8, :],
                                       ACT.Copy).then_inc(bc_copied, 1)
                        for m in range(NH2):
                            act.wait_ge(scanned, 2 * g + 1 + m)
                            act.activation(decay[:, s, m, :], delta[:, m, b * SEQ:(b + 1) * SEQ], ACT.Exp,
                                           scale=rate[:, m, bass.ds(2 * i + s, 1)]).then_inc(decay_ready, 1)

        @block.vector
        def _(dve):
            dve.wait_ge(loaded, 96)
            dve.wait_ge(std_ready, 1)
            dve.reciprocal(rstd[:, :], rstd[:, :]).then_inc(rstd_ready, 1)
            dve.wait_ge(rstd_ready, 1)
            for t in range(TOK // P):
                dve.tensor_scalar(rdiag[:, t * P:(t + 1) * P], T["ident"][:, :], rstd[:, t:t + 1], None, ALU.mult)\
                   .then_inc(diag_ready, 1)
            for c in range(NCH):
                dve.wait_ge(spread_ready, c + 1)
                dve.scalar_tensor_tensor(out=xn[:, chunk(c)], in0=h[:, chunk(c)], scalar=normw[:, 0:1],
                                         in1=ps[:, c, :], op0=ALU.mult, op1=ALU.mult).then_inc(normed, 1)
            dve.wait_ge(pad_zero, 2)
            for c in range(NCH):
                b, o = divmod(c, 2)
                for m in range(NH2):
                    dve.wait_ge(proj_ready, 4 * c + 1 + m)
                    dve.tensor_copy(pad[:, m, b, NCONV - 1 + o * CH:NCONV - 1 + (o + 1) * CH],
                                    ps[:, (c % 2) * 4 + m, :]).then_inc(xc_copied, 1)
            step = 0
            for b in range(NB):
                for m in range(NH2):
                    t = xs[:, m, b * SEQ:(b + 1) * SEQ]
                    dve.wait_ge(xc_copied, 4 * b + 4)
                    dve.tensor_scalar(t, pad[:, m, b, 0:SEQ], chan[:, m, TAP:TAP + 1], None, ALU.mult)\
                       .then_inc(conv_step, 1)
                    step += 1
                    for k in range(1, NCONV):
                        dve.wait_ge(conv_step, step)
                        last = dve.scalar_tensor_tensor(out=t, in0=pad[:, m, b, k:k + SEQ],
                                                        scalar=chan[:, m, TAP + k:TAP + k + 1], in1=t,
                                                        op0=ALU.mult, op1=ALU.add)
                        if k < NCONV - 1:
                            last.then_inc(conv_step, 1)
                            step += 1
                    last.then_inc(conv_done, 1)
            for c in range(NCH):
                dve.wait_ge(dbc_ready, c + 1)
                dve.tensor_copy(dtr[:, chunk(c)], ps[0:RK, c, :]).then_inc(dt_copied, 1)
            for c in range(NCH):
                k = 5 * c
                dve.tensor_copy(parts[BCR, 0, chunk(c)], ps[BCR, c, :]).then_inc(split_step, 1)
                dve.wait_ge(split_step, k + 1)
                dve.tensor_tensor(rest[BCR, chunk(c)], ps[BCR, c, :], parts[BCR, 0, chunk(c)], ALU.subtract)\
                   .then_inc(split_step, 1)
                dve.wait_ge(split_step, k + 2)
                dve.tensor_copy(parts[BCR, 1, chunk(c)], rest[BCR, chunk(c)]).then_inc(split_step, 1)
                dve.wait_ge(split_step, k + 3)
                dve.tensor_tensor(rest2[BCR, chunk(c)], rest[BCR, chunk(c)], parts[BCR, 1, chunk(c)], ALU.subtract)\
                   .then_inc(split_step, 1)
                dve.wait_ge(split_step, k + 4)
                dve.tensor_copy(part3[BCR, chunk(c)], rest2[BCR, chunk(c)]).then_inc(split_step, 1)
            dve.wait_ge(neg, 1)
            dve.tensor_scalar(rate[:, :, :], rate[:, :, :], -1.0, None, ALU.mult).then_inc(neg, 1)
            for u in range(4):
                b, m = divmod(u, NH2)
                bank = (4 + 2 * u) % 8
                dve.wait_ge(dl_ready, u + 1)
                dve.tensor_scalar(du[:, m, b * SEQ:(b + 1) * SEQ].rearrange("p (a t) -> p a t", a=2),
                                  ps[:, bank:bank + 2, :], chan[:, m, BDT:BDT + 1], 0.0, ALU.add, ALU.max)\
                   .then_inc(vmax, 1)
            NF = len(factors)
            dve.wait_ge(bc_stored, 48)
            for u in range(4):
                b, m = divmod(u, NH2)
                t = slice(b * SEQ, (b + 1) * SEQ)
                q = slice(u * SEQ, (u + 1) * SEQ)
                for i in range(NF):
                    k = u * NF + i
                    dve.wait_ge(sq_ready, k + 1)
                    if i:
                        dve.wait_ge(log_step, k)
                    dve.scalar_tensor_tensor(out=flat2[:, q], in0=hs[:, k % 2, :], scalar=factors[i][1],
                                             in1=flat2[:, q] if i else flat[:, q], op0=ALU.add, op1=ALU.mult)\
                       .then_inc(log_step, 1)
                dve.wait_ge(log_step, (u + 1) * NF)
                dve.tensor_tensor(delta[:, m, t], flat2[:, q], du[:, m, t], ALU.add).then_inc(delta_ready, 1)
            dve.sem_inc(scanned, 4)
            dve.sem_inc(multiplied, 2)
            for b in range(NB):
                with dve.Fori(0, NS // 2) as i:
                    for s in range(2):
                        g = b * GI + 2 * i + s
                        dve.wait_ge(drive_ready, g + 3)
                        for m in range(NH2):
                            dve.wait_ge(decay_ready, 2 * g + 1 + m)
                            dve.wait_ge(multiplied, g + 2)
                            dve.tensor_tensor_scan(hs[:, m, :], decay[:, s, m, :], drive[:, s, m, :], 0.0,
                                                   ALU.mult, ALU.add).then_inc(scanned, 1)
                        dve.wait_ge(scanned, 2 * g + 6)
                        dve.wait_ge(y_summed, g + 1)
                        dve.tensor_tensor(prod[:, s, :, :], hs[:, :, :], bc[:, s, 1:2, :].broadcast_to([P, NH2, SEQ]),
                                          ALU.mult).then_inc(multiplied, 1)
                t = slice(b * SEQ, (b + 1) * SEQ)
                dve.wait_ge(y_init, b + 1)
                dve.wait_ge(y_summed, 2 + (b + 1) * GI)
                for m in range(NH2):
                    dve.tensor_tensor(hs[:, m, :].rearrange("p (a t) -> p a t", a=2), ps[:, 2 * m:2 * m + 2, :],
                                      silu_z[:, m, t].rearrange("p (a t) -> p a t", a=2), ALU.mult).then_inc(gated, 1)
                for c in range(2):
                    dve.wait_ge(out_ready, 2 * b + c + 1)
                    tt = chunk(2 * b + c)
                    dve.tensor_tensor(h[:, tt], h[:, tt], ps[:, 4 + c, :], ALU.add).then_inc(added, 1)


N_HEAD, N_ACT, DH = 16, 4, 64
NT_B = SEQ // P


def route_heads(nc, core, T, A):
    h, ps = T["hT"], T["ps"]
    with ExitStack() as st:
        def sb(name, shape, dt=F32):
            return core.sb(st, "r_" + name, shape, dt)
        wr, br, bo = sb("wr", [P, N_HEAD]), sb("br", [NB, N_HEAD]), sb("bo", [P, 1])
        hsum, logit, nmax = sb("hsum", [P, NB]), sb("logit", [NB, N_HEAD]), sb("nmax", [NB, 1])
        top, dist, total = sb("top", [NB, 8]), sb("dist", [NB, N_HEAD]), sb("total", [NB, 3])
        val, idx = sb("val", [NB, 8]), sb("idx", [NB, 8], U32)
        ev, ez, gates = sb("ev", [NB, N_ACT]), sb("ez", [NB, 1]), sb("gates", [NB, N_ACT])
        loaded, step, act_step, pe_step, moved = (core.sem("r_" + x) for x in ("loaded", "dve", "act", "pe", "moved"))
        block = st.enter_context(nc.Block())

        @block.sync
        def _(sp):
            sp.dma_start(wr[:, :], A["wr"]).then_inc(loaded, 16)
            for b in range(NB):
                sp.dma_start(br[b:b + 1, :], A["br"]).then_inc(loaded, 16)
            sp.dma_start(bo[:, :], A["bo"]).then_inc(loaded, 16)
            sp.wait_ge(step, 9)
            for b in range(NB):
                sp.dma_start(T["head_index"][0:1, b * N_ACT:(b + 1) * N_ACT], idx[b:b + 1, 0:N_ACT]).then_inc(moved, 16)
            sp.wait_ge(moved, 32)

        @block.tensor
        def _(pe):
            pe.wait_ge(loaded, 64)
            pe.wait_ge(step, 2)
            pe.matmul(ps[0:NB, 0, 0:N_HEAD], hsum[:, :], wr[:, :], start=True, stop=True).then_inc(pe_step, 1)
            pe.wait_ge(step, 14)
            for b in range(NB):
                mm = pe.matmul(ps[:, 1, b * N_ACT:(b + 1) * N_ACT], T["ident"][0:NB, b:b + 1].broadcast_to([NB, P]),
                               gates[:, :], start=True, stop=True)
            mm.then_inc(pe_step, 1)

        @block.scalar
        def _(act):
            act.wait_ge(step, 5)
            act.activation(dist[:, :], logit[:, :], ACT.Exp, bias=nmax[:, :], accum_out=total[:, 0:1]).then_inc(act_step, 1)
            act.wait_ge(step, 10)
            act.activation(ev[:, :], val[:, 0:N_ACT], ACT.Exp, bias=nmax[:, :], accum_out=total[:, 1:2]).then_inc(act_step, 1)
            act.activation(ez[:, :], nmax[:, :], ACT.Exp).then_inc(act_step, 1)

        @block.vector
        def _(dve):
            for b in range(NB):
                dve.tensor_reduce(hsum[:, b:b + 1], h[:, b * SEQ:(b + 1) * SEQ], AX.X, ALU.add).then_inc(step, 1)
            dve.wait_ge(pe_step, 1)
            dve.scalar_tensor_tensor(out=logit[:, :], in0=ps[0:NB, 0, 0:N_HEAD], scalar=1.0 / SEQ, in1=br[:, :],
                                     op0=ALU.mult, op1=ALU.add).then_inc(step, 1)
            dve.wait_ge(step, 3)
            dve.max(top[:, :], logit[:, :]).then_inc(step, 1)
            dve.wait_ge(step, 4)
            dve.tensor_scalar(nmax[:, :], top[:, 0:1], -1.0, None, ALU.mult).then_inc(step, 1)
            dve.wait_ge(act_step, 1)
            dve.reciprocal(total[:, 2:3], total[:, 0:1]).then_inc(step, 1)
            dve.wait_ge(step, 6)
            dve.tensor_scalar(dist[:, :], dist[:, :], total[:, 2:3], None, ALU.mult).then_inc(step, 1)
            dve.wait_ge(step, 7)
            dve.max(val[:, :], dist[:, :]).then_inc(step, 1)
            dve.wait_ge(step, 8)
            dve.max_index(idx[:, :], val[:, :], dist[:, :]).then_inc(step, 1)
            dve.tensor_scalar(nmax[:, :], val[:, 0:1], -1.0, None, ALU.mult).then_inc(step, 1)
            dve.wait_ge(act_step, 3)
            dve.scalar_tensor_tensor(out=ez[:, :], in0=ez[:, :], scalar=float(N_HEAD - N_ACT), in1=total[:, 1:2],
                                     op0=ALU.mult, op1=ALU.add).then_inc(step, 1)
            dve.wait_ge(step, 11)
            dve.reciprocal(total[:, 2:3], ez[:, :]).then_inc(step, 1)
            dve.wait_ge(step, 12)
            dve.tensor_scalar(gates[:, :], ev[:, :], total[:, 2:3], None, ALU.mult).then_inc(step, 1)
            dve.tensor_tensor(T["gate_bo"][:, :], T["mod"][:, 0, 5, :], bo[:, 0:1].broadcast_to([P, NB]), ALU.mult)\
               .then_inc(step, 1)
            dve.wait_ge(pe_step, 2)
            dve.tensor_copy(T["gates"][:, :, :].rearrange("p b k -> p (b k)"), ps[:, 1, 0:NB * N_ACT]).then_inc(step, 1)


def chosen_heads(nc, core, T, A):
    x, h, ps = T["xT"], T["hT"], T["ps"]
    with ExitStack() as st:
        def sb(name, shape, dt=F32):
            return core.sb(st, "a_" + name, shape, dt)

        def sem(name):
            return core.sem("a_" + name)

        w, bias, bv, wo = sb("w", [P, 3, DH]), sb("bias", [DH, 3]), sb("bv", [1, DH]), sb("wo", [DH, D])
        gq, gkb = sb("gq", [DH, 1]), sb("gkb", [DH, 1])
        qT, kT = sb("qT", [DH, SEQ]), sb("kT", [DH, SEQ])
        v = sb("v", [P, NT_B, DH + 1])
        prob = sb("prob", [P, 2, SEQ])
        probT = sb("probT", [P, 2, NT_B, P])
        nmax = sb("nmax", [P, 2])
        rsum = sb("rsum", [P, 2])
        o = sb("o", [P, NT_B, DH])
        oT = sb("oT", [DH, SEQ])
        w_loaded, wo_loaded, w_used, wo_used = sem("w_loaded"), sem("wo_loaded"), sem("w_used"), sem("wo_used")
        ones_set, small, q_proj, k_proj, v_proj = sem("ones_set"), sem("small"), sem("q_proj"), sem("k_proj"), sem("v_proj")
        q_ready, k_ready, v_ready, bo_added = sem("q"), sem("k"), sem("v"), sem("bo_added")
        scored, maxed, expd, turned = sem("scored"), sem("maxed"), sem("expd"), sem("turned")
        t_copied = [sem("t_dve"), sem("t_act")]
        weighed, inverted, normed = sem("weighed"), sem("inverted"), sem("normed")
        o_turned, o_copied, projected, x_added = sem("o_turned"), sem("o_copied"), sem("projected"), sem("x_added")
        block = st.enter_context(nc.Block())
        two = lambda ap: ap.rearrange("p (a t) -> p a t", a=2)


        @block.sync
        def _(sp):
            for b in range(NB):
                with sp.Fori(0, N_ACT) as i:
                    g = b * N_ACT + i
                    sp.wait_ge(v_proj, g + 1)
                    sp.wait_ge(q_ready, g + 1)
                    head = sp.value_load(T["head_index"][0:1, bass.ds(g, 1)], min_val=0, max_val=N_HEAD - 1)
                    sp.dma_start(w[:, :, :].rearrange("p j d -> p (j d)"), A["wqkv_h"][bass.ds(head, 1), :, :]
                                 .rearrange("o p n -> (o p) n")).then_inc(w_loaded, 16)
                    sp.dma_start(bias[:, :], A["bqkv_h"][bass.ds(head, 1), :, :].rearrange("o p n -> (o p) n"))\
                      .then_inc(w_loaded, 16)
                    sp.dma_start(bv[:, :], A["bv_h"][bass.ds(head, 1), :]).then_inc(w_loaded, 16)
                    sp.wait_ge(projected, g + 1)
                    sp.dma_start(wo[:, :], A["wo_k"][bass.ds(i, 1), :, :].rearrange("o p n -> (o p) n"))\
                      .then_inc(wo_loaded, 16)

        @block.gpsimd
        def _(pool):
            pool.memset(v[:, :, DH:DH + 1], 1.0).then_inc(ones_set, 1)

        @block.tensor
        def _(pe):
            pe.wait_ge(ones_set, 1)
            pe.sem_inc(v_proj, 1)
            pe.sem_inc(projected, 1)
            pe.sem_inc(turned, 4)
            pe.sem_inc(weighed, 2)
            for b in range(NB):
                with pe.Fori(0, N_ACT) as i:
                    g = b * N_ACT + i
                    pe.wait_ge(w_loaded, 48 * g + 48)
                    pe.wait_ge(expd, 8 * g + 2)
                    for j, ready in ((0, q_proj), (1, k_proj)):
                        for c in range(2):
                            mm = pe.matmul(ps[0:DH, 2 * j + c, :], w[:, j, :], h[:, chunk(2 * b + c)], start=True, stop=True)
                        mm.then_inc(ready, 1)
                    pe.wait_ge(o_copied, g + 1)
                    for t in range(NT_B):
                        pe.matmul(ps[:, 4, t * DH:(t + 1) * DH], h[:, b * SEQ + t * P:b * SEQ + (t + 1) * P], w[:, 2, :],
                                  start=True, stop=False)
                        mm = pe.matmul(ps[:, 4, t * DH:(t + 1) * DH], T["ones"][0:1, :], bv[:, :], start=False, stop=True)
                    mm.then_inc(v_proj, 1)
                    pe.wait_ge(q_ready, g + 2)
                    pe.wait_ge(k_ready, g + 2)

                    def scores(t):
                        pe.wait_ge(expd, 8 * g + t + 1)
                        for c in range(2):
                            mm = pe.matmul(ps[:, 2 * (t % 2) + c, :], qT[:, t * P:(t + 1) * P], kT[:, c * CH:(c + 1) * CH],
                                           start=True, stop=True)
                        mm.then_inc(scored, 1)

                    scores(0)
                    scores(1)
                    pe.wait_ge(v_ready, g + 1)
                    for t in range(NT_B):
                        pe.wait_ge(expd, 8 * g + t + 3)
                        for half in range(2):
                            pe.wait_ge(t_copied[half], 8 * g + t + 1)
                            for j in range(4):
                                mm = pe.transpose(ps[:, 4 + half, j * P:(j + 1) * P],
                                                  prob[:, t % 2, (4 * half + j) * P:(4 * half + j + 1) * P], T["ident"][:, :])
                            mm.then_inc(turned, 1)
                        if t + 2 < NT_B:
                            scores(t + 2)
                        pe.wait_ge(normed, 8 * g + t + 1)
                        if t == 0:
                            pe.wait_ge(x_added, 2 * g + 2)
                        for j in range(NT_B):
                            if j % 4 == 0:
                                pe.wait_ge(t_copied[j // 4], 8 * g + t + 2)
                            mm = pe.matmul(ps[:, 6 + t % 2, 0:DH + 1], probT[:, t % 2, j, :], v[:, j, :],
                                           start=(j == 0), stop=(j == NT_B - 1))
                        mm.then_inc(weighed, 1)
                    pe.wait_ge(normed, 8 * g + 10)
                    pe.matmul(ps[0:DH, 4, 0:P], o[:, 0, :], T["ident"][:, :], start=True, stop=True)
                    for t in range(1, NT_B):
                        mm = pe.transpose(ps[0:DH, 4 + t // 4, (t % 4) * P:(t % 4 + 1) * P], o[:, t, :], T["ident"][:, :])
                    mm.then_inc(o_turned, 1)
                    pe.wait_ge(o_copied, g + 2)
                    pe.wait_ge(wo_loaded, 16 * g + 16)
                    for c in range(2):
                        mm = pe.matmul(ps[:, 6 + c, :], wo[:, :], oT[:, c * CH:(c + 1) * CH], start=True, stop=True)
                    mm.then_inc(projected, 1)

        @block.scalar
        def _(act):
            act.sem_inc(expd, 2)
            act.sem_inc(t_copied[1], 1)
            act.sem_inc(k_ready, 1)
            for b in range(NB):
                with act.Fori(0, N_ACT) as i:
                    g = b * N_ACT + i
                    act.wait_ge(k_proj, g + 1)
                    act.wait_ge(small, 2 * g + 2)
                    act.activation(two(kT[:, :]), ps[0:DH, 2:4, :], ACT.Identity, bias=gkb[:, :],
                                   scale=T["gates"][0:DH, b, bass.ds(i, 1)]).then_inc(k_ready, 1)

                    def exps(t):
                        act.wait_ge(maxed, 8 * g + t + 1)
                        act.wait_ge(turned, 16 * g + 2 * t + 2)
                        act.activation(two(prob[:, t % 2, :]), ps[:, 2 * (t % 2):2 * (t % 2) + 2, :], ACT.Exp,
                                       bias=nmax[:, t % 2:t % 2 + 1]).then_inc(expd, 1)

                    exps(0)
                    exps(1)
                    for t in range(NT_B):
                        act.wait_ge(turned, 16 * g + 2 * t + 6)
                        act.wait_ge(weighed, 8 * g + t + 1)
                        act.activation(probT[:, t % 2, 4:8, :].rearrange("p j q -> p (j q)"), ps[:, 5, :], ACT.Copy)\
                           .then_inc(t_copied[1], 1)
                        if t + 2 < NT_B:
                            exps(t + 2)

        @block.vector
        def _(dve):
            dve.sem_inc(t_copied[0], 1)
            dve.sem_inc(q_ready, 1)
            dve.sem_inc(normed, 2)
            dve.sem_inc(o_copied, 1)
            dve.sem_inc(x_added, 2)
            for b in range(NB):
                xb = x[:, b * SEQ:(b + 1) * SEQ]
                dve.tensor_scalar(xb, xb, T["gate_bo"][:, b:b + 1], None, ALU.add).then_inc(bo_added, 1)
                with dve.Fori(0, N_ACT) as i:
                    g = b * N_ACT + i
                    gate = T["gates"][:, b, bass.ds(i, 1)]
                    dve.wait_ge(w_loaded, 48 * g + 48)
                    dve.wait_ge(k_ready, g + 1)
                    dve.tensor_scalar(gq[:, :], gate[0:DH, :], DH ** -0.5, None, ALU.mult).then_inc(small, 1)
                    dve.tensor_scalar(gkb[:, :], bias[:, 1:2], gate[0:DH, :], None, ALU.mult).then_inc(small, 1)
                    dve.wait_ge(small, 2 * g + 1)
                    dve.wait_ge(q_proj, g + 1)
                    dve.tensor_scalar(two(qT[:, :]), ps[0:DH, 0:2, :], bias[:, 0:1], gq[:, :], ALU.add, ALU.mult)\
                       .then_inc(q_ready, 1)
                    dve.wait_ge(v_proj, g + 2)
                    dve.tensor_scalar(v[:, :, 0:DH], ps[:, 4, :].rearrange("p (t d) -> p t d", d=DH), gate, None, ALU.mult)\
                       .then_inc(v_ready, 1)

                    def maxima(t):
                        dve.wait_ge(scored, 8 * g + t + 1)
                        dve.wait_ge(expd, 8 * g + t + 1)
                        dve.tensor_reduce(nmax[:, t % 2:t % 2 + 1], ps[:, 2 * (t % 2):2 * (t % 2) + 2, :], AX.XY, ALU.max,
                                          negate=True).then_inc(maxed, 1)

                    def normalise(t):
                        dve.wait_ge(weighed, 8 * g + t + 3)
                        dve.reciprocal(rsum[:, t % 2:t % 2 + 1], ps[:, 6 + t % 2, DH:DH + 1]).then_inc(inverted, 1)
                        dve.wait_ge(inverted, 8 * g + t + 1)
                        dve.tensor_scalar(o[:, t, :], ps[:, 6 + t % 2, 0:DH], rsum[:, t % 2:t % 2 + 1], None, ALU.mult)\
                           .then_inc(normed, 1)

                    maxima(0)
                    maxima(1)
                    for t in range(NT_B):
                        dve.wait_ge(turned, 16 * g + 2 * t + 5)
                        dve.wait_ge(weighed, 8 * g + t + 1)
                        dve.tensor_copy(probT[:, t % 2, 0:4, :].rearrange("p j q -> p (j q)"), ps[:, 4, :])\
                           .then_inc(t_copied[0], 1)
                        if t + 2 < NT_B:
                            maxima(t + 2)
                        if t:
                            normalise(t - 1)
                    normalise(NT_B - 1)
                    dve.wait_ge(o_turned, g + 1)
                    dve.tensor_copy(two(oT[:, :]), ps[0:DH, 4:6, :]).then_inc(o_copied, 1)
                    dve.wait_ge(projected, g + 2)
                    dve.wait_ge(bo_added, b + 1)
                    for c in range(2):
                        dve.wait_ge(x_added, 2 * g + 1 + c)
                        xc = x[:, chunk(2 * b + c)]
                        dve.scalar_tensor_tensor(out=xc, in0=ps[:, 6 + c, :], scalar=T["mod"][:, 0, 5, b:b + 1], in1=xc,
                                                 op0=ALU.mult, op1=ALU.add).then_inc(x_added, 1)


H1, HD = 16, 8
NG = NB * H1
WIN = 128
NREL = 2 * WIN + 1
NP3 = 3
STACK = NP3 * NP3 * HD
BIAS_ROWS = slice(STACK, STACK + NP3)
MAX_ROWS = slice(STACK + NP3, STACK + 2 * NP3)
KPOS, KALL = STACK + NP3, STACK + 2 * NP3
Q_, KL_, KR_ = range(3)
LEFT, RIGHT, ONES = range(3)
LOWEST = -3.0e38


def relative_parts(nc, core, T, A, dram, v, wstack):
    h, ps = T["hT"], T["ps"]
    with ExitStack() as st:
        def sb(name, shape, dt=F32):
            return core.sb(st, "p_" + name, shape, dt)

        def sem(name):
            return core.sem("p_" + name)

        w, cols = sb("w", [P, 3, D]), sb("cols", [P, 4])
        bv, table, brow = sb("bv", [1, D]), sb("table", [HD + 1, NREL]), sb("brow", [1, 2])
        edge = sb("edge", [HD + 1, 1])
        full, part = sb("full", [P, 3, TOK]), sb("part", [P, 3, NP3, TOK], BF16)
        scaled = sb("scaled", [P, TOK])
        tpart, bpart = sb("tpart", [HD + 1, NP3, NREL], BF16), sb("bpart", [1, NP3, 2], BF16)
        consts = sb("consts", [1, 3, NP3, SEQ], BF16)
        loaded, q_ready, k_ready, v_ready = sem("loaded"), sem("q"), sem("k"), sem("v")
        k_scaled, full_ready = sem("k_scaled"), sem("full")
        p1, r1, p2, r2, p3 = sem("p1"), sem("r1"), sem("p2"), sem("r2"), sem("p3")
        tstep, ones_set, v_copied, stored, wst = sem("tstep"), sem("ones_set"), sem("v_copied"), sem("stored"), sem("wst")
        block = st.enter_context(nc.Block())

        @block.sync
        def _(sp):
            sp.dma_start(w[:, :, :], A["wqkv1"]).then_inc(loaded, 16)
            sp.dma_start(cols[:, :], A["cols1"]).then_inc(loaded, 16)
            sp.dma_start(bv[:, :], A["bv1"]).then_inc(loaded, 16)
            sp.dma_start(table[:, :], A["table"]).then_inc(loaded, 16)
            sp.dma_start(brow[:, :], A["brow"]).then_inc(loaded, 16)
            sp.dma_start(edge[:, :], A["table_edge"]).then_inc(loaded, 16)
            sp.wait_ge(tstep, 12)
            sp.wait_ge(ones_set, 1)
            sp.dma_start(dram["table"].rearrange("k r n -> r k n"), tpart[:, :, :]).then_inc(wst, 16)
            sp.dma_start(dram["const"].rearrange("c k t -> (c k t)"), consts[:, :, :, :].rearrange("o c k t -> o (c k t)"))\
              .then_inc(stored, 16)
            sp.wait_ge(wst, 16)
            for k in range(NP3):
                sp.dma_start(wstack[k * NP3 * HD:(k + 1) * NP3 * HD, :], dram["table"][:, 0:HD, :]).then_inc(stored, 16)
            sp.dma_start(wstack[BIAS_ROWS, :], dram["table"][:, HD:HD + 1, :]).then_inc(stored, 16)
            for a in range(3):
                for k, ready in enumerate((p1, p2, p3)):
                    sp.wait_ge(ready, a + 1)
                    sp.dma_start(dram["qk"][a, k].rearrange("b r t -> r b t"),
                                 part[:, a, k, :].rearrange("r (b t) -> r b t", b=NB)).then_inc(stored, 16)
            sp.wait_ge(stored, 16 * 14)

        @block.gpsimd
        def _(pool):
            pool.memset(consts[:, ONES, :, :], 1.0).then_inc(ones_set, 1)
            for a in range(3):
                pool.wait_ge(p1, a + 1)
                pool.tensor_tensor(full[:, a, :], full[:, a, :], part[:, a, 0, :], ALU.subtract).then_inc(r1, 1)

        @block.tensor
        def _(pe):
            pe.wait_ge(loaded, 96)
            for j, ready in ((0, q_ready), (1, k_ready)):
                for c in range(NCH):
                    mm = pe.matmul(ps[:, 4 * j + c, :], w[:, j, :], h[:, chunk(c)], start=True, stop=True)
                mm.then_inc(ready, 1)
            pe.wait_ge(full_ready, 1)
            for t in range(TOK // P):
                at = ps[:, t // 4, (t % 4) * P:(t % 4 + 1) * P]
                pe.matmul(at, h[:, t * P:(t + 1) * P], w[:, 2, :], start=True, stop=False)
                mm = pe.matmul(at, T["ones"][0:1, :], bv[:, :], start=False, stop=True)
            mm.then_inc(v_ready, 1)

        @block.scalar
        def _(act):
            for a in range(3):
                act.wait_ge(full_ready, a + 1)
                act.activation(part[:, a, 0, :], full[:, a, :], ACT.Copy).then_inc(p1, 1)
            for a in range(3):
                act.wait_ge(r1, a + 1)
                act.activation(part[:, a, 1, :], full[:, a, :], ACT.Copy).then_inc(p2, 1)
            for a in range(3):
                act.wait_ge(r2, a + 1)
                act.activation(part[:, a, 2, :], full[:, a, :], ACT.Copy).then_inc(p3, 1)

        @block.vector
        def _(dve):
            banks = lambda ap: ap.rearrange("p (c t) -> p c t", t=CH)
            dve.wait_ge(q_ready, 1)
            dve.tensor_scalar(banks(full[:, Q_, :]), ps[:, 0:4, :], cols[:, 0:1], None, ALU.add).then_inc(full_ready, 1)
            dve.wait_ge(k_ready, 1)
            dve.tensor_scalar(banks(scaled[:, :]), ps[:, 4:8, :], cols[:, 1:2], HD ** -0.5, ALU.add, ALU.mult)\
               .then_inc(k_scaled, 1)
            dve.wait_ge(k_scaled, 1)
            dve.tensor_scalar(full[:, KL_, :], scaled[:, :], cols[:, 2:3], None, ALU.add).then_inc(full_ready, 1)
            dve.tensor_scalar(full[:, KR_, :], scaled[:, :], cols[:, 3:4], None, ALU.add).then_inc(full_ready, 1)
            dve.tensor_scalar(table[:, :], table[:, :], edge[:, :], None, ALU.subtract).then_inc(tstep, 1)
            n = 1
            for src, parts in ((table, lambda k: tpart[:, k, :]), (brow, lambda k: bpart[:, k, :])):
                for k in range(NP3):
                    dve.wait_ge(tstep, n)
                    dve.tensor_copy(parts(k), src[:, :]).then_inc(tstep, 1)
                    n += 1
                    if k < NP3 - 1:
                        dve.wait_ge(tstep, n)
                        dve.tensor_tensor(src[:, :], src[:, :], parts(k), ALU.subtract).then_inc(tstep, 1)
                        n += 1
            dve.wait_ge(tstep, n)
            for c in range(2):
                ins = dve.tensor_copy(consts[:, c, :, :], bpart[:, :, c:c + 1].broadcast_to([1, NP3, SEQ]))
            ins.then_inc(tstep, 1)
            for a in range(3):
                dve.wait_ge(p2, a + 1)
                dve.tensor_tensor(full[:, a, :], full[:, a, :], part[:, a, 1, :], ALU.subtract).then_inc(r2, 1)
            dve.wait_ge(v_ready, 1)
            dve.wait_ge(ones_set, 1)
            for c in range(NCH):
                b, o = divmod(c, 2)
                dve.tensor_copy(v[:, 4 * o:4 * o + 4, b * H1:(b + 1) * H1, :],
                                ps[:, c, :].rearrange("p (t g d) -> p t g d", t=4, d=HD)).then_inc(v_copied, 1)


def relative_attention(nc, core, T, A, dram, v, wstack, oacc):
    ps = T["ps"]
    with ExitStack() as st:
        def sb(name, shape, dt=F32):
            return core.sb(st, "l_" + name, shape, dt)

        def sem(name):
            return core.sem("l_" + name)

        TURN_AT = 5
        NSL = 4
        stack = [sb(n, [KALL, NSL, SEQ], BF16) for n in ("qs", "kl", "kr")]
        qb = sb("qb", [KPOS, 2, SEQ], BF16)
        rel = sb("rel", [P, 2, NT_B, NREL])
        band = sb("band", [P, NSL, NT_B, 3 * P])
        probT = sb("probT", [P, 2, SEQ])
        seen = sb("seen", [P, 3, NT_B])
        nmax, nparts, nrow = sb("nmax", [P, NT_B]), sb("nparts", [P, NP3 * NT_B], BF16), sb("nrow", [NP3 * NT_B, P], BF16)
        junk, inv = sb("junk", [P, 3 * P]), sb("inv", [P, NT_B])
        VAT, VW = 32, 64
        vhead = sb("vhead", [P, 2, NT_B, VAT + VW])
        outT = sb("outT", [P, CH])
        inside = sb("inside", [P, P])
        inside_set = sem("inside")
        rows_set, lowest_set = sem("rows_set"), sem("lowest")
        stack_loaded = [sem(f"stack{s}") for s in range(NSL)]
        qb_loaded, band_loaded = [sem(f"qb{s}") for s in range(2)], [sem(f"band{s}") for s in range(2)]
        rel_ready, rel_copied, rel_stored, band_step, band_ready = (sem(x) for x in ("rel", "relc", "rels", "bstep", "bready"))
        s1_ready, maxed, dstep = sem("s1"), sem("maxed"), sem("dstep")
        n_turned, n_copied, n_loaded = sem("n_turned"), sem("n_copied"), sem("n_loaded")
        s2_ready, expd, weighed = sem("s2"), sem("expd"), sem("weighed")
        inverted, normed = sem("inverted"), sem("normed")
        v_placed, out_copied, o_turned = sem("v_placed"), sem("out_copied"), sem("o_turned")
        block = st.enter_context(nc.Block())

        def stages(eng, body):
            with eng.Fori(0, NG // 4 - 1) as i:
                for q in range(4):
                    body(4 * i + q, q, lambda k: True, lambda k, n: n * i + k // (4 // n))
            for q in range(4):
                g = NG - 4 + q
                body(g, q, lambda k: g + k < NG, lambda k, n: n * (NG // 4 - 1) + k // (4 // n))

        @block.sync
        def _(sp):
            for a in range(3):
                const = dram["const"][(ONES, LEFT, RIGHT)[a]]
                sp.dma_start(stack[a][BIAS_ROWS, :, :], const.unsqueeze(1).broadcast_to([NP3, NSL, SEQ])).then_inc(rows_set, 16)
                if a != Q_:
                    sp.dma_start(stack[a][MAX_ROWS, :, :], dram["const"][ONES].unsqueeze(1).broadcast_to([NP3, NSL, SEQ]))\
                      .then_inc(rows_set, 16)
            sp.dma_start(qb[BIAS_ROWS, :, :], dram["const"][ONES].unsqueeze(1).broadcast_to([NP3, 2, SEQ])).then_inc(rows_set, 16)

            def at(g):
                return g * HD if isinstance(g, int) else sp.snap(g * HD)

            def rows(a, first, k):
                own = slice(k, k + 1) if a == Q_ else slice(0, NP3)
                return dram["rows"][a][own, bass.ds(first, HD), :].broadcast_to([NP3, HD, SEQ])

            def load_rows(dst, s, a, first, sem):
                for k in range(NP3):
                    sp.dma_start(dst[k * NP3 * HD:(k + 1) * NP3 * HD, s, :], rows(a, first, k)).then_inc(sem, 16)

            def load_qb(first, s):
                load_rows(qb, s, Q_, first, qb_loaded[s])

            def load_stack(first, s):
                for a in range(3):
                    load_rows(stack[a], s, a, first, stack_loaded[s])

            def shift(g, s2, s4, reads_before):
                sp.wait_ge(rel_copied, NT_B * g + NT_B + 1)
                if reads_before is not None:
                    sp.wait_ge(band_loaded[s2], reads_before)
                sp.dma_start(dram["rel"][s2].rearrange("t (p r) -> p t r", p=P), rel[:, s2, :, :]).then_inc(rel_stored, 16)
                sp.wait_ge(rel_stored, 16 * g + 16)
                flat = dram["rel"][s2]
                sp.dma_start(band[:, s4, :, 0:2 * P], flat[:, 0:P * 2 * P].rearrange("t (p c) -> p t c", p=P))\
                  .then_inc(band_loaded[s2], 16)
                sp.dma_start(band[:, s4, :, 2 * P:3 * P], flat[:, P:P + P * 2 * P].rearrange("t (p c) -> p t c", p=P)[:, :, P:2 * P])\
                  .then_inc(band_loaded[s2], 16)

            def load_max(g, s4):
                sp.wait_ge(n_copied, g + 1)
                sp.dma_start(stack[Q_][MAX_ROWS, s4, :], nrow[:, :]).then_inc(n_loaded, 16)

            load_qb(at(0), 0)
            load_qb(at(1), 1)
            for g in range(3):
                load_stack(at(g), g)
            for g in range(2):
                sp.wait_ge(rel_ready, NT_B * (g + 1))
                load_qb(at(g + 2), g)
            for g in range(2):
                shift(g, g, g, None)
            load_max(0, 0)

            def body(g, q, live, per):
                if live(3):
                    first = at(g + 3)
                    sp.wait_ge(s2_ready, NT_B * g + 4 * NT_B)
                    load_stack(first, (q + 3) % NSL)
                if live(4):
                    first = at(g + 4)
                    sp.wait_ge(rel_ready, NT_B * (g + 3))
                    load_qb(first, q % 2)
                if live(2):
                    shift(g + 2, q % 2, (q + 2) % NSL, 32 * per(q + 2, 2))
                if live(1):
                    load_max(g + 1, (q + 1) % NSL)

            stages(sp, body)

        @block.gpsimd
        def _(pool):
            for kind, tiles in ((1, slice(0, 2)), (2, slice(NT_B - 2, NT_B))):
                pool.memset(seen[:, kind, tiles], LOWEST).then_inc(lowest_set, 1)
            pool.memset(inside[:, :], 1.0).then_inc(inside_set, 1)
            pool.wait_ge(inside_set, 1)
            pool.affine_select(out=inside[:, :], in_=inside[:, :], compare_op=ALU.is_ge, fill=0.0, base=0,
                               pattern=[[-1, P]], channel_multiplier=1).then_inc(inside_set, 1)
            pool.wait_ge(inside_set, 2)
            pool.sem_inc(band_ready, 2)
            pool.memset(vhead[:, :, :, :], 0.0).then_inc(inside_set, 1)
            pool.wait_ge(inside_set, 3)
            pool.memset(outT[:, :], 0.0).then_inc(inside_set, 1)
            pool.wait_ge(inside_set, 4)
            pool.memset(vhead[:, :, :, VAT + HD:VAT + HD + 1], 1.0).then_inc(inside_set, 1)
            pool.wait_ge(inside_set, 5)

            def place_v(g, s2):
                if not isinstance(g, int) or g:
                    pool.wait_ge(weighed, NT_B * g - NT_B + 2)
                pool.tensor_copy(vhead[:, s2, :, VAT:VAT + HD].unsqueeze(2), v[:, :, bass.ds(g, 1), :]).then_inc(v_placed, 1)

            def trim(g, s2, s4, reads):
                last, first = band[:, s4, :, 2 * P:3 * P], band[:, s4, :, 0:P]
                pool.wait_ge(band_loaded[s2], reads)
                pool.tensor_tensor(last, last, rel[:, s2, :, NREL - 1:NREL].broadcast_to([P, NT_B, P]), ALU.subtract)\
                    .then_inc(band_step, 1)
                pool.affine_select(out=first, in_=first, compare_op=ALU.is_ge, fill=0.0, base=0,
                                   pattern=[[0, NT_B], [1, P]], channel_multiplier=-1).then_inc(band_step, 1)
                pool.wait_ge(band_step, 2 * g + 1)
                pool.tensor_tensor(last, last, inside[:, :].unsqueeze(1).broadcast_to([P, NT_B, P]), ALU.mult)\
                    .then_inc(band_ready, 1)

            place_v(0, 0)
            for g in range(2):
                trim(g, g, g, 32)

            def body(g, q, live, per):
                if live(1):
                    place_v(g + 1, (q + 1) % 2)
                if live(2):
                    trim(g + 2, q % 2, (q + 2) % NSL, 32 * per(q + 2, 2) + 32)

            stages(pool, body)

        @block.tensor
        def _(pe):
            ident = T["ident"]

            def relative(g, k, s2, loads):
                if k == 0:
                    pe.wait_ge(qb_loaded[s2], loads)
                if k == TURN_AT and not (isinstance(g, int) and g < 3):
                    pe.wait_ge(n_copied, g - 1)
                pe.wait_ge(rel_copied, NT_B * g + k + 1)
                pe.matmul(ps[:, 7, 0:NREL], qb[0:KPOS, s2, k * P:(k + 1) * P], wstack[0:KPOS, :], start=True, stop=True)\
                  .then_inc(rel_ready, 1)

            def first_scores(g, t, s4, loads):
                if t == 0:
                    pe.wait_ge(stack_loaded[s4], loads)
                pe.wait_ge(maxed, NT_B * g + t + 1)
                edge = (t + 1) * P
                for c in range(2):
                    lo, hi = c * CH, (c + 1) * CH
                    cut = min(max(edge, lo), hi)
                    first = True
                    for a, x0, x1 in ((KL_, lo, cut), (KR_, cut, hi)):
                        if x1 > x0:
                            mm = pe.matmul(ps[:, c, x0 - lo:x1 - lo], stack[Q_][0:KPOS, s4, t * P:(t + 1) * P],
                                           stack[a][0:KPOS, s4, x0:x1], start=first, stop=False, skip_group_check=True)
                            first = False
                mm.then_inc(s1_ready, 1)

            def turn_max(g):
                pe.wait_ge(dstep, 6 * g + 6)
                pe.wait_ge(rel_copied, NT_B * (g + 2) + TURN_AT + 1 if not isinstance(g, int) or 0 < g < NG - 2
                           else NT_B * min(g + 3, NG) + 1)
                pe.transpose(ps[0:NP3 * NT_B, 7, 0:P // 2].bitcast(BF16), nparts[:, :], T["ident_bf"][:, :])\
                  .then_inc(n_turned, 1)

            def second_scores(g, t, s4):
                if t == 0:
                    pe.wait_ge(n_loaded, 16 * g + 16)
                pe.wait_ge(expd, NT_B * g + t + 1)
                bank = 2 + 2 * (t % 2)
                for c in range(2):
                    lo, hi = c * CH, (c + 1) * CH
                    cut = min(max(t * P, lo), hi)
                    first = True
                    for a, x0, x1 in ((KR_, lo, cut), (KL_, cut, hi)):
                        if x1 > x0:
                            pe.matmul(ps[:, bank + c, x0 - lo:x1 - lo], stack[a][0:KALL, s4, t * P:(t + 1) * P],
                                      stack[Q_][0:KALL, s4, x0:x1], start=first, stop=False, skip_group_check=True)
                            first = False
                for i in range(max(t - 1, 0), min(t + 2, NT_B)):
                    blk = t - i + 1
                    mm = pe.matmul(ps[:, bank + i // 4, (i % 4) * P:(i % 4 + 1) * P], band[:, s4, i, blk * P:(blk + 1) * P],
                                   ident[:, :], start=False, stop=False, skip_group_check=True)
                mm.then_inc(s2_ready, 1)

            def weigh(g, t, s2):
                pe.wait_ge(expd, NT_B * g + t + 3)
                if t == 0:
                    pe.wait_ge(v_placed, g + 1)
                    pe.wait_ge(normed, g + 1)
                for c in range(2):
                    at = VAT - c * VAT
                    mm = pe.matmul(ps[0:VW, 6, :], vhead[:, s2, t, at:at + VW], probT[:, t % 2, c * CH:(c + 1) * CH],
                                   start=(t == 0 and c == 0), stop=False, skip_group_check=True)
                mm.then_inc(weighed, 1)

            def turn_out(g):
                pe.wait_ge(out_copied, g + 1)
                for j in range(CH // P):
                    mm = pe.transpose(ps[:, 6, j * P:(j + 1) * P], outT[:, j * P:(j + 1) * P], ident[:, :])
                mm.then_inc(o_turned, 1)

            pe.wait_ge(rows_set, 96)
            pe.sem_inc(weighed, 2)
            pe.sem_inc(s2_ready, 4 * NT_B)
            for g in range(3):
                for k in range(NT_B):
                    relative(g, k, g % 2, 16 * NP3 * (g // 2 + 1))
            for t in range(NT_B):
                first_scores(0, t, 0, 9 * 16)
            turn_max(0)
            pe.wait_ge(n_copied, 1)
            second_scores(0, 0, 0)

            def body(g, q, live, per):
                s4n = (q + 1) % NSL
                for t in range(NT_B):
                    if t < NT_B - 1:
                        second_scores(g, t + 1, q)
                    if live(1) and t < NT_B // 2:
                        first_scores(g + 1, 2 * t, s4n, 9 * 16 * (per(q + 1, 1) + 1))
                    weigh(g, t, q % 2)
                    if live(1) and t < NT_B // 2:
                        first_scores(g + 1, 2 * t + 1, s4n, 9 * 16 * (per(q + 1, 1) + 1))
                    if live(1) and t == TURN_AT:
                        turn_max(g + 1)
                    if live(3):
                        relative(g + 3, t, (q + 3) % 2, 16 * NP3 * (per(q + 3, 2) + 1))
                if live(1):
                    second_scores(g + 1, 0, s4n)
                turn_out(g)

            stages(pe, body)

        @block.scalar
        def _(act):
            act.sem_inc(rel_copied, 1)
            act.sem_inc(expd, 2)

            def copy_rel(g, k, s2):
                act.wait_ge(rel_ready, NT_B * g + k + 1)
                if k == 0:
                    act.wait_ge(band_ready, g + 1)
                act.activation(rel[:, s2, k, :], ps[:, 7, 0:NREL], ACT.Copy).then_inc(rel_copied, 1)

            def copy_max(g):
                act.wait_ge(n_turned, g + 1)
                if not (isinstance(g, int) and g == 0):
                    act.wait_ge(n_loaded, 16 * g)
                act.activation(nrow[:, :], ps[0:NP3 * NT_B, 7, 0:P // 2].bitcast(BF16), ACT.Copy).then_inc(n_copied, 1)

            for g in range(3):
                for k in range(NT_B):
                    copy_rel(g, k, g % 2)
            copy_max(0)

            def body(g, q, live, per):
                for t in range(NT_B):
                    act.wait_ge(s2_ready, NT_B * (g + 4) + t + 1)
                    act.wait_ge(weighed, NT_B * g + t + 1)
                    bank = 2 + 2 * (t % 2)
                    act.activation(probT[:, t % 2, :].rearrange("p (c t) -> p c t", t=CH), ps[:, bank:bank + 2, :], ACT.Exp)\
                       .then_inc(expd, 1)
                    if live(1) and t == TURN_AT:
                        copy_max(g + 1)
                    if live(3):
                        copy_rel(g + 3, t, (q + 3) % 2)
                act.wait_ge(weighed, NT_B * g + NT_B + 2)
                act.activation(outT[0:VW, :], ps[0:VW, 6, :], ACT.Copy).then_inc(out_copied, 1)

            stages(act, body)

        @block.vector
        def _(dve):
            dve.wait_ge(lowest_set, 2)
            dve.sem_inc(maxed, 1)
            dve.sem_inc(normed, 1)

            def maxima(g, t, s4):
                if t == 0:
                    dve.wait_ge(band_ready, g + 3)
                dve.wait_ge(s1_ready, NT_B * g + t + 1)
                s1 = ps[:, 0:2, :].rearrange("p c t -> p (c t)")
                lo, hi = max(t - 1, 0) * P, min(t + 2, NT_B) * P
                if lo:
                    dve.tensor_reduce(seen[:, 1, t:t + 1], s1[:, 0:lo], AX.X, ALU.max)
                if hi < SEQ:
                    dve.tensor_reduce(seen[:, 2, t:t + 1], s1[:, hi:SEQ], AX.X, ALU.max)
                off = lo - (t - 1) * P
                dve.tensor_tensor_reduce(junk[:, 0:hi - lo], s1[:, lo:hi], band[:, s4, t, off:off + hi - lo], 1.0, LOWEST,
                                         ALU.add, ALU.max, seen[:, 0, t:t + 1]).then_inc(maxed, 1)

            def split_max(g):
                n = 6 * g
                dve.wait_ge(maxed, NT_B * g + NT_B + 1)
                if not (isinstance(g, int) and g == 0):
                    dve.wait_ge(n_turned, g)
                dve.tensor_reduce(nmax[:, :], seen[:, :, :].rearrange("p k t -> p t k"), AX.X, ALU.max, negate=True)\
                   .then_inc(dstep, 1)
                for k in range(NP3):
                    p = nparts[:, k * NT_B:(k + 1) * NT_B]
                    dve.wait_ge(dstep, n + 2 * k + 1)
                    dve.tensor_copy(p, nmax[:, :]).then_inc(dstep, 1)
                    if k < NP3 - 1:
                        dve.wait_ge(dstep, n + 2 * k + 2)
                        dve.tensor_tensor(nmax[:, :], nmax[:, :], p, ALU.subtract).then_inc(dstep, 1)

            def normalise(g):
                sums = ps[:, 6, :].rearrange("p (j c x) -> p c j x", j=CH // P, x=VAT)[:, 0:2, :, :]
                dve.wait_ge(o_turned, g + 1)
                dve.reciprocal(inv[:, :].rearrange("p (c j) -> p c j", c=2).unsqueeze(3), sums[:, :, :, HD:HD + 1]).then_inc(inverted, 1)
                dve.wait_ge(inverted, g + 1)
                for c in range(2):
                    half = slice(c * (CH // P), (c + 1) * (CH // P))
                    ins = dve.tensor_tensor(oacc[:, half, bass.ds(g, 1), :].rearrange("p t o d -> p t (o d)"),
                                            sums[:, c, :, 0:HD], inv[:, half].unsqueeze(2).broadcast_to([P, CH // P, HD]), ALU.mult)
                ins.then_inc(normed, 1)

            for t in range(NT_B):
                maxima(0, t, 0)
            split_max(0)

            def body(g, q, live, per):
                if live(1):
                    for t in range(NT_B):
                        maxima(g + 1, t, (q + 1) % NSL)
                    split_max(g + 1)
                normalise(g)

            stages(dve, body)


def add_heads(nc, core, T, oacc):
    x, ps = T["xT"], T["ps"]
    with ExitStack() as st:
        turned, added = core.sem("h_turned"), core.sem("h_added")
        block = st.enter_context(nc.Block())

        @block.tensor
        def _(pe):
            for c in range(NCH):
                b, o = divmod(c, 2)
                for j in range(4):
                    mm = pe.transpose(ps[:, c, j * P:(j + 1) * P],
                                      oacc[:, 4 * o + j, b * H1:(b + 1) * H1, :].rearrange("p g d -> p (g d)"), T["ident"][:, :])
                mm.then_inc(turned, 1)

        @block.vector
        def _(dve):
            for c in range(NCH):
                b = c * CH // SEQ
                dve.wait_ge(turned, c + 1)
                dve.scalar_tensor_tensor(out=x[:, chunk(c)], in0=ps[:, c, :], scalar=T["mod"][:, 1, 2, b:b + 1],
                                         in1=x[:, chunk(c)], op0=ALU.mult, op1=ALU.add).then_inc(added, 1)


def second_attention(nc, core, T, A, dram):
    with ExitStack() as st:
        v = core.sb(st, "v1", [P, NT_B, NG, HD])
        wstack = core.sb(st, "wstack", [KPOS, NREL], BF16)
        oacc = core.sb(st, "oacc", [P, NT_B, NG, HD])
        relative_parts(nc, core, T, A, dram, v, wstack)
        relative_attention(nc, core, T, A, dram, v, wstack, oacc)
        add_heads(nc, core, T, oacc)


NE, HID = 8, 512
HF = HID // P


def experts(nc, core, T, A, out):
    x, h, ps = T["xT"], T["hT"], T["ps"]
    NT = TOK // P
    UNITS = 2 * NCH
    with ExitStack() as st:
        def sb(name, shape, dt=F32):
            return core.sb(st, "e_" + name, shape, dt)

        def sem(name):
            return core.sem("e_" + name)

        w1, w2, b1 = sb("w1", [P, 2, 2 * HID]), sb("w2", [P, 2, HF, D]), sb("b1", [P, 2, 2 * HF])
        rw, rb, b2 = sb("rw", [P, NE]), sb("rb", [1, NE]), sb("b2", [NE, D])
        logit, top, number = sb("logit", [P, NT, NE]), sb("top", [P, NT]), sb("number", [P, NE])
        mask, maskT = sb("mask", [P, NT, NE]), sb("maskT", [NE, TOK])
        sig, hid = sb("sig", [P, 2, CH]), sb("hid", [P, 2, HF, CH])
        acc = sb("acc", [P, NT, D])
        w_loaded = [sem("w0"), sem("w1")]
        loaded, numbered, routed, step = sem("loaded"), sem("numbered"), sem("routed"), sem("step")
        mask_turned, maskT_ready, b2_ready, acc_set = sem("mask_turned"), sem("maskT"), sem("b2"), sem("acc_set")
        a_ready, g_ready, sig_ready, hid_ready = sem("a"), sem("g"), sem("sig"), sem("hid")
        y_ready, summed, turned, x_ready, stored = sem("y"), sem("summed"), sem("turned"), sem("x"), sem("stored")
        block = st.enter_context(nc.Block())

        @block.sync
        def _(sp):
            sp.dma_start(rw[:, :], A["router_w"]).then_inc(loaded, 16)
            sp.dma_start(rb[:, :], A["router_b"]).then_inc(loaded, 16)
            sp.dma_start(b2[:, :], A["b2"]).then_inc(loaded, 16)
            with sp.Fori(0, NE // 2) as i:
                for s in range(2):
                    e = bass.ds(2 * i + s, 1)
                    sp.wait_ge(y_ready, UNITS * i + 1 + NCH * s)
                    sp.dma_start(w1[:, s, :], A["w1"][e, :, :].rearrange("o p n -> (o p) n")).then_inc(w_loaded[s], 16)
                    sp.dma_start(w2[:, s, :, :], A["w2"][e, :, :].rearrange("o (k p) d -> p (o k) d", p=P))\
                      .then_inc(w_loaded[s], 16)
                    sp.dma_start(b1[:, s, :], A["b1"][e, :, :].rearrange("o p n -> (o p) n")).then_inc(w_loaded[s], 16)
            for c in range(NCH):
                sp.wait_ge(x_ready, c + 1)
                sp.dma_start(out[:, chunk(c)], x[:, chunk(c)]).then_inc(stored, 16)
            sp.wait_ge(stored, 16 * NCH)

        @block.gpsimd
        def _(pool):
            for e in range(NE):
                pool.memset(number[:, e:e + 1], float(e)).then_inc(numbered, 1)

        @block.tensor
        def _(pe):
            pe.wait_ge(loaded, 48)
            for t in range(NT):
                pe.matmul(ps[:, 0, t * NE:(t + 1) * NE], h[:, t * P:(t + 1) * P], rw[:, :], start=True, stop=False)
                mm = pe.matmul(ps[:, 0, t * NE:(t + 1) * NE], T["ones"][0:1, :], rb[:, :], start=False, stop=True)
            mm.then_inc(routed, 1)
            pe.wait_ge(step, 6)
            for t in range(NT):
                mm = pe.transpose(ps[0:NE, 4 + t // 4, (t % 4) * P:(t % 4 + 1) * P], mask[:, t, :], T["ident"][:, :])
            mm.then_inc(mask_turned, 1)
            pe.wait_ge(maskT_ready, NCH)
            for t in range(NT):
                mm = pe.matmul(ps[:, t // 4, (t % 4) * P:(t % 4 + 1) * P], maskT[:, t * P:(t + 1) * P], b2[:, :],
                               start=True, stop=True)
            mm.then_inc(b2_ready, 1)
            pe.wait_ge(acc_set, NCH)
            pe.sem_inc(y_ready, 2)
            with pe.Fori(0, NE // 2) as i:
                def hidden(u):
                    n, s, c = UNITS * i + u, u // NCH, u % NCH
                    if c == 0:
                        pe.wait_ge(w_loaded[s], 48 * i + 48)
                    for f in range(HF):
                        pe.wait_ge(hid_ready, HF * n + f + 1)
                        pe.matmul(ps[:, f % 2, :], w1[:, s, f * P:(f + 1) * P], h[:, chunk(c)], start=True, stop=True)\
                          .then_inc(a_ready, 1)
                        pe.wait_ge(sig_ready, HF * n + f + 1)
                        pe.matmul(ps[:, 2 + f % 2, :], w1[:, s, HID + f * P:HID + (f + 1) * P], h[:, chunk(c)],
                                  start=True, stop=True).then_inc(g_ready, 1)

                def down(u):
                    n, s = UNITS * i + u, u // NCH
                    pe.wait_ge(hid_ready, HF * n + HF + 2)
                    pe.wait_ge(summed, 4 * n + 4)
                    for j in range(4):
                        for f in range(HF):
                            mm = pe.matmul(ps[:, 4 + u % 2, j * P:(j + 1) * P], hid[:, u % 2, f, j * P:(j + 1) * P],
                                           w2[:, s, f, :], start=(f == 0), stop=(f == HF - 1))
                    mm.then_inc(y_ready, 1)

                hidden(0)
                for u in range(1, UNITS):
                    hidden(u)
                    down(u - 1)
                down(UNITS - 1)
            pe.wait_ge(summed, 8 + 4 * NE * NCH)
            for c in range(NCH):
                for j in range(4):
                    mm = pe.transpose(ps[:, c, j * P:(j + 1) * P], acc[:, 4 * c + j, :], T["ident"][:, :])
                mm.then_inc(turned, 1)

        @block.scalar
        def _(act):
            act.sem_inc(sig_ready, 2)
            with act.Fori(0, NE // 2) as i:
                for u in range(UNITS):
                    n, s = UNITS * i + u, u // NCH
                    for f in range(HF):
                        act.wait_ge(g_ready, HF * n + f + 1)
                        act.wait_ge(hid_ready, HF * n + f + 1)
                        act.activation(sig[:, f % 2, :], ps[:, 2 + f % 2, :], ACT.Sigmoid,
                                       bias=b1[:, s, HF + f:HF + f + 1]).then_inc(sig_ready, 1)

        @block.vector
        def _(dve):
            dve.wait_ge(routed, 1)
            dve.tensor_copy(logit[:, :, :].rearrange("p t e -> p (t e)"), ps[:, 0, 0:NT * NE]).then_inc(step, 1)
            dve.wait_ge(step, 1)
            dve.tensor_reduce(top[:, :], logit[:, :, :], AX.X, ALU.max).then_inc(step, 1)
            dve.wait_ge(step, 2)
            spread = lambda ap: ap.broadcast_to([P, NT, NE])
            dve.wait_ge(numbered, NE)
            dve.tensor_tensor(logit[:, :, :], logit[:, :, :], spread(top[:, :].unsqueeze(2)), ALU.is_lt).then_inc(step, 1)
            dve.wait_ge(step, 3)
            dve.scalar_tensor_tensor(out=logit[:, :, :], in0=logit[:, :, :], scalar=float(NE), in1=spread(number[:, :].unsqueeze(1)),
                                     op0=ALU.mult, op1=ALU.add).then_inc(step, 1)
            dve.wait_ge(step, 4)
            dve.tensor_reduce(top[:, :], logit[:, :, :], AX.X, ALU.min).then_inc(step, 1)
            dve.wait_ge(step, 5)
            dve.tensor_tensor(mask[:, :, :], logit[:, :, :], spread(top[:, :].unsqueeze(2)), ALU.is_equal).then_inc(step, 1)
            dve.wait_ge(mask_turned, 1)
            for c in range(NCH):
                dve.tensor_copy(maskT[:, chunk(c)], ps[0:NE, 4 + c, :]).then_inc(maskT_ready, 1)
            dve.wait_ge(b2_ready, 1)
            for c in range(NCH):
                dve.tensor_copy(acc[:, 4 * c:4 * c + 4, :].rearrange("p t d -> p (t d)"), ps[:, c, :]).then_inc(acc_set, 1)
            dve.wait_ge(acc_set, NCH)
            dve.sem_inc(hid_ready, 2)
            dve.sem_inc(summed, 8)
            with dve.Fori(0, NE // 2) as i:
                def gate(u):
                    n, s = UNITS * i + u, u // NCH
                    dve.wait_ge(y_ready, n + 1)
                    for f in range(HF):
                        dve.wait_ge(a_ready, HF * n + f + 1)
                        dve.wait_ge(sig_ready, HF * n + f + 3)
                        dve.scalar_tensor_tensor(out=hid[:, u % 2, f, :], in0=ps[:, f % 2, :],
                                                 scalar=b1[:, s, f:f + 1], in1=sig[:, f % 2, :],
                                                 op0=ALU.add, op1=ALU.mult).then_inc(hid_ready, 1)

                def add(u):
                    n, s, c = UNITS * i + u, u // NCH, u % NCH
                    dve.wait_ge(y_ready, n + 3)
                    dve.wait_ge(summed, 4 * n + 4)
                    for j in range(4):
                        t = 4 * c + j
                        dve.scalar_tensor_tensor(out=acc[:, t, :], in0=ps[:, 4 + u % 2, j * P:(j + 1) * P],
                                                 scalar=mask[:, t, bass.ds(2 * i + s, 1)], in1=acc[:, t, :],
                                                 op0=ALU.mult, op1=ALU.add).then_inc(summed, 1)

                gate(0)
                for u in range(1, UNITS):
                    gate(u)
                    add(u - 1)
                add(UNITS - 1)
            for c in range(NCH):
                dve.wait_ge(turned, c + 1)
                b = c * CH // SEQ
                dve.scalar_tensor_tensor(out=x[:, chunk(c)], in0=ps[:, c, :], scalar=T["mod"][:, 1, 5, b:b + 1],
                                         in1=x[:, chunk(c)], op0=ALU.mult, op1=ALU.add).then_inc(x_ready, 1)


def build(nc, A, out):
    with ExitStack() as whole:
        core = Core(nc, whole)
        T = {}
        for name, shape, dt in [("xT", [P, TOK], F32), ("hT", [P, TOK], F32), ("mean_w", [P, P], F32),
                                ("ones", [P, P], F32), ("ones_bf", [P, P], BF16), ("ident_bf", [P, P], BF16), ("ident", [P, P], F32),
                                ("eps", [P, 1], F32), ("mod", [P, 2, 6, NB], F32), ("gates", [P, NB, N_ACT], F32),
                                ("gate_bo", [P, NB], F32), ("head_index", [1, NB * N_ACT], U32)]:
            T[name] = core.sb(whole, name, shape, dt)
        T["ps"] = whole.enter_context(nc.psum_tensor("ps", [P, 8, CH], F32))
        scratch = lambda n, shape, dt: nc.dram_tensor(n, shape, dt, kind="Internal").ap()
        dram = {"qk": scratch("qk_parts", [3, NP3, NB, P, SEQ], BF16), "table": scratch("table_parts", [NP3, HD + 1, NREL], BF16),
                "const": scratch("const_rows", [3, NP3, SEQ], BF16), "rel": scratch("rel_rows", [2, NT_B, P * NREL], F32)}
        dram["rows"] = [dram["qk"][a].rearrange("k b r t -> k (b r) t") for a in range(3)]
        bc_dram = nc.dram_tensor("bc_parts", [3, NB, 2, NS, SEQ], BF16, kind="Internal").ap()
        constants_and_modulation(nc, core, T, A)
        layernorm(nc, core, T, "ln0", 0, 0, T["hT"])
        for L in range(NL):
            mamba_layer(nc, core, T, A, L, bc_dram)
        core.reuse_semaphores()
        layernorm(nc, core, T, "ln1", 0, 3, T["hT"], residual=(T["hT"], 0, 2))
        route_heads(nc, core, T, A)
        chosen_heads(nc, core, T, A)
        layernorm(nc, core, T, "ln2", 1, 0, T["hT"])
        second_attention(nc, core, T, A, dram)
        layernorm(nc, core, T, "ln3", 1, 3, T["hT"])
        experts(nc, core, T, A, out)


def layout(inputs):
    import numpy as np
    f = lambda n: np.ascontiguousarray(inputs[n])
    t = lambda a: np.ascontiguousarray(np.moveaxis(a, -1, -2))
    a = {
        "xT": t(f("L0_attn_x").reshape(TOK, D)),
        "c0": t(f("L0_c")), "c1": t(f("L1_c")), "wmod0": f("L0_wmod"), "wmod1": f("L1_wmod"),
        "normw": f("L0_attn_norm_w")[:, :, None],
        "win": t(f("L0_attn_Win")), "wx": t(f("L0_attn_Wx")), "wdt": t(f("L0_attn_Wdt")), "wout": t(f("L0_attn_Wout")),
        "chan": np.concatenate([f("L0_attn_conv_w"), f("L0_attn_conv_b")[..., None], f("L0_attn_bdt")[..., None],
                                f("L0_attn_Dp")[..., None], f("L0_attn_A_log")], axis=-1),
    }
    wqkv1 = f("L1_attn_Wqkv").reshape(H1, 3, HD, D).transpose(3, 1, 0, 2).reshape(D, 3, D)
    bqkv1 = f("L1_attn_bqkv").reshape(H1, 3, HD).transpose(1, 0, 2).reshape(3, D)
    table, tbias = f("L1_attn_Wr"), f("L1_attn_br")
    a.update({
        "wqkv1": wqkv1, "bv1": bqkv1[2:3], "brow": tbias[None, [0, NREL - 1]],
        "cols1": np.stack([bqkv1[0], bqkv1[1], np.tile(table[0], H1), np.tile(table[NREL - 1], H1)], axis=-1),
        "table": np.concatenate([table.T, tbias[None, :]], axis=0),
        "table_edge": np.concatenate([table[0], tbias[0:1]])[:, None],
    })
    heads = [f(f"L0_ffn_W{n}").reshape(D, N_HEAD, DH).transpose(1, 0, 2) for n in "qkv"]
    biases = [f(f"L0_ffn_b{n}").reshape(N_HEAD, DH) for n in "qkv"]
    a.update({
        "wr": f("L0_ffn_Wr"), "br": f("L0_ffn_br")[None, :], "bo": f("L0_ffn_bo")[:, None],
        "wqkv_h": np.concatenate(heads, axis=-1), "bqkv_h": np.stack(biases, axis=-1), "bv_h": biases[2],
        "router_w": f("L1_ffn_router_w"), "router_b": f("L1_ffn_router_b")[None, :], "w1": f("L1_ffn_w1"),
        "b1": t(f("L1_ffn_b1").reshape(NE, 2 * HF, P)), "w2": f("L1_ffn_w2"), "b2": f("L1_ffn_b2"),
        "wo_k": f("L0_ffn_Wo").reshape(N_ACT, DH, D),
    })
    return {k: np.ascontiguousarray(v) for k, v in a.items()}


def kernel(**inputs):
    import numpy as _np
    import concourse.bacc as _bacc
    from concourse import mybir as _mybir
    from concourse.bass_utils import run_bass_kernel_spmd as _run

    nc = _bacc.Bacc("TRN2", target_bir_lowering=False, num_devices=1)
    arrays = layout(inputs)
    aps = {n: nc.dram_tensor(f"in_{n}", a.shape, _mybir.dt.from_np(a.dtype), kind="ExternalInput").ap()
           for n, a in arrays.items()}
    out = nc.dram_tensor("out_xT", (D, TOK), _mybir.dt.float32, kind="ExternalOutput").ap()
    build(nc, aps, out)
    r = _run(nc, [{f"in_{n}": a for n, a in arrays.items()}], core_ids=[0])
    return _np.ascontiguousarray(r.results[0]["out_xT"].T).reshape(NB, SEQ, D)
```

```python
from contextlib import ExitStack
import concourse.bass as bass
from concourse import mybir

F32 = mybir.dt.float32
BF16 = mybir.dt.bfloat16
U32 = mybir.dt.uint32
ALU = mybir.AluOpType
ACT = mybir.ActivationFunctionType
AX = mybir.AxisListType

P = 128
NB = 2
SEQ = 1024
TOK = NB * SEQ
D = 128
CH = 512
NCH = TOK // CH
EPS = 1e-5
NL = 2
ED = 256
NH2 = ED // P
NS = 16
RK = 64
NCONV = 4
MOD_S, MOD_C, MOD_G = 0, 1, 2
E_MAMBA_ROWS = 2 * NS


class Core:

    def __init__(self, nc, whole):
        self.nc = nc
        self.whole = whole
        self.sems = []

    def sb(self, stack, name, shape, dt=F32):
        return stack.enter_context(self.nc.sbuf_tensor(name, shape, dt))

    def sem(self, name):
        handle = self.nc.alloc_semaphore(name=name)
        self.sems.append(handle)
        return handle

    def reuse_semaphores(self):
        self.nc.clear_and_free_semaphores(self.sems)
        self.nc.all_engine_barrier()
        self.sems = []


def chunk(c):
    return slice(c * CH, (c + 1) * CH)


def constants_and_modulation(nc, core, T, A):
    with ExitStack() as st:
        cT = core.sb(st, "cT", [P, 2, NB])
        silu_c = core.sb(st, "silu_c", [P, 2, NB])
        wmod = core.sb(st, "wmod", [P, 2, 6 * D])
        sign = core.sb(st, "gate_sign", [P, 2, 2, NB])
        size = core.sb(st, "gate_size", [P, 2, 2, NB])
        x_loaded, c_loaded, wmod_loaded = core.sem("x_loaded"), core.sem("c_loaded"), core.sem("wmod_loaded")
        silu_ready, mod_summed = core.sem("silu_c_ready"), core.sem("mod_summed")
        mod_step, const_ready = core.sem("mod_step"), core.sem("const_ready")
        block = st.enter_context(nc.Block())

        @block.sync
        def _(sp):
            for l in range(2):
                sp.dma_start(cT[:, l, :], A[f"c{l}"]).then_inc(c_loaded, 16)
                sp.dma_start(wmod[:, l, :], A[f"wmod{l}"]).then_inc(wmod_loaded, 16)
            sp.dma_start(T["xT"][:, :], A["xT"]).then_inc(x_loaded, 16)
            sp.wait_ge(x_loaded, 16)

        @block.gpsimd
        def _(pool):
            pool.memset(T["mean_w"][:, :], 1.0 / D).then_inc(const_ready, 1)
            pool.memset(T["ones_bf"][:, :], 1.0).then_inc(const_ready, 1)
            pool.memset(T["ones"][:, :], 1.0).then_inc(const_ready, 1)
            pool.memset(T["eps"][:, :], EPS).then_inc(const_ready, 1)
            pool.memset(T["ident"][:, :], 0.0).then_inc(const_ready, 1)
            pool.wait_ge(const_ready, 5)
            pool.affine_select(out=T["ident"][:, :], in_=T["ident"][:, :], compare_op=ALU.not_equal, fill=1.0,
                               base=0, pattern=[[-1, P]], channel_multiplier=1).then_inc(const_ready, 1)
            pool.wait_ge(const_ready, 6)
            pool.tensor_copy(T["ident_bf"][:, :], T["ident"][:, :]).then_inc(const_ready, 1)

        @block.scalar
        def _(act):
            act.wait_ge(c_loaded, 32)
            act.activation(silu_c[:, :, :], cT[:, :, :], ACT.Silu).then_inc(silu_ready, 1)

        @block.tensor
        def _(pe):
            pe.wait_ge(silu_ready, 1)
            pe.wait_ge(wmod_loaded, 32)
            for l in range(2):
                for j in range(6):
                    at = (l * 6 + j) * NB
                    mm = pe.matmul(T["ps"][:, 0, at:at + NB], wmod[:, l, j * D:(j + 1) * D], silu_c[:, l, :],
                                   start=True, stop=True)
            mm.then_inc(mod_summed, 1)

        @block.vector
        def _(dve):
            mod = T["mod"]
            dve.wait_ge(mod_summed, 1)
            dve.tensor_copy(mod[:, :, :, :].rearrange("p l j b -> p (l j b)"), T["ps"][:, 0, 0:2 * 6 * NB])\
               .then_inc(mod_step, 1)
            dve.wait_ge(mod_step, 1)
            scales = mod[:, :, 1::3, :]
            gates = mod[:, :, 2::3, :]
            dve.tensor_scalar(scales, scales, 1.0, None, ALU.add).then_inc(mod_step, 1)
            dve.tensor_scalar(sign[:, :, :, :], gates, 0.0, 2.0, ALU.is_ge, ALU.mult).then_inc(mod_step, 1)
            dve.scalar_tensor_tensor(out=size[:, :, :, :], in0=gates, scalar=-1.0, in1=gates,
                                     op0=ALU.mult, op1=ALU.max).then_inc(mod_step, 1)
            dve.wait_ge(mod_step, 4)
            dve.tensor_scalar(size[:, :, :, :], size[:, :, :, :], 0.25, None, ALU.max).then_inc(mod_step, 1)
            dve.wait_ge(mod_step, 5)
            dve.scalar_tensor_tensor(out=gates, in0=sign[:, :, :, :], scalar=-1.0, in1=size[:, :, :, :],
                                     op0=ALU.add, op1=ALU.mult).then_inc(mod_step, 1)


def column_means(pe, T, sq, c, bank, first_wait=None):
    for j in range(CH // P):
        t = c * (CH // P) + j
        mm = pe.matmul(T["ps"][:, bank, t:t + 1], sq[:, t * P:(t + 1) * P], T["mean_w"][:, 0:1], start=True, stop=True)
    return mm


def layernorm(nc, core, T, name, layer, part, dst, residual=None):
    x, ps, mod = T["xT"], T["ps"], T["mod"]
    NT = TOK // P
    TC = CH // P
    with ExitStack() as st:
        cen = core.sb(st, name + "_centred", [P, TOK])
        sq = core.sb(st, name + "_square", [P, TOK])
        diag = core.sb(st, name + "_diag", [P, TOK])
        rstd = core.sb(st, name + "_rstd", [P, NT])
        mean_ready, centred, squared = core.sem(name + "_mean"), core.sem(name + "_centred"), core.sem(name + "_squared")
        var_ready, std_ready, rstd_ready = core.sem(name + "_var"), core.sem(name + "_std"), core.sem(name + "_rstd")
        diag_ready, spread = core.sem(name + "_diag"), core.sem(name + "_spread")
        normed, done, x_added = core.sem(name + "_normed"), core.sem(name + "_done"), core.sem(name + "_residual")
        block = st.enter_context(nc.Block())

        @block.tensor
        def _(pe):
            for c in range(NCH):
                if residual is not None:
                    pe.wait_ge(x_added, c + 1)
                pe.matmul(ps[:, c, :], T["mean_w"][:, :], x[:, chunk(c)], start=True, stop=True).then_inc(mean_ready, 1)
            for c in range(NCH):
                pe.wait_ge(squared, c + 1)
                mm = column_means(pe, T, sq, c, 4)
            mm.then_inc(var_ready, 1)
            for c in range(NCH):
                pe.wait_ge(diag_ready, (c + 1) * TC)
                pe.matmul(ps[:, c, :], T["ones"][:, :], diag[:, chunk(c)], start=True, stop=True).then_inc(spread, 1)

        @block.scalar
        def _(act):
            for c in range(NCH):
                act.wait_ge(centred, c + 1)
                act.activation(sq[:, chunk(c)], cen[:, chunk(c)], ACT.Square).then_inc(squared, 1)
            act.wait_ge(var_ready, 1)
            act.activation(rstd[:, :], ps[:, 4, 0:NT], ACT.Sqrt, bias=T["eps"][:, 0:1]).then_inc(std_ready, 1)
            for c in range(NCH):
                b = c * CH // SEQ
                act.wait_ge(normed, c + 1)
                act.activation(dst[:, chunk(c)], cen[:, chunk(c)], ACT.Identity, bias=mod[:, layer, part, b:b + 1])\
                   .then_inc(done, 1)

        @block.vector
        def _(dve):
            if residual is not None:
                src, l, j = residual
                for c in range(NCH):
                    b = c * CH // SEQ
                    dve.scalar_tensor_tensor(out=x[:, chunk(c)], in0=src[:, chunk(c)], scalar=mod[:, l, j, b:b + 1],
                                             in1=x[:, chunk(c)], op0=ALU.mult, op1=ALU.add).then_inc(x_added, 1)
            for c in range(NCH):
                dve.wait_ge(mean_ready, c + 1)
                dve.tensor_tensor(cen[:, chunk(c)], x[:, chunk(c)], ps[:, c, :], ALU.subtract).then_inc(centred, 1)
            dve.wait_ge(std_ready, 1)
            dve.reciprocal(rstd[:, :], rstd[:, :]).then_inc(rstd_ready, 1)
            dve.wait_ge(rstd_ready, 1)
            for t in range(NT):
                dve.tensor_scalar(diag[:, t * P:(t + 1) * P], T["ident"][:, :], rstd[:, t:t + 1], None, ALU.mult)\
                   .then_inc(diag_ready, 1)
            dve.wait_ge(centred, NCH)
            for c in range(NCH):
                b = c * CH // SEQ
                dve.wait_ge(spread, c + 1)
                dve.scalar_tensor_tensor(out=cen[:, chunk(c)], in0=cen[:, chunk(c)],
                                         scalar=mod[:, layer, part + 1, b:b + 1], in1=ps[:, c, :],
                                         op0=ALU.mult, op1=ALU.mult).then_inc(normed, 1)


def log1p_factors(degree=8):
    import numpy as np
    f = lambda e: np.log1p(e) / e
    poly = np.polynomial.chebyshev.Chebyshev.interpolate(f, degree, domain=[0, 1])\
        .convert(kind=np.polynomial.Polynomial, domain=[-1, 1], window=[-1, 1])
    s = poly.coef[-1] ** (1 / degree)
    roots = [z for z in poly.roots() if z.imag > 0]
    assert len(roots) == degree // 2
    return float(s), [(float(-s * z.real), float((s * z.imag) ** 2)) for z in roots]


def mamba_layer(nc, core, T, A, L, bc_dram):
    h, ps = T["hT"], T["ps"]
    n = f"m{L}_"
    with ExitStack() as st:
        def sb(name, shape, dt=F32):
            return core.sb(st, n + name, shape, dt)

        def sem(name):
            return core.sem(n + name)

        win = sb("win", [P, 2 * ED])
        wx = sb("wx", [P, NH2, RK + 2 * NS])
        wdt = sb("wdt", [RK, ED])
        wout = sb("wout", [P, NH2, D])
        normw = sb("normw", [P, 1])
        chan = sb("chan", [P, NH2, NCONV + 3 + NS])
        TAP, CB, BDT, DP, AL = 0, NCONV, NCONV + 1, NCONV + 2, NCONV + 3
        rate = sb("rate", [P, NH2, NS])
        diag_d = sb("diag_d", [P, NH2, P])
        silu_z = sb("silu_z", [P, NH2, TOK])
        xs = sb("xs", [P, NH2, TOK])
        delta = sb("delta", [P, NH2, TOK])
        du = sb("du", [P, NH2, TOK])
        decay = sb("decay", [P, 2, NH2, SEQ])
        drive = sb("drive", [P, 2, NH2, SEQ])
        PADW = NCONV - 1 + SEQ
        work = sb("work", [P, NH2 * NB * PADW])
        pad = work[:, :].rearrange("p (m b t) -> p m b t", m=NH2, b=NB)
        prod = work[:, 0:2 * NH2 * SEQ].rearrange("p (s m t) -> p s m t", s=2, m=NH2)
        hs = sb("hs", [P, NH2, SEQ])
        bc = sb("bc", [P, 2, 2, SEQ])
        rows = sb("rows", [3, 2, 2, SEQ], BF16)
        xn = hs[:, :, :].rearrange("p m t -> p (m t)")
        rs = bc[:, 0, :, :].rearrange("p m t -> p (m t)")
        dtr = bc[0:RK, 1, :, :].rearrange("p m t -> p (m t)")
        parts = drive[:, 0, :, :].rearrange("p m t -> p (m t)").bitcast(BF16).rearrange("p (k t) -> p k t", k=2)
        part3 = drive[:, 1, 0, :].bitcast(BF16)
        rest = decay[:, 0, :, :].rearrange("p m t -> p (m t)")
        rest2 = decay[:, 1, :, :].rearrange("p m t -> p (m t)")
        BCR = slice(RK, RK + 2 * NS)
        flat = decay[:, :, :, :].rearrange("p s m t -> p (s m t)")
        flat2 = drive[:, :, :, :].rearrange("p s m t -> p (s m t)")

        rdiag = drive[:, 0, :, :].rearrange("p m t -> p (m t)")
        rstd = sb("rstd", [P, TOK // P])
        slope, factors = log1p_factors()
        shifts = sb("log_shifts", [P, len(factors)])

        loaded = sem("loaded")
        diag_ready, spread_ready = sem("diag"), sem("spread")
        vmax, sq_ready, log_step, delta_ready, du_ready = (sem(x) for x in ("vmax", "sq", "log", "delta", "du"))
        squared, ms_ready, std_ready, rstd_ready, normed = (sem(x) for x in ("squared", "ms", "std", "rstd", "normed"))
        proj_ready, z_ready, xc_copied = sem("proj"), sem("z"), sem("xc")
        pad_zero, conv_step, conv_done, xs_ready = sem("padzero"), sem("convstep"), sem("conv"), sem("xs")
        small = sem("small")
        neg = sem("neg")
        dbc_ready, dt_copied, split_step, bc_stored = sem("dbc"), sem("dt"), sem("split"), sem("bcstored")
        dl_ready, ab_ready, ex_ready = (sem(x) for x in ("dl", "abs", "exp"))
        rows_ready = [[sem(f"{v}rows{i}") for i in range(2)] for v in "bc"]
        row_spread, row_copied = [sem("bspread"), sem("cspread")], [sem("bcopied"), sem("ccopied")]
        decay_ready, drive_ready = sem("decay"), sem("drive")
        scanned, multiplied, y_summed = sem("scanned"), sem("multiplied"), sem("ysum")
        y_init, gated, out_ready, added = sem("yinit"), sem("gated"), sem("out"), sem("added")

        block = st.enter_context(nc.Block())
        B_, C_ = 0, 1

        def steps(eng, b, body, first=0):
            last = b == NB - 1
            with eng.Fori(first // 2, NS // 2 - 2 * last) as i:
                for s in range(2):
                    body(b * NS + 2 * i + s, 2 * i + s, s, lambda k: True)
            if last:
                for n in range(NS - 4, NS):
                    body(b * NS + n, n, n % 2, lambda k: n + k < NS)

        @block.sync
        def _(sp):
            sp.dma_start(win[:, :], A["win"][L]).then_inc(loaded, 16)
            sp.dma_start(normw[:, :], A["normw"][L]).then_inc(loaded, 16)
            sp.dma_start(chan[:, :, :], A["chan"][L].rearrange("(m p) k -> p m k", p=P)).then_inc(loaded, 16)
            sp.dma_start(wx[:, :, :], A["wx"][L].rearrange("(m p) r -> p m r", p=P)).then_inc(loaded, 16)
            sp.dma_start(wdt[:, :], A["wdt"][L]).then_inc(loaded, 16)
            sp.dma_start(wout[:, :, :], A["wout"][L].rearrange("(m p) d -> p m d", p=P)).then_inc(loaded, 16)
            sp.wait_ge(split_step, 4 * 5)
            for k in range(3):
                src = parts[BCR, k, :] if k < 2 else part3[BCR, :]
                sp.dma_start(bc_dram[k].rearrange("b v n t -> (v n) b t"), src.rearrange("n (b t) -> n b t", b=NB))\
                  .then_inc(bc_stored, 16)
            sp.wait_ge(bc_stored, 48)
            for b in range(NB):
                with sp.Fori(0, NS // 2) as i:
                    for s in range(2):
                        for v in (B_, C_):
                            sp.wait_ge(row_spread[v], b * NS + 2 * i + s + 1)
                            sp.dma_start(rows[:, v, s, :], bc_dram[:, b, v, bass.ds(2 * i + s, 1), :].rearrange('k n t -> k (n t)'))\
                              .then_inc(rows_ready[v][s], 16)

        @block.gpsimd
        def _(pool):
            for m in range(NH2):
                pool.memset(pad[:, m, :, 0:NCONV - 1], 0.0).then_inc(pad_zero, 1)
            pool.wait_ge(loaded, 96)
            for m in range(NH2):
                pool.tensor_scalar(diag_d[:, m, :], T["ident"][:, :], chan[:, m, DP:DP + 1], None, ALU.mult)\
                    .then_inc(small, 1)
            for i, (shift, _) in enumerate(factors):
                pool.memset(shifts[:, i:i + 1], shift).then_inc(small, 1)
            for u in range(4):
                b, m = divmod(u, NH2)
                t = slice(b * SEQ, (b + 1) * SEQ)
                pool.wait_ge(delta_ready, u + 1)
                pool.wait_ge(xs_ready, u + 1)
                pool.tensor_tensor(du[:, m, t], delta[:, m, t], xs[:, m, t], ALU.mult).then_inc(du_ready, 1)
            pool.wait_ge(du_ready, 4)
            pool.sem_inc(drive_ready, 2)
            for b in range(NB):
                with pool.Fori(0, NS // 2) as i:
                    for s in range(2):
                        g = b * NS + 2 * i + s
                        pool.wait_ge(row_copied[B_], g + 1)
                        pool.wait_ge(scanned, 2 * (g + 1))
                        pool.tensor_tensor(drive[:, s, :, :], du[:, :, b * SEQ:(b + 1) * SEQ],
                                           bc[:, B_, s:s + 1, :].broadcast_to([P, NH2, SEQ]), ALU.mult).then_inc(drive_ready, 1)

        @block.tensor
        def _(pe):
            for c in range(NCH):
                pe.wait_ge(squared, c + 1)
                mm = column_means(pe, T, rs, c, 4)
            mm.then_inc(ms_ready, 1)
            for c in range(NCH):
                pe.wait_ge(diag_ready, (c + 1) * (CH // P))
                pe.matmul(ps[:, c, :], T["ones"][:, :], rdiag[:, chunk(c)], start=True, stop=True).then_inc(spread_ready, 1)
            pe.wait_ge(loaded, 96)
            for c in range(NCH):
                pe.wait_ge(normed, c + 1)
                for m in range(4):
                    if c == 0 and m == 0:
                        pe.wait_ge(normed, NCH)
                    if c >= 2:
                        pe.wait_ge(z_ready, 2 * (c - 1))
                        pe.wait_ge(xc_copied, 2 * (c - 1))
                    pe.matmul(ps[:, (c % 2) * 4 + m, :], win[:, m * P:(m + 1) * P], xn[:, chunk(c)],
                              start=True, stop=True).then_inc(proj_ready, 1)
            pe.wait_ge(z_ready, 8)
            pe.wait_ge(xc_copied, 8)
            for c in range(NCH):
                pe.wait_ge(xs_ready, 2 * (c // 2) + 2)
                for m in range(NH2):
                    mm = pe.matmul(ps[0:RK + 2 * NS, c, :], wx[:, m, :], xs[:, m, chunk(c)],
                                   start=(m == 0), stop=(m == NH2 - 1))
                mm.then_inc(dbc_ready, 1)
            for b in range(NB):
                for m in range(NH2):
                    u = b * NH2 + m
                    if u < 2:
                        pe.wait_ge(dt_copied, 2 * b + 2)
                    else:
                        pe.wait_ge(dt_copied, NCH)
                        pe.wait_ge(split_step, 4 * 5)
                    for c in range(2):
                        mm = pe.matmul(ps[:, (4 + 2 * u + c) % 8, :], wdt[:, m * P:(m + 1) * P],
                                       dtr[:, chunk(2 * b + c)], start=True, stop=True)
                    mm.then_inc(dl_ready, 1)
            pe.wait_ge(small, 2)
            for x in (*row_spread, y_summed):
                pe.sem_inc(x, 2)

            def spread(v, s, turn, before):
                pe.wait_ge(rows_ready[v][s], 16 * turn)
                if not isinstance(before, int) or before:
                    pe.wait_ge(row_copied[v], before)
                for c in range(2):
                    mm = pe.matmul(ps[:, 4 + 2 * v + c, :], T["ones_bf"][0:3, :],
                                   rows[:, v, s, c * CH:(c + 1) * CH], start=True, stop=True)
                mm.then_inc(row_spread[v], 1)

            def start_sums(b):
                for m in range(NH2):
                    for c in range(2):
                        mm = pe.matmul(ps[:, 2 * m + c, :], diag_d[:, m, :], xs[:, m, chunk(2 * b + c)],
                                       start=True, stop=False, skip_group_check=True)
                mm.then_inc(y_init, 1)

            pe.wait_ge(ab_ready, 4)
            pe.wait_ge(vmax, 4)
            start_sums(0)
            spread(B_, 0, 1, 0)
            spread(C_, 0, 1, 0)
            spread(B_, 1, 1, 1)
            spread(B_, 0, 2, 2)
            spread(C_, 1, 1, 1)
            for b in range(NB):
                def step(g, n, s, live):
                    turn = lambda k: (g - s) // 2 + (s + k) // 2 + 1
                    for m in range(NH2):
                        pe.wait_ge(multiplied, 2 * g + 5 + m)
                        for c in range(2):
                            mm = pe.matmul(ps[:, 2 * m + c, :], T["ident"][:, :], prod[:, s, m, c * CH:(c + 1) * CH],
                                           start=False, stop=False, skip_group_check=True)
                        if m == 0 and live(3):
                            spread(B_, 1 - s, turn(3), g + 3)
                    mm.then_inc(y_summed, 1)
                    if live(2):
                        spread(C_, s, turn(2), g + 2)

                steps(pe, b, step)
                pe.wait_ge(gated, 2 * (b + 1))
                for c in range(2):
                    for m in range(NH2):
                        mm = pe.matmul(ps[:, c, :], wout[:, m, :], silu_z[:, m, chunk(2 * b + c)],
                                       start=(m == 0), stop=(m == NH2 - 1))
                    mm.then_inc(out_ready, 1)
                if b < NB - 1:
                    pe.wait_ge(added, 2 * (b + 1))
                    start_sums(b + 1)

        @block.scalar
        def _(act):
            for c in range(NCH):
                act.activation(rs[:, chunk(c)], h[:, chunk(c)], ACT.Square).then_inc(squared, 1)
            act.wait_ge(ms_ready, 1)
            act.activation(rstd[:, :], ps[:, 4, 0:TOK // P], ACT.Sqrt, bias=T["eps"][:, 0:1]).then_inc(std_ready, 1)
            for c in range(NCH):
                for m in range(NH2):
                    act.wait_ge(proj_ready, 4 * c + 3 + m)
                    act.activation(silu_z[:, m, chunk(c)], ps[:, (c % 2) * 4 + NH2 + m, :], ACT.Silu)\
                       .then_inc(z_ready, 1)
            act.wait_ge(loaded, 96)
            for b in range(NB):
                for m in range(NH2):
                    t = slice(b * SEQ, (b + 1) * SEQ)
                    act.wait_ge(conv_done, 2 * b + m + 1)
                    act.activation(xs[:, m, t], xs[:, m, t], ACT.Silu, bias=chan[:, m, CB:CB + 1]).then_inc(xs_ready, 1)
            act.activation(rate[:, :, :], chan[:, :, AL:AL + NS], ACT.Exp).then_inc(neg, 1)
            NF = len(factors)
            act.wait_ge(small, NH2 + NF)
            for u in range(4):
                b, m = divmod(u, NH2)
                q = slice(u * SEQ, (u + 1) * SEQ)
                bank = (4 + 2 * u) % 8
                act.wait_ge(dl_ready, u + 1)
                act.wait_ge(vmax, u + 1)
                act.wait_ge(split_step, 4 * 5)
                act.activation(flat[:, q].rearrange("p (a t) -> p a t", a=2), ps[:, bank:bank + 2, :], ACT.Abs,
                               bias=chan[:, m, BDT:BDT + 1]).then_inc(ab_ready, 1)
                act.wait_ge(ab_ready, u + 1)
                act.activation(flat[:, q], flat[:, q], ACT.Exp, scale=-1.0).then_inc(ex_ready, 1)
            for u in range(4):
                q = slice(u * SEQ, (u + 1) * SEQ)
                act.wait_ge(ex_ready, u + 1)
                for i in range(NF):
                    k = u * NF + i
                    if k >= 2:
                        act.wait_ge(log_step, k - 1)
                    act.activation(hs[:, k % 2, :], flat[:, q], ACT.Square, scale=slope, bias=shifts[:, i:i + 1])\
                       .then_inc(sq_ready, 1)
            act.wait_ge(neg, 2)
            act.wait_ge(delta_ready, 4)

            def copy_row(v, s, spread, used, uses):
                act.wait_ge(row_spread[v], spread)
                act.wait_ge(used, uses)
                act.activation(bc[:, v, s, :].rearrange("p (c t) -> p c t", t=CH), ps[:, 4 + 2 * v:6 + 2 * v, :],
                               ACT.Copy).then_inc(row_copied[v], 1)

            copy_row(B_, 0, 3, drive_ready, 1)
            for b in range(NB):
                def step(g, n, s, live):
                    for m in range(NH2):
                        act.wait_ge(scanned, 2 * g + 1 + m)
                        act.activation(decay[:, s, m, :], delta[:, m, b * SEQ:(b + 1) * SEQ], ACT.Exp,
                                       scale=rate[:, m, bass.ds(n, 1)]).then_inc(decay_ready, 1)
                    if live(1):
                        copy_row(B_, 1 - s, g + 4, drive_ready, g + 2)
                    copy_row(C_, s, g + 3, multiplied, 2 * g + 2)

                steps(act, b, step)

        @block.vector
        def _(dve):
            dve.wait_ge(loaded, 96)
            dve.wait_ge(std_ready, 1)
            dve.reciprocal(rstd[:, :], rstd[:, :]).then_inc(rstd_ready, 1)
            dve.wait_ge(rstd_ready, 1)
            for t in range(TOK // P):
                dve.tensor_scalar(rdiag[:, t * P:(t + 1) * P], T["ident"][:, :], rstd[:, t:t + 1], None, ALU.mult)\
                   .then_inc(diag_ready, 1)
            for c in range(NCH):
                dve.wait_ge(spread_ready, c + 1)
                dve.scalar_tensor_tensor(out=xn[:, chunk(c)], in0=h[:, chunk(c)], scalar=normw[:, 0:1],
                                         in1=ps[:, c, :], op0=ALU.mult, op1=ALU.mult).then_inc(normed, 1)
            dve.wait_ge(pad_zero, 2)
            for c in range(NCH):
                b, o = divmod(c, 2)
                for m in range(NH2):
                    dve.wait_ge(proj_ready, 4 * c + 1 + m)
                    dve.tensor_copy(pad[:, m, b, NCONV - 1 + o * CH:NCONV - 1 + (o + 1) * CH],
                                    ps[:, (c % 2) * 4 + m, :]).then_inc(xc_copied, 1)
            step = 0
            for b in range(NB):
                for m in range(NH2):
                    t = xs[:, m, b * SEQ:(b + 1) * SEQ]
                    dve.wait_ge(xc_copied, 4 * b + 4)
                    dve.tensor_scalar(t, pad[:, m, b, 0:SEQ], chan[:, m, TAP:TAP + 1], None, ALU.mult)\
                       .then_inc(conv_step, 1)
                    step += 1
                    for k in range(1, NCONV):
                        dve.wait_ge(conv_step, step)
                        last = dve.scalar_tensor_tensor(out=t, in0=pad[:, m, b, k:k + SEQ],
                                                        scalar=chan[:, m, TAP + k:TAP + k + 1], in1=t,
                                                        op0=ALU.mult, op1=ALU.add)
                        if k < NCONV - 1:
                            last.then_inc(conv_step, 1)
                            step += 1
                    last.then_inc(conv_done, 1)
            for c in range(NCH):
                dve.wait_ge(dbc_ready, c + 1)
                dve.tensor_copy(dtr[:, chunk(c)], ps[0:RK, c, :]).then_inc(dt_copied, 1)
            for c in range(NCH):
                k = 5 * c
                dve.tensor_copy(parts[BCR, 0, chunk(c)], ps[BCR, c, :]).then_inc(split_step, 1)
                dve.wait_ge(split_step, k + 1)
                dve.tensor_tensor(rest[BCR, chunk(c)], ps[BCR, c, :], parts[BCR, 0, chunk(c)], ALU.subtract)\
                   .then_inc(split_step, 1)
                dve.wait_ge(split_step, k + 2)
                dve.tensor_copy(parts[BCR, 1, chunk(c)], rest[BCR, chunk(c)]).then_inc(split_step, 1)
                dve.wait_ge(split_step, k + 3)
                dve.tensor_tensor(rest2[BCR, chunk(c)], rest[BCR, chunk(c)], parts[BCR, 1, chunk(c)], ALU.subtract)\
                   .then_inc(split_step, 1)
                dve.wait_ge(split_step, k + 4)
                dve.tensor_copy(part3[BCR, chunk(c)], rest2[BCR, chunk(c)]).then_inc(split_step, 1)
            dve.wait_ge(neg, 1)
            dve.tensor_scalar(rate[:, :, :], rate[:, :, :], -1.0, None, ALU.mult).then_inc(neg, 1)
            for u in range(4):
                b, m = divmod(u, NH2)
                bank = (4 + 2 * u) % 8
                dve.wait_ge(dl_ready, u + 1)
                dve.tensor_scalar(du[:, m, b * SEQ:(b + 1) * SEQ].rearrange("p (a t) -> p a t", a=2),
                                  ps[:, bank:bank + 2, :], chan[:, m, BDT:BDT + 1], 0.0, ALU.add, ALU.max)\
                   .then_inc(vmax, 1)
            NF = len(factors)
            dve.wait_ge(bc_stored, 48)
            for u in range(4):
                b, m = divmod(u, NH2)
                t = slice(b * SEQ, (b + 1) * SEQ)
                q = slice(u * SEQ, (u + 1) * SEQ)
                for i in range(NF):
                    k = u * NF + i
                    dve.wait_ge(sq_ready, k + 1)
                    if i:
                        dve.wait_ge(log_step, k)
                    dve.scalar_tensor_tensor(out=flat2[:, q], in0=hs[:, k % 2, :], scalar=factors[i][1],
                                             in1=flat2[:, q] if i else flat[:, q], op0=ALU.add, op1=ALU.mult)\
                       .then_inc(log_step, 1)
                dve.wait_ge(log_step, (u + 1) * NF)
                dve.tensor_tensor(delta[:, m, t], flat2[:, q], du[:, m, t], ALU.add).then_inc(delta_ready, 1)
            dve.sem_inc(scanned, 4)
            dve.sem_inc(multiplied, 4)

            def add_output(b):
                for c in range(2):
                    dve.wait_ge(out_ready, 2 * b + c + 1)
                    tt = chunk(2 * b + c)
                    dve.tensor_tensor(h[:, tt], h[:, tt], ps[:, c, :], ALU.add).then_inc(added, 1)

            def step(g, n, s, live):
                dve.wait_ge(drive_ready, g + 3)
                for m in range(NH2):
                    dve.wait_ge(decay_ready, 2 * g + 1 + m)
                    dve.wait_ge(multiplied, 2 * g + 3 + m)
                    dve.tensor_tensor_scan(hs[:, m, :], decay[:, s, m, :], drive[:, s, m, :], 0.0,
                                           ALU.mult, ALU.add).then_inc(scanned, 1)
                dve.wait_ge(row_copied[C_], g + 1)
                dve.wait_ge(y_summed, g + 1)
                for m in range(NH2):
                    dve.wait_ge(scanned, 2 * g + 5 + m)
                    dve.tensor_tensor(prod[:, s, m, :], hs[:, m, :], bc[:, C_, s, :], ALU.mult).then_inc(multiplied, 1)

            for b in range(NB):
                if b:
                    step(b * NS, 0, 0, None)
                    add_output(b - 1)
                    step(b * NS + 1, 1, 1, None)
                steps(dve, b, step, first=2 if b else 0)
                dve.wait_ge(y_init, b + 1)
                dve.wait_ge(y_summed, 2 + (b + 1) * NS)
                for m in range(NH2):
                    z = silu_z[:, m, b * SEQ:(b + 1) * SEQ].rearrange("p (a t) -> p a t", a=2)
                    dve.tensor_tensor(z, ps[:, 2 * m:2 * m + 2, :], z, ALU.mult).then_inc(gated, 1)
            add_output(NB - 1)


N_HEAD, N_ACT, DH = 16, 4, 64
NT_B = SEQ // P


def route_heads(nc, core, T, A):
    h, ps = T["hT"], T["ps"]
    with ExitStack() as st:
        def sb(name, shape, dt=F32):
            return core.sb(st, "r_" + name, shape, dt)
        wr, br, bo = sb("wr", [P, N_HEAD]), sb("br", [NB, N_HEAD]), sb("bo", [P, 1])
        hsum, logit, nmax = sb("hsum", [P, NB]), sb("logit", [NB, N_HEAD]), sb("nmax", [NB, 1])
        top, dist, total = sb("top", [NB, 8]), sb("dist", [NB, N_HEAD]), sb("total", [NB, 3])
        val, idx = sb("val", [NB, 8]), sb("idx", [NB, 8], U32)
        ev, ez, gates = sb("ev", [NB, N_ACT]), sb("ez", [NB, 1]), sb("gates", [NB, N_ACT])
        loaded, step, act_step, pe_step, moved = (core.sem("r_" + x) for x in ("loaded", "dve", "act", "pe", "moved"))
        block = st.enter_context(nc.Block())

        @block.sync
        def _(sp):
            sp.dma_start(wr[:, :], A["wr"]).then_inc(loaded, 16)
            for b in range(NB):
                sp.dma_start(br[b:b + 1, :], A["br"]).then_inc(loaded, 16)
            sp.dma_start(bo[:, :], A["bo"]).then_inc(loaded, 16)
            sp.wait_ge(step, 9)
            for b in range(NB):
                sp.dma_start(T["head_index"][0:1, b * N_ACT:(b + 1) * N_ACT], idx[b:b + 1, 0:N_ACT]).then_inc(moved, 16)
            sp.wait_ge(moved, 32)

        @block.tensor
        def _(pe):
            pe.wait_ge(loaded, 64)
            pe.wait_ge(step, 2)
            pe.matmul(ps[0:NB, 0, 0:N_HEAD], hsum[:, :], wr[:, :], start=True, stop=True).then_inc(pe_step, 1)
            pe.wait_ge(step, 14)
            for b in range(NB):
                mm = pe.matmul(ps[:, 1, b * N_ACT:(b + 1) * N_ACT], T["ident"][0:NB, b:b + 1].broadcast_to([NB, P]),
                               gates[:, :], start=True, stop=True)
            mm.then_inc(pe_step, 1)

        @block.scalar
        def _(act):
            act.wait_ge(step, 5)
            act.activation(dist[:, :], logit[:, :], ACT.Exp, bias=nmax[:, :], accum_out=total[:, 0:1]).then_inc(act_step, 1)
            act.wait_ge(step, 10)
            act.activation(ev[:, :], val[:, 0:N_ACT], ACT.Exp, bias=nmax[:, :], accum_out=total[:, 1:2]).then_inc(act_step, 1)
            act.activation(ez[:, :], nmax[:, :], ACT.Exp).then_inc(act_step, 1)

        @block.vector
        def _(dve):
            for b in range(NB):
                dve.tensor_reduce(hsum[:, b:b + 1], h[:, b * SEQ:(b + 1) * SEQ], AX.X, ALU.add).then_inc(step, 1)
            dve.wait_ge(pe_step, 1)
            dve.scalar_tensor_tensor(out=logit[:, :], in0=ps[0:NB, 0, 0:N_HEAD], scalar=1.0 / SEQ, in1=br[:, :],
                                     op0=ALU.mult, op1=ALU.add).then_inc(step, 1)
            dve.wait_ge(step, 3)
            dve.max(top[:, :], logit[:, :]).then_inc(step, 1)
            dve.wait_ge(step, 4)
            dve.tensor_scalar(nmax[:, :], top[:, 0:1], -1.0, None, ALU.mult).then_inc(step, 1)
            dve.wait_ge(act_step, 1)
            dve.reciprocal(total[:, 2:3], total[:, 0:1]).then_inc(step, 1)
            dve.wait_ge(step, 6)
            dve.tensor_scalar(dist[:, :], dist[:, :], total[:, 2:3], None, ALU.mult).then_inc(step, 1)
            dve.wait_ge(step, 7)
            dve.max(val[:, :], dist[:, :]).then_inc(step, 1)
            dve.wait_ge(step, 8)
            dve.max_index(idx[:, :], val[:, :], dist[:, :]).then_inc(step, 1)
            dve.tensor_scalar(nmax[:, :], val[:, 0:1], -1.0, None, ALU.mult).then_inc(step, 1)
            dve.wait_ge(act_step, 3)
            dve.scalar_tensor_tensor(out=ez[:, :], in0=ez[:, :], scalar=float(N_HEAD - N_ACT), in1=total[:, 1:2],
                                     op0=ALU.mult, op1=ALU.add).then_inc(step, 1)
            dve.wait_ge(step, 11)
            dve.reciprocal(total[:, 2:3], ez[:, :]).then_inc(step, 1)
            dve.wait_ge(step, 12)
            dve.tensor_scalar(gates[:, :], ev[:, :], total[:, 2:3], None, ALU.mult).then_inc(step, 1)
            dve.tensor_tensor(T["gate_bo"][:, :], T["mod"][:, 0, 5, :], bo[:, 0:1].broadcast_to([P, NB]), ALU.mult)\
               .then_inc(step, 1)
            dve.wait_ge(pe_step, 2)
            dve.tensor_copy(T["gates"][:, :, :].rearrange("p b k -> p (b k)"), ps[:, 1, 0:NB * N_ACT]).then_inc(step, 1)


def chosen_heads(nc, core, T, A):
    x, h, ps = T["xT"], T["hT"], T["ps"]
    with ExitStack() as st:
        def sb(name, shape, dt=F32):
            return core.sb(st, "a_" + name, shape, dt)

        def sem(name):
            return core.sem("a_" + name)

        w, bias, bv, wo = sb("w", [P, 3, DH]), sb("bias", [DH, 3]), sb("bv", [1, DH]), sb("wo", [DH, D])
        gq, gkb = sb("gq", [DH, 1]), sb("gkb", [DH, 1])
        qT, kT = sb("qT", [DH, SEQ]), sb("kT", [DH, SEQ])
        v = sb("v", [P, NT_B, DH + 1])
        prob = sb("prob", [P, 2, SEQ])
        probT = sb("probT", [P, 2, NT_B, P])
        nmax = sb("nmax", [P, 2])
        rsum = sb("rsum", [P, 2])
        o = sb("o", [P, NT_B, DH])
        oT = sb("oT", [DH, SEQ])
        w_loaded, wo_loaded, w_used, wo_used = sem("w_loaded"), sem("wo_loaded"), sem("w_used"), sem("wo_used")
        ones_set, small, q_proj, k_proj, v_proj = sem("ones_set"), sem("small"), sem("q_proj"), sem("k_proj"), sem("v_proj")
        q_ready, k_ready, v_ready, bo_added = sem("q"), sem("k"), sem("v"), sem("bo_added")
        scored, maxed, expd, turned = sem("scored"), sem("maxed"), sem("expd"), sem("turned")
        t_copied = [sem("t_dve"), sem("t_act")]
        weighed, inverted, normed = sem("weighed"), sem("inverted"), sem("normed")
        o_turned, o_copied, projected, x_added = sem("o_turned"), sem("o_copied"), sem("projected"), sem("x_added")
        block = st.enter_context(nc.Block())
        two = lambda ap: ap.rearrange("p (a t) -> p a t", a=2)


        @block.sync
        def _(sp):
            for b in range(NB):
                with sp.Fori(0, N_ACT) as i:
                    g = b * N_ACT + i
                    sp.wait_ge(v_proj, g + 1)
                    sp.wait_ge(q_ready, g + 1)
                    head = sp.value_load(T["head_index"][0:1, bass.ds(g, 1)], min_val=0, max_val=N_HEAD - 1)
                    sp.dma_start(w[:, :, :].rearrange("p j d -> p (j d)"), A["wqkv_h"][bass.ds(head, 1), :, :]
                                 .rearrange("o p n -> (o p) n")).then_inc(w_loaded, 16)
                    sp.dma_start(bias[:, :], A["bqkv_h"][bass.ds(head, 1), :, :].rearrange("o p n -> (o p) n"))\
                      .then_inc(w_loaded, 16)
                    sp.dma_start(bv[:, :], A["bv_h"][bass.ds(head, 1), :]).then_inc(w_loaded, 16)
                    sp.wait_ge(projected, g + 1)
                    sp.dma_start(wo[:, :], A["wo_k"][bass.ds(i, 1), :, :].rearrange("o p n -> (o p) n"))\
                      .then_inc(wo_loaded, 16)

        @block.gpsimd
        def _(pool):
            pool.memset(v[:, :, DH:DH + 1], 1.0).then_inc(ones_set, 1)

        @block.tensor
        def _(pe):
            pe.wait_ge(ones_set, 1)
            pe.sem_inc(v_proj, 1)
            pe.sem_inc(projected, 1)
            pe.sem_inc(turned, 4)
            pe.sem_inc(weighed, 2)
            for b in range(NB):
                with pe.Fori(0, N_ACT) as i:
                    g = b * N_ACT + i
                    pe.wait_ge(w_loaded, 48 * g + 48)
                    pe.wait_ge(expd, 8 * g + 2)
                    for j, ready in ((0, q_proj), (1, k_proj)):
                        for c in range(2):
                            mm = pe.matmul(ps[0:DH, 2 * j + c, :], w[:, j, :], h[:, chunk(2 * b + c)], start=True, stop=True)
                        mm.then_inc(ready, 1)
                    pe.wait_ge(o_copied, g + 1)
                    for t in range(NT_B):
                        pe.matmul(ps[:, 4, t * DH:(t + 1) * DH], h[:, b * SEQ + t * P:b * SEQ + (t + 1) * P], w[:, 2, :],
                                  start=True, stop=False)
                        mm = pe.matmul(ps[:, 4, t * DH:(t + 1) * DH], T["ones"][0:1, :], bv[:, :], start=False, stop=True)
                    mm.then_inc(v_proj, 1)
                    pe.wait_ge(q_ready, g + 2)
                    pe.wait_ge(k_ready, g + 2)

                    def scores(t):
                        pe.wait_ge(expd, 8 * g + t + 1)
                        for c in range(2):
                            mm = pe.matmul(ps[:, 2 * (t % 2) + c, :], qT[:, t * P:(t + 1) * P], kT[:, c * CH:(c + 1) * CH],
                                           start=True, stop=True)
                        mm.then_inc(scored, 1)

                    scores(0)
                    scores(1)
                    pe.wait_ge(v_ready, g + 1)
                    for t in range(NT_B):
                        pe.wait_ge(expd, 8 * g + t + 3)
                        for half in range(2):
                            pe.wait_ge(t_copied[half], 8 * g + t + 1)
                            for j in range(4):
                                mm = pe.transpose(ps[:, 4 + half, j * P:(j + 1) * P],
                                                  prob[:, t % 2, (4 * half + j) * P:(4 * half + j + 1) * P], T["ident"][:, :])
                            mm.then_inc(turned, 1)
                        if t + 2 < NT_B:
                            scores(t + 2)
                        pe.wait_ge(normed, 8 * g + t + 1)
                        if t == 0:
                            pe.wait_ge(x_added, 2 * g + 2)
                        for j in range(NT_B):
                            if j % 4 == 0:
                                pe.wait_ge(t_copied[j // 4], 8 * g + t + 2)
                            mm = pe.matmul(ps[:, 6 + t % 2, 0:DH + 1], probT[:, t % 2, j, :], v[:, j, :],
                                           start=(j == 0), stop=(j == NT_B - 1))
                        mm.then_inc(weighed, 1)
                    pe.wait_ge(normed, 8 * g + 10)
                    pe.matmul(ps[0:DH, 4, 0:P], o[:, 0, :], T["ident"][:, :], start=True, stop=True)
                    for t in range(1, NT_B):
                        mm = pe.transpose(ps[0:DH, 4 + t // 4, (t % 4) * P:(t % 4 + 1) * P], o[:, t, :], T["ident"][:, :])
                    mm.then_inc(o_turned, 1)
                    pe.wait_ge(o_copied, g + 2)
                    pe.wait_ge(wo_loaded, 16 * g + 16)
                    for c in range(2):
                        mm = pe.matmul(ps[:, 6 + c, :], wo[:, :], oT[:, c * CH:(c + 1) * CH], start=True, stop=True)
                    mm.then_inc(projected, 1)

        @block.scalar
        def _(act):
            act.sem_inc(expd, 2)
            act.sem_inc(t_copied[1], 1)
            act.sem_inc(k_ready, 1)
            for b in range(NB):
                with act.Fori(0, N_ACT) as i:
                    g = b * N_ACT + i
                    act.wait_ge(k_proj, g + 1)
                    act.wait_ge(small, 2 * g + 2)
                    act.activation(two(kT[:, :]), ps[0:DH, 2:4, :], ACT.Identity, bias=gkb[:, :],
                                   scale=T["gates"][0:DH, b, bass.ds(i, 1)]).then_inc(k_ready, 1)

                    def exps(t):
                        act.wait_ge(maxed, 8 * g + t + 1)
                        act.wait_ge(turned, 16 * g + 2 * t + 2)
                        act.activation(two(prob[:, t % 2, :]), ps[:, 2 * (t % 2):2 * (t % 2) + 2, :], ACT.Exp,
                                       bias=nmax[:, t % 2:t % 2 + 1]).then_inc(expd, 1)

                    exps(0)
                    exps(1)
                    for t in range(NT_B):
                        act.wait_ge(turned, 16 * g + 2 * t + 6)
                        act.wait_ge(weighed, 8 * g + t + 1)
                        act.activation(probT[:, t % 2, 4:8, :].rearrange("p j q -> p (j q)"), ps[:, 5, :], ACT.Copy)\
                           .then_inc(t_copied[1], 1)
                        if t + 2 < NT_B:
                            exps(t + 2)

        @block.vector
        def _(dve):
            dve.sem_inc(t_copied[0], 1)
            dve.sem_inc(q_ready, 1)
            dve.sem_inc(normed, 2)
            dve.sem_inc(o_copied, 1)
            dve.sem_inc(x_added, 2)
            for b in range(NB):
                xb = x[:, b * SEQ:(b + 1) * SEQ]
                dve.tensor_scalar(xb, xb, T["gate_bo"][:, b:b + 1], None, ALU.add).then_inc(bo_added, 1)
                with dve.Fori(0, N_ACT) as i:
                    g = b * N_ACT + i
                    gate = T["gates"][:, b, bass.ds(i, 1)]
                    dve.wait_ge(w_loaded, 48 * g + 48)
                    dve.wait_ge(k_ready, g + 1)
                    dve.tensor_scalar(gq[:, :], gate[0:DH, :], DH ** -0.5, None, ALU.mult).then_inc(small, 1)
                    dve.tensor_scalar(gkb[:, :], bias[:, 1:2], gate[0:DH, :], None, ALU.mult).then_inc(small, 1)
                    dve.wait_ge(small, 2 * g + 1)
                    dve.wait_ge(q_proj, g + 1)
                    dve.tensor_scalar(two(qT[:, :]), ps[0:DH, 0:2, :], bias[:, 0:1], gq[:, :], ALU.add, ALU.mult)\
                       .then_inc(q_ready, 1)
                    dve.wait_ge(v_proj, g + 2)
                    dve.tensor_scalar(v[:, :, 0:DH], ps[:, 4, :].rearrange("p (t d) -> p t d", d=DH), gate, None, ALU.mult)\
                       .then_inc(v_ready, 1)

                    def maxima(t):
                        dve.wait_ge(scored, 8 * g + t + 1)
                        dve.wait_ge(expd, 8 * g + t + 1)
                        dve.tensor_reduce(nmax[:, t % 2:t % 2 + 1], ps[:, 2 * (t % 2):2 * (t % 2) + 2, :], AX.XY, ALU.max,
                                          negate=True).then_inc(maxed, 1)

                    def normalise(t):
                        dve.wait_ge(weighed, 8 * g + t + 3)
                        dve.reciprocal(rsum[:, t % 2:t % 2 + 1], ps[:, 6 + t % 2, DH:DH + 1]).then_inc(inverted, 1)
                        dve.wait_ge(inverted, 8 * g + t + 1)
                        dve.tensor_scalar(o[:, t, :], ps[:, 6 + t % 2, 0:DH], rsum[:, t % 2:t % 2 + 1], None, ALU.mult)\
                           .then_inc(normed, 1)

                    maxima(0)
                    maxima(1)
                    for t in range(NT_B):
                        dve.wait_ge(turned, 16 * g + 2 * t + 5)
                        dve.wait_ge(weighed, 8 * g + t + 1)
                        dve.tensor_copy(probT[:, t % 2, 0:4, :].rearrange("p j q -> p (j q)"), ps[:, 4, :])\
                           .then_inc(t_copied[0], 1)
                        if t + 2 < NT_B:
                            maxima(t + 2)
                        if t:
                            normalise(t - 1)
                    normalise(NT_B - 1)
                    dve.wait_ge(o_turned, g + 1)
                    dve.tensor_copy(two(oT[:, :]), ps[0:DH, 4:6, :]).then_inc(o_copied, 1)
                    dve.wait_ge(projected, g + 2)
                    dve.wait_ge(bo_added, b + 1)
                    for c in range(2):
                        dve.wait_ge(x_added, 2 * g + 1 + c)
                        xc = x[:, chunk(2 * b + c)]
                        dve.scalar_tensor_tensor(out=xc, in0=ps[:, 6 + c, :], scalar=T["mod"][:, 0, 5, b:b + 1], in1=xc,
                                                 op0=ALU.mult, op1=ALU.add).then_inc(x_added, 1)


H1, HD = 16, 8
NG = NB * H1
WIN = 128
NREL = 2 * WIN + 1
NP3 = 3
STACK = NP3 * NP3 * HD
BIAS_ROWS = slice(STACK, STACK + NP3)
MAX_ROWS = slice(STACK + NP3, STACK + 2 * NP3)
KPOS, KALL = STACK + NP3, STACK + 2 * NP3
Q_, KL_, KR_ = range(3)
LEFT, RIGHT, ONES = range(3)
LOWEST = -3.0e38


def relative_parts(nc, core, T, A, dram, v, wstack):
    h, ps = T["hT"], T["ps"]
    with ExitStack() as st:
        def sb(name, shape, dt=F32):
            return core.sb(st, "p_" + name, shape, dt)

        def sem(name):
            return core.sem("p_" + name)

        w, cols = sb("w", [P, 3, D]), sb("cols", [P, 4])
        bv, table, brow = sb("bv", [1, D]), sb("table", [HD + 1, NREL]), sb("brow", [1, 2])
        edge = sb("edge", [HD + 1, 1])
        full, part = sb("full", [P, 3, TOK]), sb("part", [P, 3, NP3, TOK], BF16)
        scaled = sb("scaled", [P, TOK])
        tpart, bpart = sb("tpart", [HD + 1, NP3, NREL], BF16), sb("bpart", [1, NP3, 2], BF16)
        consts = sb("consts", [1, 3, NP3, SEQ], BF16)
        loaded, q_ready, k_ready, v_ready = sem("loaded"), sem("q"), sem("k"), sem("v")
        k_scaled, full_ready = sem("k_scaled"), sem("full")
        p1, r1, p2, r2, p3 = sem("p1"), sem("r1"), sem("p2"), sem("r2"), sem("p3")
        tstep, ones_set, v_copied, stored, wst = sem("tstep"), sem("ones_set"), sem("v_copied"), sem("stored"), sem("wst")
        block = st.enter_context(nc.Block())

        @block.sync
        def _(sp):
            sp.dma_start(w[:, :, :], A["wqkv1"]).then_inc(loaded, 16)
            sp.dma_start(cols[:, :], A["cols1"]).then_inc(loaded, 16)
            sp.dma_start(bv[:, :], A["bv1"]).then_inc(loaded, 16)
            sp.dma_start(table[:, :], A["table"]).then_inc(loaded, 16)
            sp.dma_start(brow[:, :], A["brow"]).then_inc(loaded, 16)
            sp.dma_start(edge[:, :], A["table_edge"]).then_inc(loaded, 16)
            sp.wait_ge(tstep, 12)
            sp.wait_ge(ones_set, 1)
            sp.dma_start(dram["table"].rearrange("k r n -> r k n"), tpart[:, :, :]).then_inc(wst, 16)
            sp.dma_start(dram["const"].rearrange("c k t -> (c k t)"), consts[:, :, :, :].rearrange("o c k t -> o (c k t)"))\
              .then_inc(stored, 16)
            sp.wait_ge(wst, 16)
            for k in range(NP3):
                sp.dma_start(wstack[k * NP3 * HD:(k + 1) * NP3 * HD, :], dram["table"][:, 0:HD, :]).then_inc(stored, 16)
            sp.dma_start(wstack[BIAS_ROWS, :], dram["table"][:, HD:HD + 1, :]).then_inc(stored, 16)
            for a in range(3):
                for k, ready in enumerate((p1, p2, p3)):
                    sp.wait_ge(ready, a + 1)
                    sp.dma_start(dram["qk"][a, k].rearrange("b r t -> r b t"),
                                 part[:, a, k, :].rearrange("r (b t) -> r b t", b=NB)).then_inc(stored, 16)
            sp.wait_ge(stored, 16 * 14)

        @block.gpsimd
        def _(pool):
            pool.memset(consts[:, ONES, :, :], 1.0).then_inc(ones_set, 1)
            for a in range(3):
                pool.wait_ge(p1, a + 1)
                pool.tensor_tensor(full[:, a, :], full[:, a, :], part[:, a, 0, :], ALU.subtract).then_inc(r1, 1)

        @block.tensor
        def _(pe):
            pe.wait_ge(loaded, 96)
            for j, ready in ((0, q_ready), (1, k_ready)):
                for c in range(NCH):
                    mm = pe.matmul(ps[:, 4 * j + c, :], w[:, j, :], h[:, chunk(c)], start=True, stop=True)
                mm.then_inc(ready, 1)
            pe.wait_ge(full_ready, 1)
            for t in range(TOK // P):
                at = ps[:, t // 4, (t % 4) * P:(t % 4 + 1) * P]
                pe.matmul(at, h[:, t * P:(t + 1) * P], w[:, 2, :], start=True, stop=False)
                mm = pe.matmul(at, T["ones"][0:1, :], bv[:, :], start=False, stop=True)
            mm.then_inc(v_ready, 1)

        @block.scalar
        def _(act):
            for a in range(3):
                act.wait_ge(full_ready, a + 1)
                act.activation(part[:, a, 0, :], full[:, a, :], ACT.Copy).then_inc(p1, 1)
            for a in range(3):
                act.wait_ge(r1, a + 1)
                act.activation(part[:, a, 1, :], full[:, a, :], ACT.Copy).then_inc(p2, 1)
            for a in range(3):
                act.wait_ge(r2, a + 1)
                act.activation(part[:, a, 2, :], full[:, a, :], ACT.Copy).then_inc(p3, 1)

        @block.vector
        def _(dve):
            banks = lambda ap: ap.rearrange("p (c t) -> p c t", t=CH)
            dve.wait_ge(q_ready, 1)
            dve.tensor_scalar(banks(full[:, Q_, :]), ps[:, 0:4, :], cols[:, 0:1], None, ALU.add).then_inc(full_ready, 1)
            dve.wait_ge(k_ready, 1)
            dve.tensor_scalar(banks(scaled[:, :]), ps[:, 4:8, :], cols[:, 1:2], HD ** -0.5, ALU.add, ALU.mult)\
               .then_inc(k_scaled, 1)
            dve.wait_ge(k_scaled, 1)
            dve.tensor_scalar(full[:, KL_, :], scaled[:, :], cols[:, 2:3], None, ALU.add).then_inc(full_ready, 1)
            dve.tensor_scalar(full[:, KR_, :], scaled[:, :], cols[:, 3:4], None, ALU.add).then_inc(full_ready, 1)
            dve.tensor_scalar(table[:, :], table[:, :], edge[:, :], None, ALU.subtract).then_inc(tstep, 1)
            n = 1
            for src, parts in ((table, lambda k: tpart[:, k, :]), (brow, lambda k: bpart[:, k, :])):
                for k in range(NP3):
                    dve.wait_ge(tstep, n)
                    dve.tensor_copy(parts(k), src[:, :]).then_inc(tstep, 1)
                    n += 1
                    if k < NP3 - 1:
                        dve.wait_ge(tstep, n)
                        dve.tensor_tensor(src[:, :], src[:, :], parts(k), ALU.subtract).then_inc(tstep, 1)
                        n += 1
            dve.wait_ge(tstep, n)
            for c in range(2):
                ins = dve.tensor_copy(consts[:, c, :, :], bpart[:, :, c:c + 1].broadcast_to([1, NP3, SEQ]))
            ins.then_inc(tstep, 1)
            for a in range(3):
                dve.wait_ge(p2, a + 1)
                dve.tensor_tensor(full[:, a, :], full[:, a, :], part[:, a, 1, :], ALU.subtract).then_inc(r2, 1)
            dve.wait_ge(v_ready, 1)
            dve.wait_ge(ones_set, 1)
            for c in range(NCH):
                b, o = divmod(c, 2)
                dve.tensor_copy(v[:, 4 * o:4 * o + 4, b * H1:(b + 1) * H1, :],
                                ps[:, c, :].rearrange("p (t g d) -> p t g d", t=4, d=HD)).then_inc(v_copied, 1)


def relative_attention(nc, core, T, A, dram, v, wstack, oacc):
    ps = T["ps"]
    with ExitStack() as st:
        def sb(name, shape, dt=F32):
            return core.sb(st, "l_" + name, shape, dt)

        def sem(name):
            return core.sem("l_" + name)

        TURN_AT = 5
        NSL = 4
        stack = [sb(n, [KALL, NSL, SEQ], BF16) for n in ("qs", "kl", "kr")]
        qb = sb("qb", [KPOS, 2, SEQ], BF16)
        rel = sb("rel", [P, 2, NT_B, NREL])
        band = sb("band", [P, NSL, NT_B, 3 * P])
        probT = sb("probT", [P, 2, SEQ])
        seen = sb("seen", [P, 3, NT_B])
        nmax, nparts, nrow = sb("nmax", [P, NT_B]), sb("nparts", [P, NP3 * NT_B], BF16), sb("nrow", [NP3 * NT_B, P], BF16)
        junk, inv = sb("junk", [P, 3 * P]), sb("inv", [P, NT_B])
        VAT, VW = 32, 64
        vhead = sb("vhead", [P, 2, NT_B, VAT + VW])
        outT = sb("outT", [P, CH])
        inside = sb("inside", [P, P])
        inside_set = sem("inside")
        rows_set, lowest_set = sem("rows_set"), sem("lowest")
        stack_loaded = [sem(f"stack{s}") for s in range(NSL)]
        qb_loaded, band_loaded = [sem(f"qb{s}") for s in range(2)], [sem(f"band{s}") for s in range(2)]
        rel_ready, rel_copied, rel_stored, band_step, band_ready = (sem(x) for x in ("rel", "relc", "rels", "bstep", "bready"))
        s1_ready, maxed, dstep = sem("s1"), sem("maxed"), sem("dstep")
        n_turned, n_copied, n_loaded = sem("n_turned"), sem("n_copied"), sem("n_loaded")
        s2_ready, expd, weighed = sem("s2"), sem("expd"), sem("weighed")
        inverted, normed = sem("inverted"), sem("normed")
        v_placed, out_copied, o_turned = sem("v_placed"), sem("out_copied"), sem("o_turned")
        block = st.enter_context(nc.Block())

        def stages(eng, body):
            with eng.Fori(0, NG // 4 - 1) as i:
                for q in range(4):
                    body(4 * i + q, q, lambda k: True, lambda k, n: n * i + k // (4 // n))
            for q in range(4):
                g = NG - 4 + q
                body(g, q, lambda k: g + k < NG, lambda k, n: n * (NG // 4 - 1) + k // (4 // n))

        @block.sync
        def _(sp):
            for a in range(3):
                const = dram["const"][(ONES, LEFT, RIGHT)[a]]
                sp.dma_start(stack[a][BIAS_ROWS, :, :], const.unsqueeze(1).broadcast_to([NP3, NSL, SEQ])).then_inc(rows_set, 16)
                if a != Q_:
                    sp.dma_start(stack[a][MAX_ROWS, :, :], dram["const"][ONES].unsqueeze(1).broadcast_to([NP3, NSL, SEQ]))\
                      .then_inc(rows_set, 16)
            sp.dma_start(qb[BIAS_ROWS, :, :], dram["const"][ONES].unsqueeze(1).broadcast_to([NP3, 2, SEQ])).then_inc(rows_set, 16)

            def at(g):
                return g * HD if isinstance(g, int) else sp.snap(g * HD)

            def rows(a, first, k):
                own = slice(k, k + 1) if a == Q_ else slice(0, NP3)
                return dram["rows"][a][own, bass.ds(first, HD), :].broadcast_to([NP3, HD, SEQ])

            def load_rows(dst, s, a, first, sem):
                for k in range(NP3):
                    sp.dma_start(dst[k * NP3 * HD:(k + 1) * NP3 * HD, s, :], rows(a, first, k)).then_inc(sem, 16)

            def load_qb(first, s):
                load_rows(qb, s, Q_, first, qb_loaded[s])

            def load_stack(first, s):
                for a in range(3):
                    load_rows(stack[a], s, a, first, stack_loaded[s])

            def shift(g, s2, s4, reads_before):
                sp.wait_ge(rel_copied, NT_B * g + NT_B + 1)
                if reads_before is not None:
                    sp.wait_ge(band_loaded[s2], reads_before)
                sp.dma_start(dram["rel"][s2].rearrange("t (p r) -> p t r", p=P), rel[:, s2, :, :]).then_inc(rel_stored, 16)
                sp.wait_ge(rel_stored, 16 * g + 16)
                flat = dram["rel"][s2]
                sp.dma_start(band[:, s4, :, 0:2 * P], flat[:, 0:P * 2 * P].rearrange("t (p c) -> p t c", p=P))\
                  .then_inc(band_loaded[s2], 16)
                sp.dma_start(band[:, s4, :, 2 * P:3 * P], flat[:, P:P + P * 2 * P].rearrange("t (p c) -> p t c", p=P)[:, :, P:2 * P])\
                  .then_inc(band_loaded[s2], 16)

            def load_max(g, s4):
                sp.wait_ge(n_copied, g + 1)
                sp.dma_start(stack[Q_][MAX_ROWS, s4, :], nrow[:, :]).then_inc(n_loaded, 16)

            load_qb(at(0), 0)
            load_qb(at(1), 1)
            for g in range(3):
                load_stack(at(g), g)
            for g in range(2):
                sp.wait_ge(rel_ready, NT_B * (g + 1))
                load_qb(at(g + 2), g)
            for g in range(2):
                shift(g, g, g, None)
            load_max(0, 0)

            def body(g, q, live, per):
                if live(3):
                    first = at(g + 3)
                    sp.wait_ge(s2_ready, NT_B * g + 4 * NT_B)
                    load_stack(first, (q + 3) % NSL)
                if live(4):
                    first = at(g + 4)
                    sp.wait_ge(rel_ready, NT_B * (g + 3))
                    load_qb(first, q % 2)
                if live(2):
                    shift(g + 2, q % 2, (q + 2) % NSL, 32 * per(q + 2, 2))
                if live(1):
                    load_max(g + 1, (q + 1) % NSL)

            stages(sp, body)

        @block.gpsimd
        def _(pool):
            for kind, tiles in ((1, slice(0, 2)), (2, slice(NT_B - 2, NT_B))):
                pool.memset(seen[:, kind, tiles], LOWEST).then_inc(lowest_set, 1)
            pool.memset(inside[:, :], 1.0).then_inc(inside_set, 1)
            pool.wait_ge(inside_set, 1)
            pool.affine_select(out=inside[:, :], in_=inside[:, :], compare_op=ALU.is_ge, fill=0.0, base=0,
                               pattern=[[-1, P]], channel_multiplier=1).then_inc(inside_set, 1)
            pool.wait_ge(inside_set, 2)
            pool.sem_inc(band_ready, 2)
            pool.memset(vhead[:, :, :, :], 0.0).then_inc(inside_set, 1)
            pool.wait_ge(inside_set, 3)
            pool.memset(outT[:, :], 0.0).then_inc(inside_set, 1)
            pool.wait_ge(inside_set, 4)
            pool.memset(vhead[:, :, :, VAT + HD:VAT + HD + 1], 1.0).then_inc(inside_set, 1)
            pool.wait_ge(inside_set, 5)

            def place_v(g, s2):
                if not isinstance(g, int) or g:
                    pool.wait_ge(weighed, NT_B * g - NT_B + 2)
                pool.tensor_copy(vhead[:, s2, :, VAT:VAT + HD].unsqueeze(2), v[:, :, bass.ds(g, 1), :]).then_inc(v_placed, 1)

            def trim(g, s2, s4, reads):
                last, first = band[:, s4, :, 2 * P:3 * P], band[:, s4, :, 0:P]
                pool.wait_ge(band_loaded[s2], reads)
                pool.tensor_tensor(last, last, rel[:, s2, :, NREL - 1:NREL].broadcast_to([P, NT_B, P]), ALU.subtract)\
                    .then_inc(band_step, 1)
                pool.affine_select(out=first, in_=first, compare_op=ALU.is_ge, fill=0.0, base=0,
                                   pattern=[[0, NT_B], [1, P]], channel_multiplier=-1).then_inc(band_step, 1)
                pool.wait_ge(band_step, 2 * g + 1)
                pool.tensor_tensor(last, last, inside[:, :].unsqueeze(1).broadcast_to([P, NT_B, P]), ALU.mult)\
                    .then_inc(band_ready, 1)

            place_v(0, 0)
            for g in range(2):
                trim(g, g, g, 32)

            def body(g, q, live, per):
                if live(1):
                    place_v(g + 1, (q + 1) % 2)
                if live(2):
                    trim(g + 2, q % 2, (q + 2) % NSL, 32 * per(q + 2, 2) + 32)

            stages(pool, body)

        @block.tensor
        def _(pe):
            ident = T["ident"]

            def relative(g, k, s2, loads):
                if k == 0:
                    pe.wait_ge(qb_loaded[s2], loads)
                if k == TURN_AT and not (isinstance(g, int) and g < 3):
                    pe.wait_ge(n_copied, g - 1)
                pe.wait_ge(rel_copied, NT_B * g + k + 1)
                pe.matmul(ps[:, 7, 0:NREL], qb[0:KPOS, s2, k * P:(k + 1) * P], wstack[0:KPOS, :], start=True, stop=True)\
                  .then_inc(rel_ready, 1)

            def first_scores(g, t, s4, loads):
                if t == 0:
                    pe.wait_ge(stack_loaded[s4], loads)
                pe.wait_ge(maxed, NT_B * g + t + 1)
                edge = (t + 1) * P
                for c in range(2):
                    lo, hi = c * CH, (c + 1) * CH
                    cut = min(max(edge, lo), hi)
                    first = True
                    for a, x0, x1 in ((KL_, lo, cut), (KR_, cut, hi)):
                        if x1 > x0:
                            mm = pe.matmul(ps[:, c, x0 - lo:x1 - lo], stack[Q_][0:KPOS, s4, t * P:(t + 1) * P],
                                           stack[a][0:KPOS, s4, x0:x1], start=first, stop=False, skip_group_check=True)
                            first = False
                mm.then_inc(s1_ready, 1)

            def turn_max(g):
                pe.wait_ge(dstep, 6 * g + 6)
                pe.wait_ge(rel_copied, NT_B * (g + 2) + TURN_AT + 1 if not isinstance(g, int) or 0 < g < NG - 2
                           else NT_B * min(g + 3, NG) + 1)
                pe.transpose(ps[0:NP3 * NT_B, 7, 0:P // 2].bitcast(BF16), nparts[:, :], T["ident_bf"][:, :])\
                  .then_inc(n_turned, 1)

            def second_scores(g, t, s4):
                if t == 0:
                    pe.wait_ge(n_loaded, 16 * g + 16)
                pe.wait_ge(expd, NT_B * g + t + 1)
                bank = 2 + 2 * (t % 2)
                for c in range(2):
                    lo, hi = c * CH, (c + 1) * CH
                    cut = min(max(t * P, lo), hi)
                    first = True
                    for a, x0, x1 in ((KR_, lo, cut), (KL_, cut, hi)):
                        if x1 > x0:
                            pe.matmul(ps[:, bank + c, x0 - lo:x1 - lo], stack[a][0:KALL, s4, t * P:(t + 1) * P],
                                      stack[Q_][0:KALL, s4, x0:x1], start=first, stop=False, skip_group_check=True)
                            first = False
                for i in range(max(t - 1, 0), min(t + 2, NT_B)):
                    blk = t - i + 1
                    mm = pe.matmul(ps[:, bank + i // 4, (i % 4) * P:(i % 4 + 1) * P], band[:, s4, i, blk * P:(blk + 1) * P],
                                   ident[:, :], start=False, stop=False, skip_group_check=True)
                mm.then_inc(s2_ready, 1)

            def weigh(g, t, s2):
                pe.wait_ge(expd, NT_B * g + t + 3)
                if t == 0:
                    pe.wait_ge(v_placed, g + 1)
                    pe.wait_ge(normed, g + 1)
                for c in range(2):
                    at = VAT - c * VAT
                    mm = pe.matmul(ps[0:VW, 6, :], vhead[:, s2, t, at:at + VW], probT[:, t % 2, c * CH:(c + 1) * CH],
                                   start=(t == 0 and c == 0), stop=False, skip_group_check=True)
                mm.then_inc(weighed, 1)

            def turn_out(g):
                pe.wait_ge(out_copied, g + 1)
                for j in range(CH // P):
                    mm = pe.transpose(ps[:, 6, j * P:(j + 1) * P], outT[:, j * P:(j + 1) * P], ident[:, :])
                mm.then_inc(o_turned, 1)

            pe.wait_ge(rows_set, 96)
            pe.sem_inc(weighed, 2)
            pe.sem_inc(s2_ready, 4 * NT_B)
            for g in range(3):
                for k in range(NT_B):
                    relative(g, k, g % 2, 16 * NP3 * (g // 2 + 1))
            for t in range(NT_B):
                first_scores(0, t, 0, 9 * 16)
            turn_max(0)
            pe.wait_ge(n_copied, 1)
            second_scores(0, 0, 0)

            def body(g, q, live, per):
                s4n = (q + 1) % NSL
                for t in range(NT_B):
                    if t < NT_B - 1:
                        second_scores(g, t + 1, q)
                    if live(1) and t < NT_B // 2:
                        first_scores(g + 1, 2 * t, s4n, 9 * 16 * (per(q + 1, 1) + 1))
                    weigh(g, t, q % 2)
                    if live(1) and t < NT_B // 2:
                        first_scores(g + 1, 2 * t + 1, s4n, 9 * 16 * (per(q + 1, 1) + 1))
                    if live(1) and t == TURN_AT:
                        turn_max(g + 1)
                    if live(3):
                        relative(g + 3, t, (q + 3) % 2, 16 * NP3 * (per(q + 3, 2) + 1))
                if live(1):
                    second_scores(g + 1, 0, s4n)
                turn_out(g)

            stages(pe, body)

        @block.scalar
        def _(act):
            act.sem_inc(rel_copied, 1)
            act.sem_inc(expd, 2)

            def copy_rel(g, k, s2):
                act.wait_ge(rel_ready, NT_B * g + k + 1)
                if k == 0:
                    act.wait_ge(band_ready, g + 1)
                act.activation(rel[:, s2, k, :], ps[:, 7, 0:NREL], ACT.Copy).then_inc(rel_copied, 1)

            def copy_max(g):
                act.wait_ge(n_turned, g + 1)
                if not (isinstance(g, int) and g == 0):
                    act.wait_ge(n_loaded, 16 * g)
                act.activation(nrow[:, :], ps[0:NP3 * NT_B, 7, 0:P // 2].bitcast(BF16), ACT.Copy).then_inc(n_copied, 1)

            for g in range(3):
                for k in range(NT_B):
                    copy_rel(g, k, g % 2)
            copy_max(0)

            def exponentials(g, t):
                act.wait_ge(s2_ready, NT_B * (g + 4) + t + 1)
                act.wait_ge(weighed, NT_B * g + t + 1)
                bank = 2 + 2 * (t % 2)
                act.activation(probT[:, t % 2, :].rearrange("p (c t) -> p c t", t=CH), ps[:, bank:bank + 2, :], ACT.Exp)\
                   .then_inc(expd, 1)

            exponentials(0, 0)

            def body(g, q, live, per):
                for t in range(NT_B):
                    if t < NT_B - 1:
                        exponentials(g, t + 1)
                    if live(1) and t == TURN_AT:
                        copy_max(g + 1)
                    if live(3):
                        copy_rel(g + 3, t, (q + 3) % 2)
                act.wait_ge(weighed, NT_B * g + NT_B + 2)
                act.activation(outT[0:VW, :], ps[0:VW, 6, :], ACT.Copy).then_inc(out_copied, 1)
                if live(1):
                    exponentials(g + 1, 0)

            stages(act, body)

        @block.vector
        def _(dve):
            dve.wait_ge(lowest_set, 2)
            dve.sem_inc(maxed, 1)
            dve.sem_inc(normed, 1)

            def maxima(g, t, s4):
                if t == 0:
                    dve.wait_ge(band_ready, g + 3)
                dve.wait_ge(s1_ready, NT_B * g + t + 1)
                s1 = ps[:, 0:2, :].rearrange("p c t -> p (c t)")
                lo, hi = max(t - 1, 0) * P, min(t + 2, NT_B) * P
                if lo:
                    dve.tensor_reduce(seen[:, 1, t:t + 1], s1[:, 0:lo], AX.X, ALU.max)
                if hi < SEQ:
                    dve.tensor_reduce(seen[:, 2, t:t + 1], s1[:, hi:SEQ], AX.X, ALU.max)
                off = lo - (t - 1) * P
                dve.tensor_tensor_reduce(junk[:, 0:hi - lo], s1[:, lo:hi], band[:, s4, t, off:off + hi - lo], 1.0, LOWEST,
                                         ALU.add, ALU.max, seen[:, 0, t:t + 1]).then_inc(maxed, 1)

            def split_max(g):
                n = 6 * g
                dve.wait_ge(maxed, NT_B * g + NT_B + 1)
                if not (isinstance(g, int) and g == 0):
                    dve.wait_ge(n_turned, g)
                dve.tensor_reduce(nmax[:, :], seen[:, :, :].rearrange("p k t -> p t k"), AX.X, ALU.max, negate=True)\
                   .then_inc(dstep, 1)
                for k in range(NP3):
                    p = nparts[:, k * NT_B:(k + 1) * NT_B]
                    dve.wait_ge(dstep, n + 2 * k + 1)
                    dve.tensor_copy(p, nmax[:, :]).then_inc(dstep, 1)
                    if k < NP3 - 1:
                        dve.wait_ge(dstep, n + 2 * k + 2)
                        dve.tensor_tensor(nmax[:, :], nmax[:, :], p, ALU.subtract).then_inc(dstep, 1)

            def normalise(g):
                sums = ps[:, 6, :].rearrange("p (j c x) -> p c j x", j=CH // P, x=VAT)[:, 0:2, :, :]
                dve.wait_ge(o_turned, g + 1)
                dve.reciprocal(inv[:, :].rearrange("p (c j) -> p c j", c=2).unsqueeze(3), sums[:, :, :, HD:HD + 1]).then_inc(inverted, 1)
                dve.wait_ge(inverted, g + 1)
                for c in range(2):
                    half = slice(c * (CH // P), (c + 1) * (CH // P))
                    ins = dve.tensor_tensor(oacc[:, half, bass.ds(g, 1), :].rearrange("p t o d -> p t (o d)"),
                                            sums[:, c, :, 0:HD], inv[:, half].unsqueeze(2).broadcast_to([P, CH // P, HD]), ALU.mult)
                ins.then_inc(normed, 1)

            for t in range(NT_B):
                maxima(0, t, 0)
            split_max(0)

            def body(g, q, live, per):
                if live(1):
                    for t in range(NT_B):
                        maxima(g + 1, t, (q + 1) % NSL)
                    split_max(g + 1)
                normalise(g)

            stages(dve, body)


def add_heads(nc, core, T, oacc):
    x, ps = T["xT"], T["ps"]
    with ExitStack() as st:
        turned, added = core.sem("h_turned"), core.sem("h_added")
        block = st.enter_context(nc.Block())

        @block.tensor
        def _(pe):
            for c in range(NCH):
                b, o = divmod(c, 2)
                for j in range(4):
                    mm = pe.transpose(ps[:, c, j * P:(j + 1) * P],
                                      oacc[:, 4 * o + j, b * H1:(b + 1) * H1, :].rearrange("p g d -> p (g d)"), T["ident"][:, :])
                mm.then_inc(turned, 1)

        @block.vector
        def _(dve):
            for c in range(NCH):
                b = c * CH // SEQ
                dve.wait_ge(turned, c + 1)
                dve.scalar_tensor_tensor(out=x[:, chunk(c)], in0=ps[:, c, :], scalar=T["mod"][:, 1, 2, b:b + 1],
                                         in1=x[:, chunk(c)], op0=ALU.mult, op1=ALU.add).then_inc(added, 1)


def second_attention(nc, core, T, A, dram):
    with ExitStack() as st:
        v = core.sb(st, "v1", [P, NT_B, NG, HD])
        wstack = core.sb(st, "wstack", [KPOS, NREL], BF16)
        oacc = core.sb(st, "oacc", [P, NT_B, NG, HD])
        relative_parts(nc, core, T, A, dram, v, wstack)
        relative_attention(nc, core, T, A, dram, v, wstack, oacc)
        add_heads(nc, core, T, oacc)


NE, HID = 8, 512
HF = HID // P
NT = TOK // P
ST = NT + NE - 1
BIASES = 2 * HID + D


def experts(nc, core, T, A, dram, out):
    x, h, ps = T["xT"], T["hT"], T["ps"]
    with ExitStack() as st:
        def sb(name, shape, dt=F32):
            return core.sb(st, "e_" + name, shape, dt)

        def sem(name):
            return core.sem("e_" + name)

        w1, w2 = sb("w1", [P, NE, 2 * HID]), sb("w2", [P, NE, HF, D])
        bias, bpart = sb("bias", [NE, BIASES]), sb("bpart", [NE, NP3, BIASES], BF16)
        brows = sb("brows", [NP3, NE, BIASES], BF16)
        rw, rb = sb("rw", [P, NE]), sb("rb", [1, NE])
        logit, top, mask = sb("logit", [P, NT, NE]), sb("top", [P, NT]), sb("mask", [P, NT, NE])
        count = sb("count", [P, ST])
        before = sb("before", [P, P])
        rank = sb("rank", [P, NT + 1, NE])
        full, tiles, ends = sb("full", [P, NE, NT]), sb("tiles", [P, NE]), sb("ends", [P, NE])
        slot, index = sb("slot", [P, NT]), sb("index", [P, NT], U32)
        passed, owner = sb("passed", [1, ST, NE]), sb("owner", [1, ST])
        expert_of = sb("expert_of", [1, ST + 1], U32)
        ht, zero = sb("ht", [P, NT, D]), sb("zero", [P, D])
        hrow, hx = sb("hrow", [P, 2, D]), sb("hx", [P, 2, P])
        sig, hid, hidT = sb("sig", [P, 2, HID]), sb("hid", [P, 2, HID]), sb("hidT", [P, 2, HF, P])
        y, yt = sb("y", [P, ST, D]), sb("yt", [P, NT, D])
        loaded, w_loaded, b_loaded, b_split, b_moved = (sem(n) for n in ("loaded", "w", "b", "bsplit", "bmoved"))
        constants, routed, step, ranked, h_turned, ht_ready = (sem(n) for n in ("const", "routed", "step", "ranked", "hturned", "ht"))
        cleared, scattered, row_loaded = sem("cleared"), sem("scattered"), [sem("row0"), sem("row1")]
        t_ready, hx_ready, g_ready, a_ready, sig_ready = (sem(n) for n in ("t", "hx", "g", "a", "sig"))
        hid_ready, hidT_turned, hidT_ready, y_ready, y_copied = (sem(n) for n in ("hid", "hidTt", "hidT", "y", "ycopied"))
        y_stored, gathered = sem("y_stored"), [sem(f"gathered{c}") for c in range(NCH)]
        turned, x_ready, stored = sem("turned"), sem("x"), sem("stored")
        block = st.enter_context(nc.Block())

        def slot_tiles(eng, body):
            with eng.Fori(0, (ST - 3) // 2) as i:
                for u in range(2):
                    body(2 * i + u, u, i, lambda k: True)
            for j in range(ST - 3, ST):
                body(j, j % 2, j // 2, lambda k: j + k < ST)

        @block.sync
        def _(sp):
            sp.dma_start(rw[:, :], A["router_w"]).then_inc(loaded, 16)
            sp.dma_start(rb[:, :], A["router_b"]).then_inc(loaded, 16)
            sp.dma_start(bias[:, :], A["biases"]).then_inc(b_loaded, 16)
            sp.wait_ge(constants, 2)
            sp.dma_start(dram["h_sorted"].rearrange("(t p) d -> p t d", p=P), zero[:, :].unsqueeze(1).broadcast_to([P, ST, D]))\
              .then_inc(cleared, 16)
            for e in range(NE):
                sp.dma_start(w1[:, e, :], A["w1"][e]).then_inc(w_loaded, 16)
                sp.dma_start(w2[:, e, :, :], A["w2"][e].rearrange("(k p) d -> p k d", p=P)).then_inc(w_loaded, 16)
            sp.wait_ge(b_split, 2 * NP3 - 1)
            for k in range(NP3):
                sp.dma_start(brows[k:k + 1, :, :], bpart[:, k, :]).then_inc(b_moved, 16)
            sp.wait_ge(scattered, 16 * NT)

            def load(j, s, i, live):
                sp.wait_ge(t_ready, j + 1)
                sp.dma_start(hrow[:, s, :], dram["h_sorted"][bass.ds(j * P, P), :]).then_inc(row_loaded[s], 16)

            slot_tiles(sp, load)
            for c in range(NCH):
                sp.wait_ge(x_ready, c + 1)
                sp.dma_start(out[:, chunk(c)], x[:, chunk(c)]).then_inc(stored, 16)
            sp.wait_ge(stored, 16 * NCH)

        @block.gpsimd
        def _(pool):
            pool.memset(before[:, :], 1.0).then_inc(constants, 1)
            pool.wait_ge(constants, 1)
            pool.memset(zero[:, :], 0.0).then_inc(constants, 1)
            pool.wait_ge(constants, 2)
            pool.affine_select(out=before[:, :], in_=before[:, :], compare_op=ALU.is_ge, fill=0.0, base=-1,
                               pattern=[[1, P]], channel_multiplier=-1).then_inc(constants, 1)
            for k in range(ST):
                pool.wait_ge(constants, 3 + k)
                pool.memset(count[:, k:k + 1], float(k)).then_inc(constants, 1)
            pool.wait_ge(cleared, 16)
            pool.wait_ge(step, 15)
            for t in range(NT):
                if t % 4 == 0:
                    pool.wait_ge(ht_ready, t // 4 + 1)
                pool.indirect_dma_start(out=dram["h_sorted"], out_offset=bass.IndirectOffsetOnAxis(ap=index[:, t:t + 1], axis=0),
                                        in_=ht[:, t, :], in_offset=None).then_inc(scattered, 16)
            part = 6
            for first in range(0, ST, part):
                last = min(first + part, ST)
                pool.wait_ge(y_copied, last + 1)
                pool.dma_start(dram["y_sorted"][first * P:last * P, :].rearrange("(t p) d -> p t d", p=P), y[:, first:last, :])\
                    .then_inc(y_stored, 16)
            pool.wait_ge(y_stored, 16 * -(-ST // part))
            for t in range(NT):
                pool.indirect_dma_start(out=yt[:, t, :], out_offset=None, in_=dram["y_sorted"],
                                        in_offset=bass.IndirectOffsetOnAxis(ap=index[:, t:t + 1], axis=0))\
                    .then_inc(gathered[t // 4], 16)

        @block.tensor
        def _(pe):
            ident = T["ident"]
            pe.wait_ge(loaded, 32)
            for t in range(NT):
                pe.matmul(ps[:, 0, t * NE:(t + 1) * NE], h[:, t * P:(t + 1) * P], rw[:, :], start=True, stop=False)
                mm = pe.matmul(ps[:, 0, t * NE:(t + 1) * NE], T["ones"][0:1, :], rb[:, :], start=False, stop=True)
            mm.then_inc(routed, 1)
            for c in range(NCH):
                for j in range(4):
                    t = 4 * c + j
                    mm = pe.transpose(ps[:, 4 + c, j * P:(j + 1) * P], h[:, t * P:(t + 1) * P], ident[:, :])
                mm.then_inc(h_turned, 1)
            pe.wait_ge(constants, 3)
            pe.wait_ge(step, 6)
            pe.matmul(ps[:, 1, 0:NT * NE], before[:, :], mask[:, :, :].rearrange("p t e -> p (t e)"), start=True, stop=False,
                      skip_group_check=True)
            for t in range(NT):
                mm = pe.matmul(ps[:, 1, (t + 1) * NE:(NT + 1) * NE].rearrange("p (t e) -> p t e", e=NE), T["ones"][:, :],
                               mask[:, t:t + 1, :].broadcast_to([P, NT - t, NE]), start=False, stop=False, skip_group_check=True)
            mm.then_inc(ranked, 1)
            pe.sem_inc(t_ready, 2)
            pe.wait_ge(step, 18)
            pe.wait_ge(w_loaded, 32 * NE)
            pe.wait_ge(b_moved, 16 * NP3)

            def turn(s, turns):
                pe.wait_ge(row_loaded[s], 16 * turns)
                pe.transpose(ps[:, 6, 0:P], hrow[:, s, :], ident[:, :]).then_inc(t_ready, 1)

            def expert(j):
                return pe.value_load(expert_of[0:1, bass.ds(j, 1)], min_val=0, max_val=NE - 1)

            def hidden(half, s, e, ready):
                cols = slice(half * HID, (half + 1) * HID)
                bank = ps[:, 2 * half + s, :]
                pe.matmul(bank, hx[:, s, :], w1[:, bass.ds(e, 1), cols].rearrange("p o n -> p (o n)"), start=True, stop=False)
                pe.matmul(bank, T["ones_bf"][0:NP3, :], brows[:, bass.ds(e, 1), cols].rearrange("p o n -> p (o n)"),
                          start=False, stop=True).then_inc(ready, 1)

            turn(0, 1)
            pe.wait_ge(hx_ready, 1)
            turn(1, 1)
            e = expert(0)
            hidden(1, 0, e, g_ready)
            hidden(0, 0, e, a_ready)

            def tile(j, s, i, live):
                if live(1):
                    e = expert(j + 1)
                    pe.wait_ge(hx_ready, j + 2)
                    pe.wait_ge(sig_ready, j + 1)
                    hidden(1, 1 - s, e, g_ready)
                pe.wait_ge(hidT_ready, j + 1)
                pe.wait_ge(hid_ready, j + 3)
                for f in range(HF):
                    mm = pe.transpose(ps[:, 4, f * P:(f + 1) * P], hid[:, s, f * P:(f + 1) * P], ident[:, :])
                mm.then_inc(hidT_turned, 1)
                if live(1):
                    hidden(0, 1 - s, e, a_ready)
                own = expert(j)
                pe.wait_ge(y_copied, j + 1)
                pe.wait_ge(hidT_ready, j + 2)
                for f in range(HF):
                    pe.matmul(ps[:, 5, 0:D], hidT[:, s, f, :], w2[:, bass.ds(own, 1), f, :].rearrange("p o n -> p (o n)"),
                              start=(f == 0), stop=False)
                pe.matmul(ps[:, 5, 0:D], T["ones_bf"][0:NP3, :],
                          brows[:, bass.ds(own, 1), 2 * HID:BIASES].rearrange("p o n -> p (o n)"),
                          start=False, stop=True).then_inc(y_ready, 1)
                if live(2):
                    turn(s, i + 2)

            slot_tiles(pe, tile)
            for c in range(NCH):
                pe.wait_ge(gathered[c], 64)
                if c == 0:
                    pe.wait_ge(y_copied, ST + 1)
                for j in range(4):
                    mm = pe.transpose(ps[:, c, j * P:(j + 1) * P], yt[:, 4 * c + j, :], ident[:, :])
                mm.then_inc(turned, 1)

        @block.scalar
        def _(act):
            act.sem_inc(sig_ready, 1)
            act.sem_inc(y_copied, 1)
            for c in range(NCH):
                act.wait_ge(h_turned, c + 1)
                act.activation(ht[:, 4 * c:4 * c + 4, :].rearrange("p t d -> p (t d)"), ps[:, 4 + c, :], ACT.Copy)\
                   .then_inc(ht_ready, 1)

            def copy_hx(s, turned):
                act.wait_ge(t_ready, turned)
                act.activation(hx[:, s, :], ps[:, 6, 0:P], ACT.Copy).then_inc(hx_ready, 1)

            def sigmoid(s, ready, used):
                act.wait_ge(g_ready, ready)
                act.wait_ge(hid_ready, used)
                act.activation(sig[:, s, :], ps[:, 2 + s, :], ACT.Sigmoid).then_inc(sig_ready, 1)

            copy_hx(0, 3)
            copy_hx(1, 4)
            sigmoid(0, 1, 1)

            def tile(j, s, i, live):
                if live(1):
                    sigmoid(1 - s, j + 2, j + 2)
                act.wait_ge(y_ready, j + 1)
                act.activation(y[:, bass.ds(j, 1), :].rearrange("p o d -> p (o d)"), ps[:, 5, 0:D], ACT.Copy).then_inc(y_copied, 1)
                if live(2):
                    copy_hx(s, j + 5)

            slot_tiles(act, tile)

        @block.vector
        def _(dve):
            dve.sem_inc(hid_ready, 2)
            dve.sem_inc(hidT_ready, 1)
            dve.wait_ge(b_loaded, 16)
            for k in range(NP3):
                if k:
                    dve.wait_ge(b_split, 2 * k)
                dve.tensor_copy(bpart[:, k, :], bias[:, :]).then_inc(b_split, 1)
                if k < NP3 - 1:
                    dve.wait_ge(b_split, 2 * k + 1)
                    dve.tensor_tensor(bias[:, :], bias[:, :], bpart[:, k, :], ALU.subtract).then_inc(b_split, 1)
            spread = lambda ap: ap.broadcast_to([P, NT, NE])
            dve.wait_ge(routed, 1)
            dve.tensor_copy(logit[:, :, :].rearrange("p t e -> p (t e)"), ps[:, 0, 0:NT * NE]).then_inc(step, 1)
            dve.wait_ge(step, 1)
            dve.tensor_reduce(top[:, :], logit[:, :, :], AX.X, ALU.max).then_inc(step, 1)
            dve.wait_ge(step, 2)
            dve.wait_ge(constants, 3 + ST)
            dve.tensor_tensor(logit[:, :, :], logit[:, :, :], spread(top[:, :].unsqueeze(2)), ALU.is_lt).then_inc(step, 1)
            dve.wait_ge(step, 3)
            dve.scalar_tensor_tensor(out=logit[:, :, :], in0=logit[:, :, :], scalar=float(NE),
                                     in1=spread(count[:, 0:NE].unsqueeze(1)), op0=ALU.mult, op1=ALU.add).then_inc(step, 1)
            dve.wait_ge(step, 4)
            dve.tensor_reduce(top[:, :], logit[:, :, :], AX.X, ALU.min).then_inc(step, 1)
            dve.wait_ge(step, 5)
            dve.tensor_tensor(mask[:, :, :], logit[:, :, :], spread(top[:, :].unsqueeze(2)), ALU.is_equal).then_inc(step, 1)
            dve.wait_ge(ranked, 1)
            dve.tensor_copy(rank[:, :, :].rearrange("p t e -> p (t e)"), ps[:, 1, 0:(NT + 1) * NE]).then_inc(step, 1)
            dve.wait_ge(step, 7)
            dve.scalar_tensor_tensor(out=full[:, :, :], in0=rank[:, NT, :].unsqueeze(2).broadcast_to([P, NE, NT]), scalar=1.0 / P,
                                     in1=count[:, 0:NT].unsqueeze(1).broadcast_to([P, NE, NT]), op0=ALU.mult, op1=ALU.is_gt)\
               .then_inc(step, 1)
            dve.wait_ge(step, 8)
            dve.tensor_reduce(tiles[:, :], full[:, :, :], AX.X, ALU.add).then_inc(step, 1)
            dve.wait_ge(step, 9)
            dve.tensor_tensor_scan(ends[:, :], T["ones"][:, 0:NE], tiles[:, :], 0.0, ALU.mult, ALU.add).then_inc(step, 1)
            dve.wait_ge(step, 10)
            dve.tensor_tensor(tiles[:, :], ends[:, :], tiles[:, :], ALU.subtract).then_inc(step, 1)
            dve.wait_ge(step, 11)
            dve.scalar_tensor_tensor(out=rank[:, 0:NT, :], in0=spread(tiles[:, :].unsqueeze(1)), scalar=float(P),
                                     in1=rank[:, 0:NT, :], op0=ALU.mult, op1=ALU.add).then_inc(step, 1)
            dve.wait_ge(step, 12)
            dve.tensor_tensor(rank[:, 0:NT, :], rank[:, 0:NT, :], mask[:, :, :], ALU.mult).then_inc(step, 1)
            dve.wait_ge(step, 13)
            dve.tensor_reduce(slot[:, :], rank[:, 0:NT, :], AX.X, ALU.add).then_inc(step, 1)
            dve.wait_ge(step, 14)
            dve.tensor_copy(index[:, :], slot[:, :]).then_inc(step, 1)
            dve.tensor_tensor(passed[:, :, :], ends[0:1, :].unsqueeze(1).broadcast_to([1, ST, NE]),
                              count[0:1, :].unsqueeze(2).broadcast_to([1, ST, NE]), ALU.is_le).then_inc(step, 1)
            dve.wait_ge(step, 16)
            dve.tensor_reduce(owner[:, :], passed[:, :, :], AX.X, ALU.add).then_inc(step, 1)
            dve.wait_ge(step, 17)
            dve.tensor_scalar(expert_of[:, 0:ST], owner[:, :], float(NE - 1), None, ALU.min).then_inc(step, 1)

            def gate(s, a, sigmoids):
                dve.wait_ge(a_ready, a)
                dve.wait_ge(sig_ready, sigmoids)
                dve.tensor_tensor(hid[:, s, :], ps[:, s, :], sig[:, s, :], ALU.mult).then_inc(hid_ready, 1)

            gate(0, 1, 2)

            def tile(j, s, i, live):
                dve.wait_ge(hidT_turned, j + 1)
                dve.tensor_copy(hidT[:, s, :, :].rearrange("p f t -> p (f t)"), ps[:, 4, :]).then_inc(hidT_ready, 1)
                if live(1):
                    gate(1 - s, j + 2, j + 3)

            slot_tiles(dve, tile)
            for c in range(NCH):
                dve.wait_ge(turned, c + 1)
                b = c * CH // SEQ
                dve.scalar_tensor_tensor(out=x[:, chunk(c)], in0=ps[:, c, :], scalar=T["mod"][:, 1, 5, b:b + 1],
                                         in1=x[:, chunk(c)], op0=ALU.mult, op1=ALU.add).then_inc(x_ready, 1)


def build(nc, A, out):
    with ExitStack() as whole:
        core = Core(nc, whole)
        T = {}
        for name, shape, dt in [("xT", [P, TOK], F32), ("hT", [P, TOK], F32), ("mean_w", [P, P], F32),
                                ("ones", [P, P], F32), ("ones_bf", [P, P], BF16), ("ident_bf", [P, P], BF16), ("ident", [P, P], F32),
                                ("eps", [P, 1], F32), ("mod", [P, 2, 6, NB], F32), ("gates", [P, NB, N_ACT], F32),
                                ("gate_bo", [P, NB], F32), ("head_index", [1, NB * N_ACT], U32)]:
            T[name] = core.sb(whole, name, shape, dt)
        T["ps"] = whole.enter_context(nc.psum_tensor("ps", [P, 8, CH], F32))
        scratch = lambda n, shape, dt: nc.dram_tensor(n, shape, dt, kind="Internal").ap()
        dram = {"qk": scratch("qk_parts", [3, NP3, NB, P, SEQ], BF16), "table": scratch("table_parts", [NP3, HD + 1, NREL], BF16),
                "const": scratch("const_rows", [3, NP3, SEQ], BF16), "rel": scratch("rel_rows", [2, NT_B, P * NREL], F32)}
        for name in ("h_sorted", "y_sorted"):
            dram[name] = scratch(name, [ST * P, D], F32)
        dram["rows"] = [dram["qk"][a].rearrange("k b r t -> k (b r) t") for a in range(3)]
        bc_dram = nc.dram_tensor("bc_parts", [3, NB, 2, NS, SEQ], BF16, kind="Internal").ap()
        constants_and_modulation(nc, core, T, A)
        layernorm(nc, core, T, "ln0", 0, 0, T["hT"])
        for L in range(NL):
            mamba_layer(nc, core, T, A, L, bc_dram)
        core.reuse_semaphores()
        layernorm(nc, core, T, "ln1", 0, 3, T["hT"], residual=(T["hT"], 0, 2))
        route_heads(nc, core, T, A)
        chosen_heads(nc, core, T, A)
        layernorm(nc, core, T, "ln2", 1, 0, T["hT"])
        second_attention(nc, core, T, A, dram)
        layernorm(nc, core, T, "ln3", 1, 3, T["hT"])
        experts(nc, core, T, A, dram, out)


def layout(inputs):
    import numpy as np
    f = lambda n: np.ascontiguousarray(inputs[n])
    t = lambda a: np.ascontiguousarray(np.moveaxis(a, -1, -2))
    a = {
        "xT": t(f("L0_attn_x").reshape(TOK, D)),
        "c0": t(f("L0_c")), "c1": t(f("L1_c")), "wmod0": f("L0_wmod"), "wmod1": f("L1_wmod"),
        "normw": f("L0_attn_norm_w")[:, :, None],
        "win": t(f("L0_attn_Win")), "wx": t(f("L0_attn_Wx")), "wdt": t(f("L0_attn_Wdt")), "wout": t(f("L0_attn_Wout")),
        "chan": np.concatenate([f("L0_attn_conv_w"), f("L0_attn_conv_b")[..., None], f("L0_attn_bdt")[..., None],
                                f("L0_attn_Dp")[..., None], f("L0_attn_A_log")], axis=-1),
    }
    wqkv1 = f("L1_attn_Wqkv").reshape(H1, 3, HD, D).transpose(3, 1, 0, 2).reshape(D, 3, D)
    bqkv1 = f("L1_attn_bqkv").reshape(H1, 3, HD).transpose(1, 0, 2).reshape(3, D)
    table, tbias = f("L1_attn_Wr"), f("L1_attn_br")
    a.update({
        "wqkv1": wqkv1, "bv1": bqkv1[2:3], "brow": tbias[None, [0, NREL - 1]],
        "cols1": np.stack([bqkv1[0], bqkv1[1], np.tile(table[0], H1), np.tile(table[NREL - 1], H1)], axis=-1),
        "table": np.concatenate([table.T, tbias[None, :]], axis=0),
        "table_edge": np.concatenate([table[0], tbias[0:1]])[:, None],
    })
    heads = [f(f"L0_ffn_W{n}").reshape(D, N_HEAD, DH).transpose(1, 0, 2) for n in "qkv"]
    biases = [f(f"L0_ffn_b{n}").reshape(N_HEAD, DH) for n in "qkv"]
    a.update({
        "wr": f("L0_ffn_Wr"), "br": f("L0_ffn_br")[None, :], "bo": f("L0_ffn_bo")[:, None],
        "wqkv_h": np.concatenate(heads, axis=-1), "bqkv_h": np.stack(biases, axis=-1), "bv_h": biases[2],
        "router_w": f("L1_ffn_router_w"), "router_b": f("L1_ffn_router_b")[None, :], "w1": f("L1_ffn_w1"),
        "biases": np.concatenate([f("L1_ffn_b1"), f("L1_ffn_b2")], 1), "w2": f("L1_ffn_w2"),
        "wo_k": f("L0_ffn_Wo").reshape(N_ACT, DH, D),
    })
    return {k: np.ascontiguousarray(v) for k, v in a.items()}


def kernel(**inputs):
    import numpy as _np
    import concourse.bacc as _bacc
    from concourse import mybir as _mybir
    from concourse.bass_utils import run_bass_kernel_spmd as _run

    nc = _bacc.Bacc("TRN2", target_bir_lowering=False, num_devices=1)
    arrays = layout(inputs)
    aps = {n: nc.dram_tensor(f"in_{n}", a.shape, _mybir.dt.from_np(a.dtype), kind="ExternalInput").ap()
           for n, a in arrays.items()}
    out = nc.dram_tensor("out_xT", (D, TOK), _mybir.dt.float32, kind="ExternalOutput").ap()
    build(nc, aps, out)
    r = _run(nc, [{f"in_{n}": a for n, a in arrays.items()}], core_ids=[0])
    return _np.ascontiguousarray(r.results[0]["out_xT"].T).reshape(NB, SEQ, D)
```

```python
from contextlib import ExitStack
import concourse.bass as bass
from concourse import mybir

F32 = mybir.dt.float32
BF16 = mybir.dt.bfloat16
U32 = mybir.dt.uint32
ALU = mybir.AluOpType
ACT = mybir.ActivationFunctionType
AX = mybir.AxisListType

P = 128
NB = 2
SEQ = 1024
TOK = NB * SEQ
D = 128
CH = 512
NCH = TOK // CH
EPS = 1e-5
NL = 2
ED = 256
NH2 = ED // P
NS = 16
RK = 64
NCONV = 4


class Core:

    def __init__(self, nc, whole):
        self.nc = nc
        self.whole = whole
        self.sems = []

    def sb(self, stack, name, shape, dt=F32):
        return stack.enter_context(self.nc.sbuf_tensor(name, shape, dt))

    def sem(self, name):
        handle = self.nc.alloc_semaphore(name=name)
        self.sems.append(handle)
        return handle

    def reuse_semaphores(self):
        self.nc.clear_and_free_semaphores(self.sems)
        self.nc.all_engine_barrier()
        self.sems = []


def chunk(c):
    return slice(c * CH, (c + 1) * CH)


def constants_and_modulation(nc, core, T, A):
    with ExitStack() as st:
        cT = core.sb(st, "cT", [P, 2, NB])
        silu_c = core.sb(st, "silu_c", [P, 2, NB])
        wmod = core.sb(st, "wmod", [P, 2, 6 * D])
        sign = core.sb(st, "gate_sign", [P, 2, 2, NB])
        size = core.sb(st, "gate_size", [P, 2, 2, NB])
        x_loaded, c_loaded, wmod_loaded = core.sem("x_loaded"), core.sem("c_loaded"), core.sem("wmod_loaded")
        silu_ready, mod_summed = core.sem("silu_c_ready"), core.sem("mod_summed")
        mod_step, const_ready = core.sem("mod_step"), core.sem("const_ready")
        block = st.enter_context(nc.Block())

        @block.sync
        def _(sp):
            for l in range(2):
                sp.dma_start(cT[:, l, :], A[f"c{l}"]).then_inc(c_loaded, 16)
                sp.dma_start(wmod[:, l, :], A[f"wmod{l}"]).then_inc(wmod_loaded, 16)
            sp.dma_start(T["xT"][:, :], A["xT"]).then_inc(x_loaded, 16)
            sp.wait_ge(x_loaded, 16)

        @block.gpsimd
        def _(pool):
            pool.memset(T["mean_w"][:, :], 1.0 / D).then_inc(const_ready, 1)
            pool.memset(T["ones_bf"][:, :], 1.0).then_inc(const_ready, 1)
            pool.memset(T["ones"][:, :], 1.0).then_inc(const_ready, 1)
            pool.memset(T["eps"][:, :], EPS).then_inc(const_ready, 1)
            pool.memset(T["ident"][:, :], 0.0).then_inc(const_ready, 1)
            pool.wait_ge(const_ready, 5)
            pool.affine_select(out=T["ident"][:, :], in_=T["ident"][:, :], compare_op=ALU.not_equal, fill=1.0,
                               base=0, pattern=[[-1, P]], channel_multiplier=1).then_inc(const_ready, 1)
            pool.wait_ge(const_ready, 6)
            pool.tensor_copy(T["ident_bf"][:, :], T["ident"][:, :]).then_inc(const_ready, 1)

        @block.scalar
        def _(act):
            act.wait_ge(c_loaded, 32)
            act.activation(silu_c[:, :, :], cT[:, :, :], ACT.Silu).then_inc(silu_ready, 1)

        @block.tensor
        def _(pe):
            pe.wait_ge(silu_ready, 1)
            pe.wait_ge(wmod_loaded, 32)
            for l in range(2):
                for j in range(6):
                    at = (l * 6 + j) * NB
                    mm = pe.matmul(T["ps"][:, 0, at:at + NB], wmod[:, l, j * D:(j + 1) * D], silu_c[:, l, :],
                                   start=True, stop=True)
            mm.then_inc(mod_summed, 1)

        @block.vector
        def _(dve):
            mod = T["mod"]
            dve.wait_ge(mod_summed, 1)
            dve.tensor_copy(mod[:, :, :, :].rearrange("p l j b -> p (l j b)"), T["ps"][:, 0, 0:2 * 6 * NB])\
               .then_inc(mod_step, 1)
            dve.wait_ge(mod_step, 1)
            scales = mod[:, :, 1::3, :]
            gates = mod[:, :, 2::3, :]
            dve.tensor_scalar(scales, scales, 1.0, None, ALU.add).then_inc(mod_step, 1)
            dve.tensor_scalar(sign[:, :, :, :], gates, 0.0, 2.0, ALU.is_ge, ALU.mult).then_inc(mod_step, 1)
            dve.scalar_tensor_tensor(out=size[:, :, :, :], in0=gates, scalar=-1.0, in1=gates,
                                     op0=ALU.mult, op1=ALU.max).then_inc(mod_step, 1)
            dve.wait_ge(mod_step, 4)
            dve.tensor_scalar(size[:, :, :, :], size[:, :, :, :], 0.25, None, ALU.max).then_inc(mod_step, 1)
            dve.wait_ge(mod_step, 5)
            dve.scalar_tensor_tensor(out=gates, in0=sign[:, :, :, :], scalar=-1.0, in1=size[:, :, :, :],
                                     op0=ALU.add, op1=ALU.mult).then_inc(mod_step, 1)


def spread_column(pe, T, column, c):
    for j in range(CH // P):
        t = c * (CH // P) + j
        mm = pe.matmul(T["ps"][:, c, j * P:(j + 1) * P], column[:, t:t + 1].broadcast_to([P, P]), T["ident"][:, :],
                       start=True, stop=True)
    return mm


def column_means(pe, T, sq, c, bank):
    for j in range(CH // P):
        t = c * (CH // P) + j
        mm = pe.matmul(T["ps"][:, bank, t:t + 1], sq[:, t * P:(t + 1) * P], T["mean_w"][:, 0:1], start=True, stop=True)
    return mm


def layernorm(nc, core, T, name, layer, part, dst, residual=None):
    x, ps, mod = T["xT"], T["ps"], T["mod"]
    NT = TOK // P
    with ExitStack() as st:
        cen = core.sb(st, name + "_centred", [P, TOK])
        sq = core.sb(st, name + "_square", [P, TOK])
        rstd = core.sb(st, name + "_rstd", [P, NT])
        mean_ready, centred, squared = core.sem(name + "_mean"), core.sem(name + "_centred"), core.sem(name + "_squared")
        var_ready, std_ready, rstd_ready = core.sem(name + "_var"), core.sem(name + "_std"), core.sem(name + "_rstd")
        spread = core.sem(name + "_spread")
        normed, done, x_added = core.sem(name + "_normed"), core.sem(name + "_done"), core.sem(name + "_residual")
        block = st.enter_context(nc.Block())

        @block.tensor
        def _(pe):
            for c in range(NCH):
                if residual is not None:
                    pe.wait_ge(x_added, c + 1)
                pe.matmul(ps[:, c, :], T["mean_w"][:, :], x[:, chunk(c)], start=True, stop=True).then_inc(mean_ready, 1)
            for c in range(NCH):
                pe.wait_ge(squared, c + 1)
                mm = column_means(pe, T, sq, c, 4)
            mm.then_inc(var_ready, 1)
            pe.wait_ge(rstd_ready, 1)
            for c in range(NCH):
                spread_column(pe, T, rstd, c).then_inc(spread, 1)

        @block.scalar
        def _(act):
            for c in range(NCH):
                act.wait_ge(centred, c + 1)
                act.activation(sq[:, chunk(c)], cen[:, chunk(c)], ACT.Square).then_inc(squared, 1)
            act.wait_ge(var_ready, 1)
            act.activation(rstd[:, :], ps[:, 4, 0:NT], ACT.Sqrt, bias=T["eps"][:, 0:1]).then_inc(std_ready, 1)
            for c in range(NCH):
                b = c * CH // SEQ
                act.wait_ge(normed, c + 1)
                act.activation(dst[:, chunk(c)], cen[:, chunk(c)], ACT.Identity, bias=mod[:, layer, part, b:b + 1])\
                   .then_inc(done, 1)

        @block.vector
        def _(dve):
            if residual is not None:
                src, l, j = residual
                for c in range(NCH):
                    b = c * CH // SEQ
                    dve.scalar_tensor_tensor(out=x[:, chunk(c)], in0=src[:, chunk(c)], scalar=mod[:, l, j, b:b + 1],
                                             in1=x[:, chunk(c)], op0=ALU.mult, op1=ALU.add).then_inc(x_added, 1)
            for c in range(NCH):
                dve.wait_ge(mean_ready, c + 1)
                dve.tensor_tensor(cen[:, chunk(c)], x[:, chunk(c)], ps[:, c, :], ALU.subtract).then_inc(centred, 1)
            dve.wait_ge(std_ready, 1)
            dve.reciprocal(rstd[:, :], rstd[:, :]).then_inc(rstd_ready, 1)
            dve.wait_ge(centred, NCH)
            for c in range(NCH):
                b = c * CH // SEQ
                dve.wait_ge(spread, c + 1)
                dve.scalar_tensor_tensor(out=cen[:, chunk(c)], in0=cen[:, chunk(c)],
                                         scalar=mod[:, layer, part + 1, b:b + 1], in1=ps[:, c, :],
                                         op0=ALU.mult, op1=ALU.mult).then_inc(normed, 1)


def log1p_factors(degree=8):
    import numpy as np
    f = lambda e: np.log1p(e) / e
    poly = np.polynomial.chebyshev.Chebyshev.interpolate(f, degree, domain=[0, 1])\
        .convert(kind=np.polynomial.Polynomial, domain=[-1, 1], window=[-1, 1])
    s = poly.coef[-1] ** (1 / degree)
    roots = [z for z in poly.roots() if z.imag > 0]
    assert len(roots) == degree // 2
    return float(s), [(float(-s * z.real), float((s * z.imag) ** 2)) for z in roots]


def mamba_layer(nc, core, T, A, L, bc_dram):
    h, ps = T["hT"], T["ps"]
    n = f"m{L}_"
    with ExitStack() as st:
        def sb(name, shape, dt=F32):
            return core.sb(st, n + name, shape, dt)

        def sem(name):
            return core.sem(n + name)

        win = sb("win", [P, 2 * ED])
        wx = sb("wx", [P, NH2, RK + 2 * NS])
        wdt = sb("wdt", [RK, ED])
        wout = sb("wout", [P, NH2, D])
        normw = sb("normw", [P, 1])
        chan = sb("chan", [P, NH2, NCONV + 3 + NS])
        TAP, CB, BDT, DP, AL = 0, NCONV, NCONV + 1, NCONV + 2, NCONV + 3
        rate = sb("rate", [P, NH2, NS])
        diag_d = sb("diag_d", [P, NH2, P])
        silu_z = sb("silu_z", [P, NH2, TOK])
        xs = sb("xs", [P, NH2, TOK])
        delta = sb("delta", [P, NH2, TOK])
        du = sb("du", [P, NH2, TOK])
        decay = sb("decay", [P, 2, NH2, SEQ])
        drive = sb("drive", [P, 2, NH2, SEQ])
        PADW = NCONV - 1 + SEQ
        work = sb("work", [P, NH2 * NB * PADW])
        pad = work[:, :].rearrange("p (m b t) -> p m b t", m=NH2, b=NB)
        prod = work[:, 0:2 * NH2 * SEQ].rearrange("p (s m t) -> p s m t", s=2, m=NH2)
        hs = sb("hs", [P, NH2, SEQ])
        bc = sb("bc", [P, 2, 2, SEQ])
        rows = sb("rows", [3, 2, 2, SEQ], BF16)
        xn = hs[:, :, :].rearrange("p m t -> p (m t)")
        rs = bc[:, 0, :, :].rearrange("p m t -> p (m t)")
        dbc = bc[0:RK + 2 * NS, 1, :, :].rearrange("p m t -> p (m t)")
        parts = work[:, 0:3 * TOK // 2].bitcast(BF16).rearrange("p (k t) -> p k t", k=3)
        BCR = slice(RK, RK + 2 * NS)
        flat = decay[:, :, :, :].rearrange("p s m t -> p (s m t)")
        flat2 = drive[:, :, :, :].rearrange("p s m t -> p (s m t)")
        rstd = sb("rstd", [P, TOK // P])
        slope, factors = log1p_factors()
        shifts = sb("log_shifts", [P, len(factors)])

        factor_order = [(2 * len(factors) * p + 2 * i + j, 2 * p + j, i)
                        for p in range(NB) for i in range(len(factors)) for j in range(2)]
        MORE_AT = 2
        loaded = sem("loaded")
        spread_ready = sem("spread")
        vmax, sq_ready, log_step, delta_ready, du_ready = (sem(x) for x in ("vmax", "sq", "log", "delta", "du"))
        squared, ms_ready, std_ready, rstd_ready, normed = (sem(x) for x in ("squared", "ms", "std", "rstd", "normed"))
        proj_ready, z_ready, xc_copied = sem("proj"), sem("z"), sem("xc")
        xc_late = sem("xc_late")
        pad_zero, conv_step, conv_done, xs_ready = sem("padzero"), sem("convstep"), sem("conv"), sem("xs")
        small = sem("small")
        neg = sem("neg")
        dbc_ready, dt_copied, split_step = sem("dbc"), sem("dt"), sem("split")
        bc_stored = [sem(f"bcstored{b}") for b in range(NB)]
        du_late = sem("du_late")
        dl_ready, ab_ready, ex_ready = (sem(x) for x in ("dl", "abs", "exp"))
        rows_ready = [[sem(f"{v}rows{i}") for i in range(2)] for v in "bc"]
        row_spread, row_copied = [sem("bspread"), sem("cspread")], [sem("bcopied"), sem("ccopied")]
        decay_ready, drive_ready = sem("decay"), sem("drive")
        scanned, multiplied, y_summed = sem("scanned"), sem("multiplied"), sem("ysum")
        y_init, gated, out_ready, added = sem("yinit"), sem("gated"), sem("out"), sem("added")

        block = st.enter_context(nc.Block())
        B_, C_ = 0, 1

        def steps(eng, b, body, first=0):
            last = b == NB - 1
            with eng.Fori(first // 2, NS // 2 - 2 * last) as i:
                for s in range(2):
                    body(b * NS + 2 * i + s, 2 * i + s, s, lambda k: True)
            if last:
                for n in range(NS - 4, NS):
                    body(b * NS + n, n, n % 2, lambda k: n + k < NS)

        @block.sync
        def _(sp):
            sp.dma_start(win[:, :], A["win"][L]).then_inc(loaded, 16)
            sp.dma_start(normw[:, :], A["normw"][L]).then_inc(loaded, 16)
            sp.dma_start(chan[:, :, :], A["chan"][L].rearrange("(m p) k -> p m k", p=P)).then_inc(loaded, 16)
            sp.dma_start(wx[:, :, :], A["wx"][L].rearrange("(m p) r -> p m r", p=P)).then_inc(loaded, 16)
            sp.dma_start(wdt[:, :], A["wdt"][L]).then_inc(loaded, 16)
            sp.dma_start(wout[:, :, :], A["wout"][L].rearrange("(m p) d -> p m d", p=P)).then_inc(loaded, 16)
            for b in range(NB):
                sp.wait_ge(split_step, 5 * (b + 1))
                for k in range(3):
                    sp.dma_start(bc_dram[k, b].rearrange("v n t -> (v n) t"), parts[BCR, k, b * SEQ:(b + 1) * SEQ])\
                      .then_inc(bc_stored[b], 16)
            for b in range(NB):
                sp.wait_ge(bc_stored[b], 48)
                with sp.Fori(0, NS // 2) as i:
                    for s in range(2):
                        for v in (B_, C_):
                            sp.wait_ge(row_spread[v], b * NS + 2 * i + s + 1)
                            sp.dma_start(rows[:, v, s, :], bc_dram[:, b, v, bass.ds(2 * i + s, 1), :].rearrange('k n t -> k (n t)'))\
                              .then_inc(rows_ready[v][s], 16)

        @block.gpsimd
        def _(pool):
            for m in range(NH2):
                pool.memset(pad[:, m, :, 0:NCONV - 1], 0.0).then_inc(pad_zero, 1)
            pool.wait_ge(loaded, 96)
            for m in range(NH2):
                pool.tensor_scalar(diag_d[:, m, :], T["ident"][:, :], chan[:, m, DP:DP + 1], None, ALU.mult)\
                    .then_inc(small, 1)
            for i, (shift, _) in enumerate(factors):
                pool.memset(shifts[:, i:i + 1], shift).then_inc(small, 1)
            pool.wait_ge(small, NH2 + len(factors))
            pool.wait_ge(conv_done, 4)
            for b in range(NB):
                own = dbc[BCR, b * SEQ:(b + 1) * SEQ]
                pool.wait_ge(dt_copied, 2 * b + 2)
                for k in range(3):
                    p = parts[BCR, k, b * SEQ:(b + 1) * SEQ]
                    if k or b:
                        pool.wait_ge(split_step, 5 * b + 2 * k)
                    pool.tensor_copy(p, own).then_inc(split_step, 1)
                    if k < 2:
                        pool.wait_ge(split_step, 5 * b + 2 * k + 1)
                        pool.tensor_tensor(own, own, p, ALU.subtract).then_inc(split_step, 1)
            pool.wait_ge(split_step, 10)
            for m in range(NH2):
                pool.wait_ge(delta_ready, m + 1)
                pool.tensor_tensor(du[:, m, 0:SEQ], delta[:, m, 0:SEQ], xs[:, m, 0:SEQ], ALU.mult).then_inc(du_ready, 1)
            pool.wait_ge(du_ready, 2)
            pool.sem_inc(drive_ready, 2)
            for b in range(NB):
                if b:
                    pool.wait_ge(du_late, 2)
                with pool.Fori(0, NS // 2) as i:
                    for s in range(2):
                        g = b * NS + 2 * i + s
                        pool.wait_ge(row_copied[B_], g + 1)
                        pool.wait_ge(scanned, 2 * (g + 1))
                        pool.tensor_tensor(drive[:, s, :, :], du[:, :, b * SEQ:(b + 1) * SEQ],
                                           bc[:, B_, s:s + 1, :].broadcast_to([P, NH2, SEQ]), ALU.mult).then_inc(drive_ready, 1)

        @block.tensor
        def _(pe):
            for c in range(NCH):
                pe.wait_ge(squared, c + 1)
                mm = column_means(pe, T, rs, c, 4)
            mm.then_inc(ms_ready, 1)
            pe.wait_ge(rstd_ready, 1)
            for c in range(NCH):
                spread_column(pe, T, rstd, c).then_inc(spread_ready, 1)
            pe.wait_ge(loaded, 96)
            for c in range(NCH):
                pe.wait_ge(normed, c + 1)
                for m in range(4):
                    if c == 0 and m == 0:
                        pe.wait_ge(normed, NCH)
                    if c >= 2:
                        pe.wait_ge(z_ready, 2 * (c - 1))
                        pe.wait_ge(xc_copied, 2 * (c - 1))
                    pe.matmul(ps[:, (c % 2) * 4 + m, :], win[:, m * P:(m + 1) * P], xn[:, chunk(c)],
                              start=True, stop=True).then_inc(proj_ready, 1)
            pe.wait_ge(z_ready, 8)
            pe.wait_ge(xc_late, 4)
            for b in range(NB):
                pe.wait_ge(xs_ready, 2 * b + 2)
                for c in (2 * b, 2 * b + 1):
                    for m in range(NH2):
                        mm = pe.matmul(ps[0:RK + 2 * NS, c, :], wx[:, m, :], xs[:, m, chunk(c)],
                                       start=(m == 0), stop=(m == NH2 - 1))
                    mm.then_inc(dbc_ready, 1)
                pe.wait_ge(dt_copied, 2 * b + 2)
                for m in range(NH2):
                    u = b * NH2 + m
                    for c in range(2):
                        mm = pe.matmul(ps[:, (4 + 2 * u + c) % 8, :], wdt[:, m * P:(m + 1) * P],
                                       dbc[0:RK, chunk(2 * b + c)], start=True, stop=True)
                    mm.then_inc(dl_ready, 1)
            pe.wait_ge(small, 2)
            for x in (*row_spread, y_summed):
                pe.sem_inc(x, 2)

            def spread(v, s, turn, before):
                pe.wait_ge(rows_ready[v][s], 16 * turn)
                if not isinstance(before, int) or before:
                    pe.wait_ge(row_copied[v], before)
                for c in range(2):
                    mm = pe.matmul(ps[:, 4 + 2 * v + c, :], T["ones_bf"][0:3, :],
                                   rows[:, v, s, c * CH:(c + 1) * CH], start=True, stop=True)
                mm.then_inc(row_spread[v], 1)

            def start_sums(b):
                for m in range(NH2):
                    for c in range(2):
                        mm = pe.matmul(ps[:, 2 * m + c, :], diag_d[:, m, :], xs[:, m, chunk(2 * b + c)],
                                       start=True, stop=False, skip_group_check=True)
                mm.then_inc(y_init, 1)

            pe.wait_ge(ab_ready, 4)
            pe.wait_ge(vmax, 4)
            start_sums(0)
            spread(B_, 0, 1, 0)
            spread(C_, 0, 1, 0)
            spread(B_, 1, 1, 1)
            spread(B_, 0, 2, 2)
            spread(C_, 1, 1, 1)
            for b in range(NB):
                def step(g, n, s, live):
                    turn = lambda k: (g - s) // 2 + (s + k) // 2 + 1
                    for m in range(NH2):
                        pe.wait_ge(multiplied, 2 * g + 5 + m)
                        for c in range(2):
                            mm = pe.matmul(ps[:, 2 * m + c, :], T["ident"][:, :], prod[:, s, m, c * CH:(c + 1) * CH],
                                           start=False, stop=False, skip_group_check=True)
                        if m == 0 and live(3):
                            spread(B_, 1 - s, turn(3), g + 3)
                    mm.then_inc(y_summed, 1)
                    if live(2):
                        spread(C_, s, turn(2), g + 2)

                steps(pe, b, step)
                pe.wait_ge(gated, 2 * (b + 1))
                for c in range(2):
                    for m in range(NH2):
                        mm = pe.matmul(ps[:, c, :], wout[:, m, :], silu_z[:, m, chunk(2 * b + c)],
                                       start=(m == 0), stop=(m == NH2 - 1))
                    mm.then_inc(out_ready, 1)
                if b < NB - 1:
                    pe.wait_ge(added, 2 * (b + 1))
                    start_sums(b + 1)

        @block.scalar
        def _(act):
            for c in range(NCH):
                act.activation(rs[:, chunk(c)], h[:, chunk(c)], ACT.Square).then_inc(squared, 1)
            act.wait_ge(ms_ready, 1)
            act.activation(rstd[:, :], ps[:, 4, 0:TOK // P], ACT.Sqrt, bias=T["eps"][:, 0:1]).then_inc(std_ready, 1)
            for c in range(NCH):
                if c >= 2:
                    for m in range(NH2):
                        act.wait_ge(pad_zero, 2)
                        act.wait_ge(proj_ready, 4 * c + 1 + m)
                        act.activation(pad[:, m, 1, NCONV - 1 + (c - 2) * CH:NCONV - 1 + (c - 1) * CH],
                                       ps[:, (c % 2) * 4 + m, :], ACT.Copy).then_inc(xc_late, 1)
                for m in range(NH2):
                    act.wait_ge(proj_ready, 4 * c + 3 + m)
                    act.activation(silu_z[:, m, chunk(c)], ps[:, (c % 2) * 4 + NH2 + m, :], ACT.Silu)\
                       .then_inc(z_ready, 1)
            act.wait_ge(loaded, 96)
            for b in range(NB):
                for m in range(NH2):
                    t = slice(b * SEQ, (b + 1) * SEQ)
                    act.wait_ge(conv_done, 2 * b + m + 1)
                    act.activation(xs[:, m, t], xs[:, m, t], ACT.Silu, bias=chan[:, m, CB:CB + 1]).then_inc(xs_ready, 1)
            act.activation(rate[:, :, :], chan[:, :, AL:AL + NS], ACT.Exp).then_inc(neg, 1)
            act.wait_ge(small, NH2 + len(factors))

            def exponential(u):
                q = slice(u * SEQ, (u + 1) * SEQ)
                bank = (4 + 2 * u) % 8
                act.wait_ge(dl_ready, u + 1)
                act.wait_ge(vmax, u + 1)
                act.activation(flat[:, q].rearrange("p (a t) -> p a t", a=2), ps[:, bank:bank + 2, :], ACT.Abs,
                               bias=chan[:, u % NH2, BDT:BDT + 1]).then_inc(ab_ready, 1)
                act.wait_ge(ab_ready, u + 1)
                act.activation(flat[:, q], flat[:, q], ACT.Exp, scale=-1.0).then_inc(ex_ready, 1)

            exponential(0)
            exponential(1)
            for k, u, i in factor_order:
                if k == MORE_AT:
                    exponential(2)
                    exponential(3)
                act.wait_ge(ex_ready, u + 1)
                if k >= 2:
                    act.wait_ge(log_step, k - 1)
                act.activation(hs[:, u % 2, :], flat[:, u * SEQ:(u + 1) * SEQ], ACT.Square, scale=slope, bias=shifts[:, i:i + 1])\
                   .then_inc(sq_ready, 1)
            act.wait_ge(neg, 2)

            def copy_row(v, s, spread, used, uses):
                act.wait_ge(row_spread[v], spread)
                act.wait_ge(used, uses)
                act.activation(bc[:, v, s, :].rearrange("p (c t) -> p c t", t=CH), ps[:, 4 + 2 * v:6 + 2 * v, :],
                               ACT.Copy).then_inc(row_copied[v], 1)

            copy_row(B_, 0, 3, drive_ready, 1)
            for b in range(NB):
                def step(g, n, s, live):
                    for m in range(NH2):
                        act.wait_ge(scanned, 2 * g + 1 + m)
                        act.activation(decay[:, s, m, :], delta[:, m, b * SEQ:(b + 1) * SEQ], ACT.Exp,
                                       scale=rate[:, m, bass.ds(n, 1)]).then_inc(decay_ready, 1)
                    if live(1):
                        copy_row(B_, 1 - s, g + 4, drive_ready, g + 2)
                    copy_row(C_, s, g + 3, multiplied, 2 * g + 2)

                steps(act, b, step)

        @block.vector
        def _(dve):
            dve.wait_ge(loaded, 96)
            dve.wait_ge(std_ready, 1)
            dve.reciprocal(rstd[:, :], rstd[:, :]).then_inc(rstd_ready, 1)
            for c in range(NCH):
                dve.wait_ge(spread_ready, c + 1)
                dve.scalar_tensor_tensor(out=xn[:, chunk(c)], in0=h[:, chunk(c)], scalar=normw[:, 0:1],
                                         in1=ps[:, c, :], op0=ALU.mult, op1=ALU.mult).then_inc(normed, 1)
            dve.wait_ge(pad_zero, 2)
            for c in range(2):
                for m in range(NH2):
                    dve.wait_ge(proj_ready, 4 * c + 1 + m)
                    dve.tensor_copy(pad[:, m, 0, NCONV - 1 + c * CH:NCONV - 1 + (c + 1) * CH],
                                    ps[:, (c % 2) * 4 + m, :]).then_inc(xc_copied, 1)

            def convolve(b, m):
                n = (NCONV - 1) * (b * NH2 + m)
                t = xs[:, m, b * SEQ:(b + 1) * SEQ]
                dve.wait_ge(xc_late if b else xc_copied, 4)
                dve.tensor_scalar(t, pad[:, m, b, 0:SEQ], chan[:, m, TAP:TAP + 1], None, ALU.mult)\
                   .then_inc(conv_step, 1)
                for k in range(1, NCONV):
                    dve.wait_ge(conv_step, n + k)
                    last = dve.scalar_tensor_tensor(out=t, in0=pad[:, m, b, k:k + SEQ],
                                                    scalar=chan[:, m, TAP + k:TAP + k + 1], in1=t,
                                                    op0=ALU.mult, op1=ALU.add)
                    if k < NCONV - 1:
                        last.then_inc(conv_step, 1)
                last.then_inc(conv_done, 1)

            def copy_dbc(c):
                dve.wait_ge(dbc_ready, c + 1)
                dve.tensor_copy(dbc[:, chunk(c)], ps[0:RK + 2 * NS, c, :]).then_inc(dt_copied, 1)

            def positive(u):
                b, m = divmod(u, NH2)
                bank = (4 + 2 * u) % 8
                dve.wait_ge(dl_ready, u + 1)
                dve.tensor_scalar(du[:, m, b * SEQ:(b + 1) * SEQ].rearrange("p (a t) -> p a t", a=2),
                                  ps[:, bank:bank + 2, :], chan[:, m, BDT:BDT + 1], 0.0, ALU.add, ALU.max)\
                   .then_inc(vmax, 1)

            convolve(0, 0)
            convolve(0, 1)
            convolve(1, 0)
            copy_dbc(0)
            copy_dbc(1)
            convolve(1, 1)
            positive(0)
            positive(1)
            copy_dbc(2)
            copy_dbc(3)
            dve.wait_ge(neg, 1)
            dve.tensor_scalar(rate[:, :, :], rate[:, :, :], -1.0, None, ALU.mult).then_inc(neg, 1)
            for k, u, i in factor_order:
                if k == MORE_AT:
                    positive(2)
                    positive(3)
                b, m = divmod(u, NH2)
                t = slice(b * SEQ, (b + 1) * SEQ)
                q = slice(u * SEQ, (u + 1) * SEQ)
                dve.wait_ge(sq_ready, k + 1)
                if i:
                    dve.wait_ge(log_step, k - 1)
                dve.scalar_tensor_tensor(out=flat2[:, q], in0=hs[:, u % 2, :], scalar=factors[i][1],
                                         in1=flat2[:, q] if i else flat[:, q], op0=ALU.add, op1=ALU.mult)\
                   .then_inc(log_step, 1)
                if i == len(factors) - 1 and u % 2:
                    for v in (u - 1, u):
                        dve.wait_ge(log_step, k + v - u + 1)
                        q = slice(v * SEQ, (v + 1) * SEQ)
                        dve.tensor_tensor(delta[:, v % 2, t], flat2[:, q], du[:, v % 2, t], ALU.add).then_inc(delta_ready, 1)
                    if b == 0:
                        dve.wait_ge(delta_ready, 2)
                        dve.sem_inc(scanned, 2)
            for m in range(NH2):
                dve.wait_ge(delta_ready, 3 + m)
                dve.tensor_tensor(du[:, m, SEQ:TOK], delta[:, m, SEQ:TOK], xs[:, m, SEQ:TOK], ALU.mult).then_inc(du_late, 1)
            dve.wait_ge(du_late, 2)
            dve.sem_inc(scanned, 2)
            dve.wait_ge(bc_stored[NB - 1], 48)
            dve.sem_inc(multiplied, 4)

            def add_output(b):
                for c in range(2):
                    dve.wait_ge(out_ready, 2 * b + c + 1)
                    tt = chunk(2 * b + c)
                    dve.tensor_tensor(h[:, tt], h[:, tt], ps[:, c, :], ALU.add).then_inc(added, 1)

            def step(g, n, s, live):
                dve.wait_ge(drive_ready, g + 3)
                for m in range(NH2):
                    dve.wait_ge(decay_ready, 2 * g + 1 + m)
                    dve.wait_ge(multiplied, 2 * g + 3 + m)
                    dve.tensor_tensor_scan(hs[:, m, :], decay[:, s, m, :], drive[:, s, m, :], 0.0,
                                           ALU.mult, ALU.add).then_inc(scanned, 1)
                dve.wait_ge(row_copied[C_], g + 1)
                dve.wait_ge(y_summed, g + 1)
                for m in range(NH2):
                    dve.wait_ge(scanned, 2 * g + 5 + m)
                    dve.tensor_tensor(prod[:, s, m, :], hs[:, m, :], bc[:, C_, s, :], ALU.mult).then_inc(multiplied, 1)

            for b in range(NB):
                if b:
                    step(b * NS, 0, 0, None)
                    add_output(b - 1)
                    step(b * NS + 1, 1, 1, None)
                steps(dve, b, step, first=2 if b else 0)
                dve.wait_ge(y_init, b + 1)
                dve.wait_ge(y_summed, 2 + (b + 1) * NS)
                for m in range(NH2):
                    z = silu_z[:, m, b * SEQ:(b + 1) * SEQ].rearrange("p (a t) -> p a t", a=2)
                    dve.tensor_tensor(z, ps[:, 2 * m:2 * m + 2, :], z, ALU.mult).then_inc(gated, 1)
            add_output(NB - 1)


N_HEAD, N_ACT, DH = 16, 4, 64
NT_B = SEQ // P


def route_heads(nc, core, T, A):
    h, ps = T["hT"], T["ps"]
    with ExitStack() as st:
        def sb(name, shape, dt=F32):
            return core.sb(st, "r_" + name, shape, dt)
        wr, br, bo = sb("wr", [P, N_HEAD]), sb("br", [NB, N_HEAD]), sb("bo", [P, 1])
        hsum, logit, nmax = sb("hsum", [P, NB]), sb("logit", [NB, N_HEAD]), sb("nmax", [NB, 1])
        top, dist, total = sb("top", [NB, 8]), sb("dist", [NB, N_HEAD]), sb("total", [NB, 3])
        val, idx = sb("val", [NB, 8]), sb("idx", [NB, 8], U32)
        ev, ez, gates = sb("ev", [NB, N_ACT]), sb("ez", [NB, 1]), sb("gates", [NB, N_ACT])
        loaded, step, act_step, pe_step, moved = (core.sem("r_" + x) for x in ("loaded", "dve", "act", "pe", "moved"))
        block = st.enter_context(nc.Block())

        @block.sync
        def _(sp):
            sp.dma_start(wr[:, :], A["wr"]).then_inc(loaded, 16)
            for b in range(NB):
                sp.dma_start(br[b:b + 1, :], A["br"]).then_inc(loaded, 16)
            sp.dma_start(bo[:, :], A["bo"]).then_inc(loaded, 16)
            sp.wait_ge(step, 9)
            for b in range(NB):
                sp.dma_start(T["head_index"][0:1, b * N_ACT:(b + 1) * N_ACT], idx[b:b + 1, 0:N_ACT]).then_inc(moved, 16)
            sp.wait_ge(moved, 32)

        @block.tensor
        def _(pe):
            pe.wait_ge(loaded, 64)
            pe.wait_ge(step, 2)
            pe.matmul(ps[0:NB, 0, 0:N_HEAD], hsum[:, :], wr[:, :], start=True, stop=True).then_inc(pe_step, 1)
            pe.wait_ge(step, 14)
            for b in range(NB):
                mm = pe.matmul(ps[:, 1, b * N_ACT:(b + 1) * N_ACT], T["ident"][0:NB, b:b + 1].broadcast_to([NB, P]),
                               gates[:, :], start=True, stop=True)
            mm.then_inc(pe_step, 1)

        @block.scalar
        def _(act):
            act.wait_ge(step, 5)
            act.activation(dist[:, :], logit[:, :], ACT.Exp, bias=nmax[:, :], accum_out=total[:, 0:1]).then_inc(act_step, 1)
            act.wait_ge(step, 10)
            act.activation(ev[:, :], val[:, 0:N_ACT], ACT.Exp, bias=nmax[:, :], accum_out=total[:, 1:2]).then_inc(act_step, 1)
            act.activation(ez[:, :], nmax[:, :], ACT.Exp).then_inc(act_step, 1)

        @block.vector
        def _(dve):
            for b in range(NB):
                dve.tensor_reduce(hsum[:, b:b + 1], h[:, b * SEQ:(b + 1) * SEQ], AX.X, ALU.add).then_inc(step, 1)
            dve.wait_ge(pe_step, 1)
            dve.scalar_tensor_tensor(out=logit[:, :], in0=ps[0:NB, 0, 0:N_HEAD], scalar=1.0 / SEQ, in1=br[:, :],
                                     op0=ALU.mult, op1=ALU.add).then_inc(step, 1)
            dve.wait_ge(step, 3)
            dve.max(top[:, :], logit[:, :]).then_inc(step, 1)
            dve.wait_ge(step, 4)
            dve.tensor_scalar(nmax[:, :], top[:, 0:1], -1.0, None, ALU.mult).then_inc(step, 1)
            dve.wait_ge(act_step, 1)
            dve.reciprocal(total[:, 2:3], total[:, 0:1]).then_inc(step, 1)
            dve.wait_ge(step, 6)
            dve.tensor_scalar(dist[:, :], dist[:, :], total[:, 2:3], None, ALU.mult).then_inc(step, 1)
            dve.wait_ge(step, 7)
            dve.max(val[:, :], dist[:, :]).then_inc(step, 1)
            dve.wait_ge(step, 8)
            dve.max_index(idx[:, :], val[:, :], dist[:, :]).then_inc(step, 1)
            dve.tensor_scalar(nmax[:, :], val[:, 0:1], -1.0, None, ALU.mult).then_inc(step, 1)
            dve.wait_ge(act_step, 3)
            dve.scalar_tensor_tensor(out=ez[:, :], in0=ez[:, :], scalar=float(N_HEAD - N_ACT), in1=total[:, 1:2],
                                     op0=ALU.mult, op1=ALU.add).then_inc(step, 1)
            dve.wait_ge(step, 11)
            dve.reciprocal(total[:, 2:3], ez[:, :]).then_inc(step, 1)
            dve.wait_ge(step, 12)
            dve.tensor_scalar(gates[:, :], ev[:, :], total[:, 2:3], None, ALU.mult).then_inc(step, 1)
            dve.tensor_tensor(T["gate_bo"][:, :], T["mod"][:, 0, 5, :], bo[:, 0:1].broadcast_to([P, NB]), ALU.mult)\
               .then_inc(step, 1)
            dve.wait_ge(pe_step, 2)
            dve.tensor_copy(T["gates"][:, :, :].rearrange("p b k -> p (b k)"), ps[:, 1, 0:NB * N_ACT]).then_inc(step, 1)


def chosen_heads(nc, core, T, A):
    x, h, ps = T["xT"], T["hT"], T["ps"]
    with ExitStack() as st:
        def sb(name, shape, dt=F32):
            return core.sb(st, "a_" + name, shape, dt)

        def sem(name):
            return core.sem("a_" + name)

        PAIRS, TP = N_ACT // 2, 2 * NT_B
        half = [slice(0, DH), slice(DH, 2 * DH)]
        w, bias, bv, wo = sb("w", [P, 3, P]), sb("bias", [P, 3]), sb("bv", [P, P]), sb("wo", [P, D])
        gk, gq, gkb = sb("gk", [P, 1]), sb("gq", [P, 1]), sb("gkb", [P, 1])
        bvg = sb("bvg", [P, P])
        qT, kT = sb("qT", [P, SEQ]), sb("kT", [P, SEQ])
        b_loaded, bv_gated = sem("b_loaded"), sem("bv_gated")
        v = sb("v", [P, NT_B, 2, DH + 1])
        prob = sb("prob", [P, 2, SEQ])
        probT = sb("probT", [P, 2, NT_B, P])
        nmax = sb("nmax", [P, 2])
        rsum = sb("rsum", [P, 2])
        o = sb("o", [P, NT_B, 2, DH])
        oT = sb("oT", [P, SEQ])
        w_loaded, wo_loaded = sem("w_loaded"), sem("wo_loaded")
        ones_set, small, q_proj, k_proj, v_proj = sem("ones_set"), sem("small"), sem("q_proj"), sem("k_proj"), sem("v_proj")
        q_ready, k_ready, v_ready, bo_added = sem("q"), sem("k"), sem("v"), sem("bo_added")
        scored, maxed, expd, turned = sem("scored"), sem("maxed"), sem("expd"), sem("turned")
        t_copied = [sem("t_dve"), sem("t_act")]
        weighed, inverted, normed = sem("weighed"), sem("inverted"), sem("normed")
        o_turned, o_copied, projected, x_added = sem("o_turned"), sem("o_copied"), sem("projected"), sem("x_added")
        block = st.enter_context(nc.Block())
        two = lambda ap: ap.rearrange("p (a t) -> p a t", a=2)


        @block.sync
        def _(sp):
            for b in range(NB):
                with sp.Fori(0, PAIRS) as i:
                    g = b * PAIRS + i
                    sp.wait_ge(v_proj, g + 1)
                    sp.wait_ge(q_ready, g + 1)
                    heads = [sp.value_load(T["head_index"][0:1, bass.ds(2 * g + j, 1)], min_val=0, max_val=N_HEAD - 1)
                             for j in range(2)]
                    for j, head in enumerate(heads):
                        sp.dma_start(w[:, :, half[j]], A["wqkv_h"][bass.ds(head, 1), :, :]
                                     .rearrange("o p (j d) -> (o p) j d", j=3)).then_inc(w_loaded, 16)
                    for j, head in enumerate(heads):
                        sp.dma_start(bias[half[j], :], A["bqkv_h"][bass.ds(head, 1), :, :].rearrange("o p n -> (o p) n"))\
                          .then_inc(b_loaded, 16)
                        sp.dma_start(bv[:, half[j]], A["bv_h"][bass.ds(head, 1), :].broadcast_to([P, DH])).then_inc(b_loaded, 16)
                    sp.wait_ge(projected, g + 1)
                    sp.dma_start(wo[:, :], A["wo_k"][bass.ds(2 * i, 2), :, :].rearrange("o p n -> (o p) n"))\
                      .then_inc(wo_loaded, 16)

        @block.gpsimd
        def _(pool):
            pool.memset(v[:, :, :, DH:DH + 1], 1.0).then_inc(ones_set, 1)

        @block.tensor
        def _(pe):
            pe.wait_ge(ones_set, 1)
            pe.sem_inc(v_proj, 1)
            pe.sem_inc(projected, 1)
            pe.sem_inc(turned, 4)
            pe.sem_inc(weighed, 2)
            for b in range(NB):
                with pe.Fori(0, PAIRS) as i:
                    g = b * PAIRS + i
                    pe.wait_ge(w_loaded, 32 * g + 32)
                    pe.wait_ge(expd, TP * g + 2)
                    for j, ready in ((0, q_proj), (1, k_proj)):
                        for c in range(2):
                            mm = pe.matmul(ps[:, 2 * j + c, :], w[:, j, :], h[:, chunk(2 * b + c)], start=True, stop=True)
                        mm.then_inc(ready, 1)
                    pe.wait_ge(o_copied, g + 1)
                    for t in range(NT_B):
                        at = ps[:, 4 + t // 4, (t % 4) * P:(t % 4 + 1) * P]
                        mm = pe.matmul(at, h[:, b * SEQ + t * P:b * SEQ + (t + 1) * P], w[:, 2, :], start=True, stop=True)
                    mm.then_inc(v_proj, 1)
                    pe.wait_ge(q_ready, g + 2)
                    pe.wait_ge(k_ready, g + 2)

                    def scores(n):
                        own, t = half[n // NT_B], n % NT_B
                        pe.wait_ge(expd, TP * g + n + 1)
                        for c in range(2):
                            mm = pe.matmul(ps[:, 2 * (n % 2) + c, :], qT[own, t * P:(t + 1) * P], kT[own, c * CH:(c + 1) * CH],
                                           start=True, stop=True)
                        mm.then_inc(scored, 1)

                    scores(0)
                    scores(1)
                    pe.wait_ge(v_ready, g + 1)
                    for n in range(TP):
                        pe.wait_ge(expd, TP * g + n + 3)
                        for side in range(2):
                            pe.wait_ge(t_copied[side], TP * g + n + 1)
                            for j in range(4):
                                mm = pe.transpose(ps[:, 4 + side, j * P:(j + 1) * P],
                                                  prob[:, n % 2, (4 * side + j) * P:(4 * side + j + 1) * P], T["ident"][:, :])
                            mm.then_inc(turned, 1)
                        if n + 2 < TP:
                            scores(n + 2)
                        pe.wait_ge(normed, TP * g + n + 1)
                        if n == 0:
                            pe.wait_ge(x_added, 2 * g + 2)
                        for j in range(NT_B):
                            if j % 4 == 0:
                                pe.wait_ge(t_copied[j // 4], TP * g + n + 2)
                            mm = pe.matmul(ps[:, 6 + n % 2, 0:DH + 1], probT[:, n % 2, j, :], v[:, j, n // NT_B, :],
                                           start=(j == 0), stop=(j == NT_B - 1))
                        mm.then_inc(weighed, 1)
                    pe.wait_ge(normed, TP * g + TP + 2)
                    for t in range(NT_B):
                        mm = pe.transpose(ps[:, 4 + t // 4, (t % 4) * P:(t % 4 + 1) * P],
                                          o[:, t, :, :].rearrange("p j d -> p (j d)"), T["ident"][:, :])
                    mm.then_inc(o_turned, 1)
                    pe.wait_ge(o_copied, g + 2)
                    pe.wait_ge(wo_loaded, 16 * g + 16)
                    for c in range(2):
                        mm = pe.matmul(ps[:, 6 + c, :], wo[:, :], oT[:, c * CH:(c + 1) * CH], start=True, stop=True)
                    mm.then_inc(projected, 1)

        @block.scalar
        def _(act):
            act.sem_inc(expd, 2)
            act.sem_inc(t_copied[1], 1)
            act.sem_inc(k_ready, 1)
            for b in range(NB):
                with act.Fori(0, PAIRS) as i:
                    g = b * PAIRS + i
                    act.wait_ge(k_proj, g + 1)
                    act.wait_ge(small, 6 * g + 6)
                    act.activation(two(kT[:, :]), ps[:, 2:4, :], ACT.Identity, bias=gkb[:, :], scale=gk[:, :]).then_inc(k_ready, 1)

                    def exps(n):
                        act.wait_ge(maxed, TP * g + n + 1)
                        act.wait_ge(turned, 2 * TP * g + 2 * n + 2)
                        act.activation(two(prob[:, n % 2, :]), ps[:, 2 * (n % 2):2 * (n % 2) + 2, :], ACT.Exp,
                                       bias=nmax[:, n % 2:n % 2 + 1]).then_inc(expd, 1)

                    exps(0)
                    exps(1)
                    for n in range(TP):
                        act.wait_ge(turned, 2 * TP * g + 2 * n + 6)
                        act.wait_ge(weighed, TP * g + n + 1)
                        act.activation(probT[:, n % 2, 4:8, :].rearrange("p j q -> p (j q)"), ps[:, 5, :], ACT.Copy)\
                           .then_inc(t_copied[1], 1)
                        if n + 2 < TP:
                            exps(n + 2)

        @block.vector
        def _(dve):
            dve.sem_inc(t_copied[0], 1)
            dve.sem_inc(q_ready, 1)
            dve.sem_inc(normed, 2)
            dve.sem_inc(o_copied, 1)
            dve.sem_inc(x_added, 2)
            for b in range(NB):
                xb = x[:, b * SEQ:(b + 1) * SEQ]
                dve.tensor_scalar(xb, xb, T["gate_bo"][:, b:b + 1], None, ALU.add).then_inc(bo_added, 1)
                with dve.Fori(0, PAIRS) as i:
                    g = b * PAIRS + i
                    dve.wait_ge(b_loaded, 64 * g + 64)
                    dve.wait_ge(k_ready, g + 1)
                    dve.wait_ge(x_added, 2 * g + 2)
                    gates = [T["gates"][:, b, bass.ds(2 * i + j, 1)] for j in range(2)]
                    for j, own in enumerate(half):
                        dve.tensor_scalar(bvg[:, own], bv[:, own], gates[j], None, ALU.mult).then_inc(bv_gated, 1)
                    for j, own in enumerate(half):
                        dve.tensor_copy(gk[own, :], gates[j][own, :]).then_inc(small, 1)
                        dve.tensor_scalar(gq[own, :], gates[j][own, :], DH ** -0.5, None, ALU.mult).then_inc(small, 1)
                        dve.tensor_scalar(gkb[own, :], bias[own, 1:2], gates[j][own, :], None, ALU.mult).then_inc(small, 1)
                    dve.wait_ge(small, 6 * g + 6)
                    dve.wait_ge(q_proj, g + 1)
                    dve.tensor_scalar(two(qT[:, :]), ps[:, 0:2, :], bias[:, 0:1], gq[:, :], ALU.add, ALU.mult)\
                       .then_inc(q_ready, 1)
                    dve.wait_ge(v_proj, g + 2)
                    dve.wait_ge(bv_gated, 2 * g + 2)
                    for j, own in enumerate(half):
                        ins = dve.scalar_tensor_tensor(
                            out=v[:, :, j, 0:DH], in0=ps[:, 4:6, :].rearrange("p a (t d) -> p (a t) d", d=P)[:, :, own],
                            scalar=gates[j], in1=bvg[:, own].unsqueeze(1).broadcast_to([P, NT_B, DH]), op0=ALU.mult, op1=ALU.add)
                    ins.then_inc(v_ready, 1)

                    def maxima(n):
                        dve.wait_ge(scored, TP * g + n + 1)
                        dve.wait_ge(expd, TP * g + n + 1)
                        dve.tensor_reduce(nmax[:, n % 2:n % 2 + 1], ps[:, 2 * (n % 2):2 * (n % 2) + 2, :], AX.XY, ALU.max,
                                          negate=True).then_inc(maxed, 1)

                    def normalise(n):
                        dve.wait_ge(weighed, TP * g + n + 3)
                        dve.reciprocal(rsum[:, n % 2:n % 2 + 1], ps[:, 6 + n % 2, DH:DH + 1]).then_inc(inverted, 1)
                        dve.wait_ge(inverted, TP * g + n + 1)
                        dve.tensor_scalar(o[:, n % NT_B, n // NT_B, :], ps[:, 6 + n % 2, 0:DH], rsum[:, n % 2:n % 2 + 1], None,
                                          ALU.mult).then_inc(normed, 1)

                    maxima(0)
                    maxima(1)
                    for n in range(TP):
                        dve.wait_ge(turned, 2 * TP * g + 2 * n + 5)
                        dve.wait_ge(weighed, TP * g + n + 1)
                        dve.tensor_copy(probT[:, n % 2, 0:4, :].rearrange("p j q -> p (j q)"), ps[:, 4, :])\
                           .then_inc(t_copied[0], 1)
                        if n + 2 < TP:
                            maxima(n + 2)
                        if n:
                            normalise(n - 1)
                    normalise(TP - 1)
                    dve.wait_ge(o_turned, g + 1)
                    dve.tensor_copy(two(oT[:, :]), ps[:, 4:6, :]).then_inc(o_copied, 1)
                    dve.wait_ge(projected, g + 2)
                    dve.wait_ge(bo_added, b + 1)
                    for c in range(2):
                        dve.wait_ge(x_added, 2 * g + 1 + c)
                        xc = x[:, chunk(2 * b + c)]
                        dve.scalar_tensor_tensor(out=xc, in0=ps[:, 6 + c, :], scalar=T["mod"][:, 0, 5, b:b + 1], in1=xc,
                                                 op0=ALU.mult, op1=ALU.add).then_inc(x_added, 1)


H1, HD = 16, 8
NG = NB * H1
WIN = 128
NREL = 2 * WIN + 1
NP3 = 3
STACK = NP3 * NP3 * HD
BIAS_ROWS = slice(STACK, STACK + NP3)
MAX_ROWS = slice(STACK + NP3, STACK + 2 * NP3)
KPOS, KALL = STACK + NP3, STACK + 2 * NP3
Q_, KL_, KR_ = range(3)
LEFT, RIGHT, ONES = range(3)
LOWEST = -3.0e38


def relative_parts(nc, core, T, A, dram, v, wstack):
    h, ps = T["hT"], T["ps"]
    with ExitStack() as st:
        def sb(name, shape, dt=F32):
            return core.sb(st, "p_" + name, shape, dt)

        def sem(name):
            return core.sem("p_" + name)

        w, cols = sb("w", [P, 3, D]), sb("cols", [P, 4])
        bv, table, brow = sb("bv", [1, D]), sb("table", [HD + 1, NREL]), sb("brow", [1, 2])
        edge = sb("edge", [HD + 1, 1])
        full, part = sb("full", [P, 3, TOK]), sb("part", [P, 3, NP3, TOK], BF16)
        scaled = sb("scaled", [P, TOK])
        tpart, bpart = sb("tpart", [HD + 1, NP3, NREL], BF16), sb("bpart", [1, NP3, 2], BF16)
        consts = sb("consts", [1, 3, NP3, SEQ], BF16)
        loaded, q_ready, k_ready, v_ready = sem("loaded"), sem("q"), sem("k"), sem("v")
        k_scaled, full_ready = sem("k_scaled"), sem("full")
        r1_late, w_loaded = sem("r1_late"), sem("w_loaded")
        p1, r1, p2, r2, p3 = sem("p1"), sem("r1"), sem("p2"), sem("r2"), sem("p3")
        tstep, ones_set, v_copied, stored, wst = sem("tstep"), sem("ones_set"), sem("v_copied"), sem("stored"), sem("wst")
        block = st.enter_context(nc.Block())

        @block.sync
        def _(sp):
            sp.dma_start(w[:, :, :], A["wqkv1"]).then_inc(w_loaded, 16)
            sp.dma_start(cols[:, :], A["cols1"]).then_inc(loaded, 16)
            sp.dma_start(bv[:, :], A["bv1"]).then_inc(loaded, 16)
            sp.dma_start(table[:, :], A["table"]).then_inc(loaded, 16)
            sp.dma_start(brow[:, :], A["brow"]).then_inc(loaded, 16)
            sp.dma_start(edge[:, :], A["table_edge"]).then_inc(loaded, 16)
            for k, ready in enumerate((p1, p2, p3)):
                for a in range(3):
                    sp.wait_ge(ready, a + 1)
                    sp.dma_start(dram["qk"][a, k].rearrange("b r t -> r b t"),
                                 part[:, a, k, :].rearrange("r (b t) -> r b t", b=NB)).then_inc(stored, 16)
            sp.wait_ge(stored, 16 * 9)

        @block.gpsimd
        def _(pool):
            pool.memset(consts[:, ONES, :, :], 1.0).then_inc(ones_set, 1)
            pool.wait_ge(tstep, 11)
            pool.dma_start(dram["table"].rearrange("k r n -> r k n"), tpart[:, :, :]).then_inc(wst, 16)
            for a in (Q_, KL_):
                pool.wait_ge(p1, a + 1)
                pool.tensor_tensor(full[:, a, :], full[:, a, :], part[:, a, 0, :], ALU.subtract).then_inc(r1, 1)
            pool.wait_ge(ones_set, 3)
            pool.dma_start(dram["const"].rearrange("c k t -> (c k t)"), consts[:, :, :, :].rearrange("o c k t -> o (c k t)"))\
                .then_inc(wst, 16)
            pool.wait_ge(wst, 32)
            for k in range(NP3):
                pool.dma_start(wstack[k * NP3 * HD:(k + 1) * NP3 * HD, :], dram["table"][:, 0:HD, :]).then_inc(wst, 16)
            pool.dma_start(wstack[BIAS_ROWS, :], dram["table"][:, HD:HD + 1, :]).then_inc(wst, 16)
            pool.wait_ge(wst, 16 * 6)

        @block.tensor
        def _(pe):
            pe.wait_ge(w_loaded, 16)
            for j, ready in ((0, q_ready), (1, k_ready)):
                for c in range(NCH):
                    mm = pe.matmul(ps[:, 4 * j + c, :], w[:, j, :], h[:, chunk(c)], start=True, stop=True)
                mm.then_inc(ready, 1)
            pe.wait_ge(full_ready, 1)
            pe.wait_ge(loaded, 80)
            for t in range(TOK // P):
                at = ps[:, t // 4, (t % 4) * P:(t % 4 + 1) * P]
                pe.matmul(at, h[:, t * P:(t + 1) * P], w[:, 2, :], start=True, stop=False)
                mm = pe.matmul(at, T["ones"][0:1, :], bv[:, :], start=False, stop=True)
            mm.then_inc(v_ready, 1)

        @block.scalar
        def _(act):
            act.wait_ge(tstep, 11)
            for c in range(2):
                act.activation(consts[:, c, :, :], bpart[:, :, c:c + 1].broadcast_to([1, NP3, SEQ]), ACT.Copy).then_inc(ones_set, 1)
            for a in range(3):
                act.wait_ge(full_ready, a + 1)
                act.activation(part[:, a, 0, :], full[:, a, :], ACT.Copy).then_inc(p1, 1)
            for a in range(3):
                act.wait_ge(*((r1, a + 1) if a < KR_ else (r1_late, 1)))
                act.activation(part[:, a, 1, :], full[:, a, :], ACT.Copy).then_inc(p2, 1)
            for a in range(3):
                act.wait_ge(r2, a + 1)
                act.activation(part[:, a, 2, :], full[:, a, :], ACT.Copy).then_inc(p3, 1)

        @block.vector
        def _(dve):
            banks = lambda ap: ap.rearrange("p (c t) -> p c t", t=CH)
            dve.wait_ge(loaded, 80)
            dve.tensor_scalar(table[:, :], table[:, :], edge[:, :], None, ALU.subtract).then_inc(tstep, 1)
            n = 1
            for src, parts in ((table, lambda k: tpart[:, k, :]), (brow, lambda k: bpart[:, k, :])):
                for k in range(NP3):
                    dve.wait_ge(tstep, n)
                    dve.tensor_copy(parts(k), src[:, :]).then_inc(tstep, 1)
                    n += 1
                    if k < NP3 - 1:
                        dve.wait_ge(tstep, n)
                        dve.tensor_tensor(src[:, :], src[:, :], parts(k), ALU.subtract).then_inc(tstep, 1)
                        n += 1
            dve.wait_ge(q_ready, 1)
            dve.tensor_scalar(banks(full[:, Q_, :]), ps[:, 0:4, :], cols[:, 0:1], None, ALU.add).then_inc(full_ready, 1)
            dve.wait_ge(k_ready, 1)
            dve.tensor_scalar(banks(scaled[:, :]), ps[:, 4:8, :], cols[:, 1:2], HD ** -0.5, ALU.add, ALU.mult)\
               .then_inc(k_scaled, 1)
            dve.wait_ge(k_scaled, 1)
            dve.tensor_scalar(full[:, KL_, :], scaled[:, :], cols[:, 2:3], None, ALU.add).then_inc(full_ready, 1)
            dve.tensor_scalar(full[:, KR_, :], scaled[:, :], cols[:, 3:4], None, ALU.add).then_inc(full_ready, 1)
            dve.wait_ge(p1, KR_ + 1)
            dve.tensor_tensor(full[:, KR_, :], full[:, KR_, :], part[:, KR_, 0, :], ALU.subtract).then_inc(r1_late, 1)
            for a in range(3):
                dve.wait_ge(p2, a + 1)
                dve.tensor_tensor(full[:, a, :], full[:, a, :], part[:, a, 1, :], ALU.subtract).then_inc(r2, 1)
            dve.wait_ge(v_ready, 1)
            for c in range(NCH):
                b, o = divmod(c, 2)
                dve.tensor_copy(v[:, 4 * o:4 * o + 4, b * H1:(b + 1) * H1, :],
                                ps[:, c, :].rearrange("p (t g d) -> p t g d", t=4, d=HD)).then_inc(v_copied, 1)


def relative_attention(nc, core, T, A, dram, v, wstack, oacc):
    ps = T["ps"]
    with ExitStack() as st:
        def sb(name, shape, dt=F32):
            return core.sb(st, "l_" + name, shape, dt)

        def sem(name):
            return core.sem("l_" + name)

        TURN_AT = 5
        NSL = 4
        stack = [sb(n, [KALL, NSL, SEQ], BF16) for n in ("qs", "kl", "kr")]
        qb = sb("qb", [KPOS, 2, SEQ], BF16)
        rel = sb("rel", [P, 2, NT_B, NREL])
        band = sb("band", [P, NSL, NT_B, 3 * P])
        probT = sb("probT", [P, 2, SEQ])
        seen = sb("seen", [P, 3, NT_B])
        nmax, nparts, nrow = sb("nmax", [P, NT_B]), sb("nparts", [P, NP3 * NT_B], BF16), sb("nrow", [NP3 * NT_B, P], BF16)
        junk, inv = sb("junk", [P, 3 * P]), sb("inv", [P, NT_B])
        VAT, VW = 32, 64
        vhead = sb("vhead", [P, 2, NT_B, VAT + VW])
        outT = sb("outT", [P, CH])
        inside = sb("inside", [P, P])
        inside_set = sem("inside")
        rows_set, qb_rows_set, lowest_set = sem("rows_set"), sem("qb_rows_set"), sem("lowest")
        stack_loaded = [sem(f"stack{s}") for s in range(NSL)]
        qb_loaded, band_loaded = [sem(f"qb{s}") for s in range(2)], [sem(f"band{s}") for s in range(2)]
        rel_ready, rel_copied, rel_stored, band_step, band_ready = (sem(x) for x in ("rel", "relc", "rels", "bstep", "bready"))
        s1_ready, maxed, dstep = sem("s1"), sem("maxed"), sem("dstep")
        n_turned, n_copied, n_loaded = sem("n_turned"), sem("n_copied"), sem("n_loaded")
        s2_ready, expd, weighed = sem("s2"), sem("expd"), sem("weighed")
        inverted, normed = sem("inverted"), sem("normed")
        v_placed, out_copied, o_turned = sem("v_placed"), sem("out_copied"), sem("o_turned")
        block = st.enter_context(nc.Block())

        def rel_bank(g, k):
            return 2 + k % 4 if isinstance(g, int) and g < 2 else 7

        def score_bank(g, t):
            return 2 * (t % 3) if isinstance(g, int) and g == 0 else 0

        def stages(eng, body):
            with eng.Fori(0, NG // 4 - 1) as i:
                for q in range(4):
                    body(4 * i + q, q, lambda k: True, lambda k, n: n * i + k // (4 // n))
            for q in range(4):
                g = NG - 4 + q
                body(g, q, lambda k: g + k < NG, lambda k, n: n * (NG // 4 - 1) + k // (4 // n))

        @block.sync
        def _(sp):
            def at(g):
                return g * HD if isinstance(g, int) else sp.snap(g * HD)

            def rows(a, first, k):
                own = slice(k, k + 1) if a == Q_ else slice(0, NP3)
                return dram["rows"][a][own, bass.ds(first, HD), :].broadcast_to([NP3, HD, SEQ])

            def load_rows(dst, s, a, first, sem):
                for k in range(NP3):
                    sp.dma_start(dst[k * NP3 * HD:(k + 1) * NP3 * HD, s, :], rows(a, first, k)).then_inc(sem, 16)

            def load_qb(first, s):
                load_rows(qb, s, Q_, first, qb_loaded[s])

            def load_stack(first, s):
                for a in range(3):
                    load_rows(stack[a], s, a, first, stack_loaded[s])

            def store_rel(g, s2, reads_before):
                sp.wait_ge(rel_copied, NT_B * g + NT_B + 1)
                if reads_before is not None:
                    sp.wait_ge(band_loaded[s2], reads_before)
                sp.dma_start(dram["rel"][s2].rearrange("t (p r) -> p t r", p=P), rel[:, s2, :, :]).then_inc(rel_stored, 16)

            def load_band(g, s2, s4):
                sp.wait_ge(rel_stored, 16 * g + 16)
                flat = dram["rel"][s2]
                sp.dma_start(band[:, s4, :, 0:2 * P], flat[:, 0:P * 2 * P].rearrange("t (p c) -> p t c", p=P))\
                  .then_inc(band_loaded[s2], 16)
                sp.dma_start(band[:, s4, :, 2 * P:3 * P], flat[:, P:P + P * 2 * P].rearrange("t (p c) -> p t c", p=P)[:, :, P:2 * P])\
                  .then_inc(band_loaded[s2], 16)

            def load_max(g, s4):
                sp.wait_ge(n_copied, g + 1)
                sp.dma_start(stack[Q_][MAX_ROWS, s4, :], nrow[:, :]).then_inc(n_loaded, 16)

            sp.dma_start(qb[BIAS_ROWS, :, :], dram["const"][ONES].unsqueeze(1).broadcast_to([NP3, 2, SEQ])).then_inc(qb_rows_set, 16)
            load_qb(at(0), 0)
            load_qb(at(1), 1)
            store_rel(0, 0, None)
            for a in range(3):
                const = dram["const"][(ONES, LEFT, RIGHT)[a]]
                sp.dma_start(stack[a][BIAS_ROWS, :, :], const.unsqueeze(1).broadcast_to([NP3, NSL, SEQ])).then_inc(rows_set, 16)
                if a != Q_:
                    sp.dma_start(stack[a][MAX_ROWS, :, :], dram["const"][ONES].unsqueeze(1).broadcast_to([NP3, NSL, SEQ]))\
                      .then_inc(rows_set, 16)
            load_band(0, 0, 0)
            load_stack(at(0), 0)
            load_qb(at(2), 0)
            store_rel(1, 1, None)
            load_band(1, 1, 1)
            load_stack(at(1), 1)
            load_max(0, 0)
            load_qb(at(3), 1)
            load_stack(at(2), 2)

            def body(g, q, live, per):
                if live(3):
                    first = at(g + 3)
                    sp.wait_ge(s2_ready, NT_B * g + 4 * NT_B)
                    load_stack(first, (q + 3) % NSL)
                if live(4):
                    first = at(g + 4)
                    sp.wait_ge(rel_ready, NT_B * (g + 3))
                    load_qb(first, q % 2)
                if live(2):
                    store_rel(g + 2, q % 2, 32 * per(q + 2, 2))
                    load_band(g + 2, q % 2, (q + 2) % NSL)
                if live(1):
                    load_max(g + 1, (q + 1) % NSL)

            stages(sp, body)

        @block.gpsimd
        def _(pool):
            for kind, tiles in ((1, slice(0, 2)), (2, slice(NT_B - 2, NT_B))):
                pool.memset(seen[:, kind, tiles], LOWEST).then_inc(lowest_set, 1)
            pool.memset(inside[:, :], 1.0).then_inc(inside_set, 1)
            pool.wait_ge(inside_set, 1)
            pool.affine_select(out=inside[:, :], in_=inside[:, :], compare_op=ALU.is_ge, fill=0.0, base=0,
                               pattern=[[-1, P]], channel_multiplier=1).then_inc(inside_set, 1)
            pool.wait_ge(inside_set, 2)
            pool.sem_inc(band_ready, 2)
            pool.memset(vhead[:, :, :, :], 0.0).then_inc(inside_set, 1)
            pool.wait_ge(inside_set, 3)
            pool.memset(outT[:, :], 0.0).then_inc(inside_set, 1)
            pool.wait_ge(inside_set, 4)
            pool.memset(vhead[:, :, :, VAT + HD:VAT + HD + 1], 1.0).then_inc(inside_set, 1)
            pool.wait_ge(inside_set, 5)

            def place_v(g, s2):
                if not isinstance(g, int) or g:
                    pool.wait_ge(weighed, NT_B * g - NT_B + 2)
                pool.tensor_copy(vhead[:, s2, :, VAT:VAT + HD].unsqueeze(2), v[:, :, bass.ds(g, 1), :]).then_inc(v_placed, 1)

            def trim(g, s2, s4, reads):
                last, first = band[:, s4, :, 2 * P:3 * P], band[:, s4, :, 0:P]
                pool.wait_ge(band_loaded[s2], reads)
                pool.tensor_tensor(last, last, rel[:, s2, :, NREL - 1:NREL].broadcast_to([P, NT_B, P]), ALU.subtract)\
                    .then_inc(band_step, 1)
                pool.affine_select(out=first, in_=first, compare_op=ALU.is_ge, fill=0.0, base=0,
                                   pattern=[[0, NT_B], [1, P]], channel_multiplier=-1).then_inc(band_step, 1)
                pool.wait_ge(band_step, 2 * g + 1)
                pool.tensor_tensor(last, last, inside[:, :].unsqueeze(1).broadcast_to([P, NT_B, P]), ALU.mult)\
                    .then_inc(band_ready, 1)

            place_v(0, 0)
            for g in range(2):
                trim(g, g, g, 32)

            def body(g, q, live, per):
                if live(1):
                    place_v(g + 1, (q + 1) % 2)
                if live(2):
                    trim(g + 2, q % 2, (q + 2) % NSL, 32 * per(q + 2, 2) + 32)

            stages(pool, body)

        @block.tensor
        def _(pe):
            ident = T["ident"]

            def relative(g, k, s2, loads):
                if k == 0:
                    pe.wait_ge(qb_loaded[s2], loads)
                if k == TURN_AT and not (isinstance(g, int) and g < 3):
                    pe.wait_ge(n_copied, g - 1)
                n = NT_B * g + k
                if not isinstance(g, int) or g >= 2:
                    pe.wait_ge(rel_copied, n + 1)
                elif n >= 4:
                    pe.wait_ge(rel_copied, n - 2)
                pe.matmul(ps[:, rel_bank(g, k), 0:NREL], qb[0:KPOS, s2, k * P:(k + 1) * P], wstack[0:KPOS, :], start=True, stop=True)\
                  .then_inc(rel_ready, 1)

            def first_scores(g, t, s4, loads):
                if t == 0:
                    pe.wait_ge(stack_loaded[s4], loads)
                if not isinstance(g, int) or g:
                    pe.wait_ge(maxed, NT_B * g + t + 1)
                elif t >= 3:
                    pe.wait_ge(maxed, t - 1)
                bank = score_bank(g, t)
                edge = (t + 1) * P
                for c in range(2):
                    lo, hi = c * CH, (c + 1) * CH
                    cut = min(max(edge, lo), hi)
                    first = True
                    for a, x0, x1 in ((KL_, lo, cut), (KR_, cut, hi)):
                        if x1 > x0:
                            mm = pe.matmul(ps[:, bank + c, x0 - lo:x1 - lo], stack[Q_][0:KPOS, s4, t * P:(t + 1) * P],
                                           stack[a][0:KPOS, s4, x0:x1], start=first, stop=False, skip_group_check=True)
                            first = False
                mm.then_inc(s1_ready, 1)

            def turn_max(g, relatives):
                pe.wait_ge(dstep, 6 * g + 6)
                pe.wait_ge(rel_copied, relatives + 1)
                pe.transpose(ps[0:NP3 * NT_B, 7, 0:P // 2].bitcast(BF16), nparts[:, :], T["ident_bf"][:, :])\
                  .then_inc(n_turned, 1)

            def second_scores(g, t, s4):
                if t == 0:
                    pe.wait_ge(n_loaded, 16 * g + 16)
                pe.wait_ge(expd, NT_B * g + t + 1)
                bank = 2 + 2 * (t % 2)
                for c in range(2):
                    lo, hi = c * CH, (c + 1) * CH
                    cut = min(max(t * P, lo), hi)
                    first = True
                    for a, x0, x1 in ((KR_, lo, cut), (KL_, cut, hi)):
                        if x1 > x0:
                            pe.matmul(ps[:, bank + c, x0 - lo:x1 - lo], stack[a][0:KALL, s4, t * P:(t + 1) * P],
                                      stack[Q_][0:KALL, s4, x0:x1], start=first, stop=False, skip_group_check=True)
                            first = False
                for i in range(max(t - 1, 0), min(t + 2, NT_B)):
                    blk = t - i + 1
                    mm = pe.matmul(ps[:, bank + i // 4, (i % 4) * P:(i % 4 + 1) * P], band[:, s4, i, blk * P:(blk + 1) * P],
                                   ident[:, :], start=False, stop=False, skip_group_check=True)
                mm.then_inc(s2_ready, 1)

            def weigh(g, t, s2):
                pe.wait_ge(expd, NT_B * g + t + 3)
                if t == 0:
                    pe.wait_ge(v_placed, g + 1)
                    pe.wait_ge(normed, g + 1)
                for c in range(2):
                    at = VAT - c * VAT
                    mm = pe.matmul(ps[0:VW, 6, :], vhead[:, s2, t, at:at + VW], probT[:, t % 2, c * CH:(c + 1) * CH],
                                   start=(t == 0 and c == 0), stop=False, skip_group_check=True)
                mm.then_inc(weighed, 1)

            def turn_out(g):
                pe.wait_ge(out_copied, g + 1)
                for j in range(CH // P):
                    mm = pe.transpose(ps[:, 6, j * P:(j + 1) * P], outT[:, j * P:(j + 1) * P], ident[:, :])
                mm.then_inc(o_turned, 1)

            pe.sem_inc(weighed, 2)
            pe.sem_inc(s2_ready, 4 * NT_B)
            pe.wait_ge(qb_rows_set, 16)
            for g in range(2):
                for k in range(NT_B):
                    relative(g, k, g, 16 * NP3)
            pe.wait_ge(rows_set, 80)
            pe.wait_ge(rel_copied, 2 * NT_B + 1)
            for t in range(NT_B):
                first_scores(0, t, 0, 9 * 16)
                for k in range(2 * t - NT_B, 2 * t - NT_B + 2):
                    if k >= 0:
                        relative(2, k, 0, 2 * 16 * NP3)
            turn_max(0, 3 * NT_B)
            pe.wait_ge(n_copied, 1)
            second_scores(0, 0, 0)

            FIRST_AT = {0: (0, 1), 1: (None, 2), 2: (3, 4), 3: (None, 5), 4: (6, 7)}

            def body(g, q, live, per):
                s4n = (q + 1) % NSL

                def next_relative(k):
                    if live(3):
                        relative(g + 3, k, (q + 3) % 2, 16 * NP3 * (per(q + 3, 2) + 1))

                for t in range(NT_B):
                    if t < NT_B - 1:
                        second_scores(g, t + 1, q)
                    if t == TURN_AT + 1:
                        next_relative(TURN_AT)
                    early, late = FIRST_AT.get(t, (None, None)) if live(1) else (None, None)
                    if early is not None:
                        next_relative(t)
                        first_scores(g + 1, early, s4n, 9 * 16 * (per(q + 1, 1) + 1))
                    weigh(g, t, q % 2)
                    if late is not None:
                        first_scores(g + 1, late, s4n, 9 * 16 * (per(q + 1, 1) + 1))
                    if t != TURN_AT:
                        if early is None:
                            next_relative(t)
                    elif live(1):
                        turn_max(g + 1, NT_B * (g + 3) + TURN_AT if live(3) else NT_B * NG)
                if live(1):
                    second_scores(g + 1, 0, s4n)
                turn_out(g)

            stages(pe, body)

        @block.scalar
        def _(act):
            act.sem_inc(rel_copied, 1)
            act.sem_inc(expd, 2)

            def copy_rel(g, k, s2):
                act.wait_ge(rel_ready, NT_B * g + k + 1)
                if k == 0:
                    act.wait_ge(band_ready, g + 1)
                act.activation(rel[:, s2, k, :], ps[:, rel_bank(g, k), 0:NREL], ACT.Copy).then_inc(rel_copied, 1)

            def copy_max(g):
                act.wait_ge(n_turned, g + 1)
                if not (isinstance(g, int) and g == 0):
                    act.wait_ge(n_loaded, 16 * g)
                act.activation(nrow[:, :], ps[0:NP3 * NT_B, 7, 0:P // 2].bitcast(BF16), ACT.Copy).then_inc(n_copied, 1)

            for g in range(2):
                for k in range(NT_B):
                    copy_rel(g, k, g)
            for k in range(NT_B):
                copy_rel(2, k, 0)
            copy_max(0)

            def exponentials(g, t):
                act.wait_ge(s2_ready, NT_B * (g + 4) + t + 1)
                act.wait_ge(weighed, NT_B * g + t + 1)
                bank = 2 + 2 * (t % 2)
                act.activation(probT[:, t % 2, :].rearrange("p (c t) -> p c t", t=CH), ps[:, bank:bank + 2, :], ACT.Exp)\
                   .then_inc(expd, 1)

            exponentials(0, 0)

            def body(g, q, live, per):
                for t in range(NT_B):
                    if t < NT_B - 1:
                        exponentials(g, t + 1)
                    if live(1) and t == TURN_AT:
                        copy_max(g + 1)
                    if live(3) and t != TURN_AT:
                        for k in ((TURN_AT, t) if t == TURN_AT + 1 else (t,)):
                            copy_rel(g + 3, k, (q + 3) % 2)
                act.wait_ge(weighed, NT_B * g + NT_B + 2)
                act.activation(outT[0:VW, :], ps[0:VW, 6, :], ACT.Copy).then_inc(out_copied, 1)
                if live(1):
                    exponentials(g + 1, 0)

            stages(act, body)

        @block.vector
        def _(dve):
            dve.wait_ge(lowest_set, 2)
            dve.sem_inc(maxed, 1)
            dve.sem_inc(normed, 1)

            def maxima(g, t, s4):
                if t == 0:
                    dve.wait_ge(band_ready, g + 3)
                dve.wait_ge(s1_ready, NT_B * g + t + 1)
                bank = score_bank(g, t)
                s1 = ps[:, bank:bank + 2, :].rearrange("p c t -> p (c t)")
                lo, hi = max(t - 1, 0) * P, min(t + 2, NT_B) * P
                if lo:
                    dve.tensor_reduce(seen[:, 1, t:t + 1], s1[:, 0:lo], AX.X, ALU.max)
                if hi < SEQ:
                    dve.tensor_reduce(seen[:, 2, t:t + 1], s1[:, hi:SEQ], AX.X, ALU.max)
                off = lo - (t - 1) * P
                if isinstance(g, int) and g == 0:
                    dve.wait_ge(maxed, t + 1)
                dve.tensor_tensor_reduce(junk[:, 0:hi - lo], s1[:, lo:hi], band[:, s4, t, off:off + hi - lo], 1.0, LOWEST,
                                         ALU.add, ALU.max, seen[:, 0, t:t + 1]).then_inc(maxed, 1)

            def split_max(g):
                n = 6 * g
                dve.wait_ge(maxed, NT_B * g + NT_B + 1)
                if not (isinstance(g, int) and g == 0):
                    dve.wait_ge(n_turned, g)
                dve.tensor_reduce(nmax[:, :], seen[:, :, :].rearrange("p k t -> p t k"), AX.X, ALU.max, negate=True)\
                   .then_inc(dstep, 1)
                for k in range(NP3):
                    p = nparts[:, k * NT_B:(k + 1) * NT_B]
                    dve.wait_ge(dstep, n + 2 * k + 1)
                    dve.tensor_copy(p, nmax[:, :]).then_inc(dstep, 1)
                    if k < NP3 - 1:
                        dve.wait_ge(dstep, n + 2 * k + 2)
                        dve.tensor_tensor(nmax[:, :], nmax[:, :], p, ALU.subtract).then_inc(dstep, 1)

            def normalise(g):
                sums = ps[:, 6, :].rearrange("p (j c x) -> p c j x", j=CH // P, x=VAT)[:, 0:2, :, :]
                dve.wait_ge(o_turned, g + 1)
                dve.reciprocal(inv[:, :].rearrange("p (c j) -> p c j", c=2).unsqueeze(3), sums[:, :, :, HD:HD + 1]).then_inc(inverted, 1)
                dve.wait_ge(inverted, g + 1)
                for c in range(2):
                    half = slice(c * (CH // P), (c + 1) * (CH // P))
                    ins = dve.tensor_tensor(oacc[:, half, bass.ds(g, 1), :].rearrange("p t o d -> p t (o d)"),
                                            sums[:, c, :, 0:HD], inv[:, half].unsqueeze(2).broadcast_to([P, CH // P, HD]), ALU.mult)
                ins.then_inc(normed, 1)

            for t in range(NT_B):
                maxima(0, t, 0)
            split_max(0)

            def body(g, q, live, per):
                if live(1):
                    for t in range(NT_B):
                        maxima(g + 1, t, (q + 1) % NSL)
                    split_max(g + 1)
                normalise(g)

            stages(dve, body)


def add_heads(nc, core, T, oacc):
    x, ps = T["xT"], T["ps"]
    with ExitStack() as st:
        turned, added = core.sem("h_turned"), core.sem("h_added")
        block = st.enter_context(nc.Block())

        @block.tensor
        def _(pe):
            for c in range(NCH):
                b, o = divmod(c, 2)
                for j in range(4):
                    mm = pe.transpose(ps[:, c, j * P:(j + 1) * P],
                                      oacc[:, 4 * o + j, b * H1:(b + 1) * H1, :].rearrange("p g d -> p (g d)"), T["ident"][:, :])
                mm.then_inc(turned, 1)

        @block.vector
        def _(dve):
            for c in range(NCH):
                b = c * CH // SEQ
                dve.wait_ge(turned, c + 1)
                dve.scalar_tensor_tensor(out=x[:, chunk(c)], in0=ps[:, c, :], scalar=T["mod"][:, 1, 2, b:b + 1],
                                         in1=x[:, chunk(c)], op0=ALU.mult, op1=ALU.add).then_inc(added, 1)


def second_attention(nc, core, T, A, dram):
    with ExitStack() as st:
        v = core.sb(st, "v1", [P, NT_B, NG, HD])
        wstack = core.sb(st, "wstack", [KPOS, NREL], BF16)
        oacc = core.sb(st, "oacc", [P, NT_B, NG, HD])
        relative_parts(nc, core, T, A, dram, v, wstack)
        relative_attention(nc, core, T, A, dram, v, wstack, oacc)
        add_heads(nc, core, T, oacc)


NE, HID = 8, 512
HF = HID // P
NT = TOK // P
ST = NT + NE - 1
BIASES = 2 * HID + D


def experts(nc, core, T, A, dram, out):
    x, h, ps = T["xT"], T["hT"], T["ps"]
    with ExitStack() as st:
        def sb(name, shape, dt=F32):
            return core.sb(st, "e_" + name, shape, dt)

        def sem(name):
            return core.sem("e_" + name)

        w1, w2 = sb("w1", [P, NE, 2 * HID]), sb("w2", [P, NE, HF, D])
        bias, bpart = sb("bias", [NE, BIASES]), sb("bpart", [NE, NP3, BIASES], BF16)
        brows = sb("brows", [NP3, NE, BIASES], BF16)
        rw, rb = sb("rw", [P, NE]), sb("rb", [P, NE])
        logit, top, mask = sb("logit", [P, NT, NE]), sb("top", [P, NT]), sb("mask", [P, NT, NE], BF16)
        count = sb("count", [P, ST])
        before = sb("before", [P, P])
        before_bf = sb("before_bf", [P, P], BF16)
        rank = sb("rank", [P, NT + 1, NE])
        full, tiles, ends = sb("full", [P, NE, NT]), sb("tiles", [P, NE]), sb("ends", [P, NE])
        slot, index = sb("slot", [P, NT]), sb("index", [P, NT], U32)
        passed, owner = sb("passed", [1, ST, NE]), sb("owner", [1, ST])
        expert_of = sb("expert_of", [1, ST + 1], U32)
        ht, zero = sb("ht", [P, NT, D]), sb("zero", [P, D])
        hrow, hx = sb("hrow", [P, 2, D]), sb("hx", [P, 2, P])
        sig, hid, hidT = sb("sig", [P, 2, HID]), sb("hid", [P, 2, HID]), sb("hidT", [P, 2, HF, P])
        y, yt = sb("y", [P, ST, D]), sb("yt", [P, NT, D])
        rw_loaded, rb_loaded, w_loaded, b_loaded, b_split, b_moved = (sem(n) for n in ("rw", "rb", "w", "b", "bsplit", "bmoved"))
        constants, routed, step, ranked, h_turned, ht_ready = (sem(n) for n in ("const", "routed", "step", "ranked", "hturned", "ht"))
        cleared, scattered, row_loaded = sem("cleared"), sem("scattered"), [sem("row0"), sem("row1")]
        t_ready, hx_ready, g_ready, a_ready, sig_ready = (sem(n) for n in ("t", "hx", "g", "a", "sig"))
        hid_ready, hidT_turned, hidT_ready, y_ready, y_copied = (sem(n) for n in ("hid", "hidTt", "hidT", "y", "ycopied"))
        y_stored, gathered = sem("y_stored"), [sem(f"gathered{c}") for c in range(NCH)]
        turned, x_ready, stored = sem("turned"), sem("x"), sem("stored")
        block = st.enter_context(nc.Block())

        def slot_tiles(eng, body):
            with eng.Fori(0, (ST - 3) // 2) as i:
                for u in range(2):
                    body(2 * i + u, u, i, lambda k: True)
            for j in range(ST - 3, ST):
                body(j, j % 2, j // 2, lambda k: j + k < ST)

        @block.sync
        def _(sp):
            sp.dma_start(rw[:, :], A["router_w"]).then_inc(rw_loaded, 16)
            sp.dma_start(rb[:, :], A["router_b"].broadcast_to([P, NE])).then_inc(rb_loaded, 16)
            sp.dma_start(bias[:, :], A["biases"]).then_inc(b_loaded, 16)
            sp.wait_ge(constants, 2)
            sp.dma_start(dram["h_sorted"].rearrange("(t p) d -> p t d", p=P), zero[:, :].unsqueeze(1).broadcast_to([P, ST, D]))\
              .then_inc(cleared, 16)
            for e in range(NE):
                sp.dma_start(w1[:, e, :], A["w1"][e]).then_inc(w_loaded, 16)
                sp.dma_start(w2[:, e, :, :], A["w2"][e].rearrange("(k p) d -> p k d", p=P)).then_inc(w_loaded, 16)
            sp.wait_ge(b_split, 2 * NP3 - 1)
            for k in range(NP3):
                sp.dma_start(brows[k:k + 1, :, :], bpart[:, k, :]).then_inc(b_moved, 16)
            sp.wait_ge(scattered, 16 * NT)

            def load(j, s, i, live):
                sp.wait_ge(t_ready, j + 1)
                sp.dma_start(hrow[:, s, :], dram["h_sorted"][bass.ds(j * P, P), :]).then_inc(row_loaded[s], 16)

            slot_tiles(sp, load)
            for c in range(NCH):
                sp.wait_ge(x_ready, c + 1)
                sp.dma_start(out[:, chunk(c)], x[:, chunk(c)]).then_inc(stored, 16)
            sp.wait_ge(stored, 16 * NCH)

        @block.gpsimd
        def _(pool):
            pool.memset(before[:, :], 1.0).then_inc(constants, 1)
            pool.wait_ge(constants, 1)
            pool.memset(zero[:, :], 0.0).then_inc(constants, 1)
            pool.wait_ge(constants, 2)
            pool.affine_select(out=before[:, :], in_=before[:, :], compare_op=ALU.is_ge, fill=0.0, base=-1,
                               pattern=[[1, P]], channel_multiplier=-1).then_inc(constants, 1)
            pool.wait_ge(constants, 3)
            pool.tensor_copy(before_bf[:, :], before[:, :]).then_inc(constants, 1)
            for k in range(ST):
                pool.memset(count[:, k:k + 1], float(k)).then_inc(constants, 1)
            pool.wait_ge(cleared, 16)
            pool.wait_ge(step, 15)
            for t in range(NT):
                if t % 4 == 0:
                    pool.wait_ge(ht_ready, t // 4 + 1)
                pool.indirect_dma_start(out=dram["h_sorted"], out_offset=bass.IndirectOffsetOnAxis(ap=index[:, t:t + 1], axis=0),
                                        in_=ht[:, t, :], in_offset=None).then_inc(scattered, 16)
            part = 6
            for first in range(0, ST, part):
                last = min(first + part, ST)
                pool.wait_ge(y_copied, last + 1)
                pool.dma_start(dram["y_sorted"][first * P:last * P, :].rearrange("(t p) d -> p t d", p=P), y[:, first:last, :])\
                    .then_inc(y_stored, 16)
            pool.wait_ge(y_stored, 16 * -(-ST // part))
            for t in range(NT):
                pool.indirect_dma_start(out=yt[:, t, :], out_offset=None, in_=dram["y_sorted"],
                                        in_offset=bass.IndirectOffsetOnAxis(ap=index[:, t:t + 1], axis=0))\
                    .then_inc(gathered[t // 4], 16)

        @block.tensor
        def _(pe):
            ident = T["ident"]
            pe.wait_ge(rw_loaded, 16)
            for t in range(NT):
                mm = pe.matmul(ps[:, 0, t * NE:(t + 1) * NE], h[:, t * P:(t + 1) * P], rw[:, :], start=True, stop=True)
            mm.then_inc(routed, 1)

            def turn_h(c):
                for j in range(4):
                    t = 4 * c + j
                    mm = pe.transpose(ps[:, 4 + c, j * P:(j + 1) * P], h[:, t * P:(t + 1) * P], ident[:, :])
                mm.then_inc(h_turned, 1)

            for c in range(NCH // 2):
                turn_h(c)
            pe.wait_ge(constants, 4)
            pe.wait_ge(step, 6)
            pe.matmul(ps[:, 1, 0:NT * NE], before_bf[:, :], mask[:, :, :].rearrange("p t e -> p (t e)"), start=True, stop=False,
                      skip_group_check=True)
            for t in range(NT):
                mm = pe.matmul(ps[:, 1, (t + 1) * NE:(NT + 1) * NE].rearrange("p (t e) -> p t e", e=NE), T["ones_bf"][:, :],
                               mask[:, t:t + 1, :].broadcast_to([P, NT - t, NE]), start=False, stop=False, skip_group_check=True)
            mm.then_inc(ranked, 1)
            for c in range(NCH // 2, NCH):
                turn_h(c)
            pe.sem_inc(t_ready, 2)
            pe.wait_ge(step, 18)
            pe.wait_ge(w_loaded, 32 * NE)
            pe.wait_ge(b_moved, 16 * NP3)

            def turn(s, turns):
                pe.wait_ge(row_loaded[s], 16 * turns)
                pe.transpose(ps[:, 6, 0:P], hrow[:, s, :], ident[:, :]).then_inc(t_ready, 1)

            def expert(j):
                return pe.value_load(expert_of[0:1, bass.ds(j, 1)], min_val=0, max_val=NE - 1)

            def hidden(half, s, e, ready):
                cols = slice(half * HID, (half + 1) * HID)
                bank = ps[:, 2 * half + s, :]
                pe.matmul(bank, hx[:, s, :], w1[:, bass.ds(e, 1), cols].rearrange("p o n -> p (o n)"), start=True, stop=False)
                pe.matmul(bank, T["ones_bf"][0:NP3, :], brows[:, bass.ds(e, 1), cols].rearrange("p o n -> p (o n)"),
                          start=False, stop=True).then_inc(ready, 1)

            turn(0, 1)
            pe.wait_ge(hx_ready, 1)
            turn(1, 1)
            e = expert(0)
            hidden(1, 0, e, g_ready)
            hidden(0, 0, e, a_ready)

            def tile(j, s, i, live):
                if live(1):
                    e = expert(j + 1)
                    pe.wait_ge(hx_ready, j + 2)
                    pe.wait_ge(sig_ready, j + 1)
                    hidden(1, 1 - s, e, g_ready)
                pe.wait_ge(hidT_ready, j + 1)
                pe.wait_ge(hid_ready, j + 3)
                for f in range(HF):
                    mm = pe.transpose(ps[:, 4, f * P:(f + 1) * P], hid[:, s, f * P:(f + 1) * P], ident[:, :])
                mm.then_inc(hidT_turned, 1)
                if live(1):
                    hidden(0, 1 - s, e, a_ready)
                own = expert(j)
                pe.wait_ge(y_copied, j + 1)
                pe.wait_ge(hidT_ready, j + 2)
                for f in range(HF):
                    pe.matmul(ps[:, 5, 0:D], hidT[:, s, f, :], w2[:, bass.ds(own, 1), f, :].rearrange("p o n -> p (o n)"),
                              start=(f == 0), stop=False)
                pe.matmul(ps[:, 5, 0:D], T["ones_bf"][0:NP3, :],
                          brows[:, bass.ds(own, 1), 2 * HID:BIASES].rearrange("p o n -> p (o n)"),
                          start=False, stop=True).then_inc(y_ready, 1)
                if live(2):
                    turn(s, i + 2)

            slot_tiles(pe, tile)
            for c in range(NCH):
                pe.wait_ge(gathered[c], 64)
                if c == 0:
                    pe.wait_ge(y_copied, ST + 1)
                for j in range(4):
                    mm = pe.transpose(ps[:, c, j * P:(j + 1) * P], yt[:, 4 * c + j, :], ident[:, :])
                mm.then_inc(turned, 1)

        @block.scalar
        def _(act):
            act.sem_inc(sig_ready, 1)
            act.sem_inc(y_copied, 1)
            for c in range(NCH):
                act.wait_ge(h_turned, c + 1)
                act.activation(ht[:, 4 * c:4 * c + 4, :].rearrange("p t d -> p (t d)"), ps[:, 4 + c, :], ACT.Copy)\
                   .then_inc(ht_ready, 1)

            def copy_hx(s, turned):
                act.wait_ge(t_ready, turned)
                act.activation(hx[:, s, :], ps[:, 6, 0:P], ACT.Copy).then_inc(hx_ready, 1)

            def sigmoid(s, ready, used):
                act.wait_ge(g_ready, ready)
                act.wait_ge(hid_ready, used)
                act.activation(sig[:, s, :], ps[:, 2 + s, :], ACT.Sigmoid).then_inc(sig_ready, 1)

            copy_hx(0, 3)
            copy_hx(1, 4)
            sigmoid(0, 1, 1)

            def tile(j, s, i, live):
                if live(1):
                    sigmoid(1 - s, j + 2, j + 2)
                act.wait_ge(y_ready, j + 1)
                act.activation(y[:, bass.ds(j, 1), :].rearrange("p o d -> p (o d)"), ps[:, 5, 0:D], ACT.Copy).then_inc(y_copied, 1)
                if live(2):
                    copy_hx(s, j + 5)

            slot_tiles(act, tile)

        @block.vector
        def _(dve):
            dve.sem_inc(hid_ready, 2)
            dve.sem_inc(hidT_ready, 1)
            dve.wait_ge(b_loaded, 16)
            for k in range(NP3):
                if k:
                    dve.wait_ge(b_split, 2 * k)
                dve.tensor_copy(bpart[:, k, :], bias[:, :]).then_inc(b_split, 1)
                if k < NP3 - 1:
                    dve.wait_ge(b_split, 2 * k + 1)
                    dve.tensor_tensor(bias[:, :], bias[:, :], bpart[:, k, :], ALU.subtract).then_inc(b_split, 1)
            spread = lambda ap: ap.broadcast_to([P, NT, NE])
            dve.wait_ge(routed, 1)
            dve.wait_ge(rb_loaded, 16)
            dve.tensor_tensor(logit[:, :, :], ps[:, 0, 0:NT * NE].rearrange("p (t e) -> p t e", e=NE),
                              spread(rb[:, :].unsqueeze(1)), ALU.add).then_inc(step, 1)
            dve.wait_ge(step, 1)
            dve.tensor_reduce(top[:, :], logit[:, :, :], AX.X, ALU.max).then_inc(step, 1)
            dve.wait_ge(step, 2)
            dve.wait_ge(constants, 4 + ST)
            dve.tensor_tensor(logit[:, :, :], logit[:, :, :], spread(top[:, :].unsqueeze(2)), ALU.is_lt).then_inc(step, 1)
            dve.wait_ge(step, 3)
            dve.scalar_tensor_tensor(out=logit[:, :, :], in0=logit[:, :, :], scalar=float(NE),
                                     in1=spread(count[:, 0:NE].unsqueeze(1)), op0=ALU.mult, op1=ALU.add).then_inc(step, 1)
            dve.wait_ge(step, 4)
            dve.tensor_reduce(top[:, :], logit[:, :, :], AX.X, ALU.min).then_inc(step, 1)
            dve.wait_ge(step, 5)
            dve.tensor_tensor(mask[:, :, :], logit[:, :, :], spread(top[:, :].unsqueeze(2)), ALU.is_equal).then_inc(step, 1)
            dve.wait_ge(ranked, 1)
            dve.tensor_copy(rank[:, :, :].rearrange("p t e -> p (t e)"), ps[:, 1, 0:(NT + 1) * NE]).then_inc(step, 1)
            dve.wait_ge(step, 7)
            dve.scalar_tensor_tensor(out=full[:, :, :], in0=rank[:, NT, :].unsqueeze(2).broadcast_to([P, NE, NT]), scalar=1.0 / P,
                                     in1=count[:, 0:NT].unsqueeze(1).broadcast_to([P, NE, NT]), op0=ALU.mult, op1=ALU.is_gt)\
               .then_inc(step, 1)
            dve.wait_ge(step, 8)
            dve.tensor_reduce(tiles[:, :], full[:, :, :], AX.X, ALU.add).then_inc(step, 1)
            dve.wait_ge(step, 9)
            dve.tensor_tensor_scan(ends[:, :], T["ones"][:, 0:NE], tiles[:, :], 0.0, ALU.mult, ALU.add).then_inc(step, 1)
            dve.wait_ge(step, 10)
            dve.tensor_tensor(tiles[:, :], ends[:, :], tiles[:, :], ALU.subtract).then_inc(step, 1)
            dve.wait_ge(step, 11)
            dve.scalar_tensor_tensor(out=rank[:, 0:NT, :], in0=spread(tiles[:, :].unsqueeze(1)), scalar=float(P),
                                     in1=rank[:, 0:NT, :], op0=ALU.mult, op1=ALU.add).then_inc(step, 1)
            dve.wait_ge(step, 12)
            dve.tensor_tensor(rank[:, 0:NT, :], rank[:, 0:NT, :], mask[:, :, :], ALU.mult).then_inc(step, 1)
            dve.wait_ge(step, 13)
            dve.tensor_reduce(slot[:, :], rank[:, 0:NT, :], AX.X, ALU.add).then_inc(step, 1)
            dve.wait_ge(step, 14)
            dve.tensor_copy(index[:, :], slot[:, :]).then_inc(step, 1)
            dve.tensor_tensor(passed[:, :, :], ends[0:1, :].unsqueeze(1).broadcast_to([1, ST, NE]),
                              count[0:1, :].unsqueeze(2).broadcast_to([1, ST, NE]), ALU.is_le).then_inc(step, 1)
            dve.wait_ge(step, 16)
            dve.tensor_reduce(owner[:, :], passed[:, :, :], AX.X, ALU.add).then_inc(step, 1)
            dve.wait_ge(step, 17)
            dve.tensor_scalar(expert_of[:, 0:ST], owner[:, :], float(NE - 1), None, ALU.min).then_inc(step, 1)

            def gate(s, a, sigmoids):
                dve.wait_ge(a_ready, a)
                dve.wait_ge(sig_ready, sigmoids)
                dve.tensor_tensor(hid[:, s, :], ps[:, s, :], sig[:, s, :], ALU.mult).then_inc(hid_ready, 1)

            gate(0, 1, 2)

            def tile(j, s, i, live):
                dve.wait_ge(hidT_turned, j + 1)
                dve.tensor_copy(hidT[:, s, :, :].rearrange("p f t -> p (f t)"), ps[:, 4, :]).then_inc(hidT_ready, 1)
                if live(1):
                    gate(1 - s, j + 2, j + 3)

            slot_tiles(dve, tile)
            for c in range(NCH):
                dve.wait_ge(turned, c + 1)
                b = c * CH // SEQ
                dve.scalar_tensor_tensor(out=x[:, chunk(c)], in0=ps[:, c, :], scalar=T["mod"][:, 1, 5, b:b + 1],
                                         in1=x[:, chunk(c)], op0=ALU.mult, op1=ALU.add).then_inc(x_ready, 1)


def build(nc, A, out):
    with ExitStack() as whole:
        core = Core(nc, whole)
        T = {}
        for name, shape, dt in [("xT", [P, TOK], F32), ("hT", [P, TOK], F32), ("mean_w", [P, P], F32),
                                ("ones", [P, P], F32), ("ones_bf", [P, P], BF16), ("ident_bf", [P, P], BF16), ("ident", [P, P], F32),
                                ("eps", [P, 1], F32), ("mod", [P, 2, 6, NB], F32), ("gates", [P, NB, N_ACT], F32),
                                ("gate_bo", [P, NB], F32), ("head_index", [1, NB * N_ACT], U32)]:
            T[name] = core.sb(whole, name, shape, dt)
        T["ps"] = whole.enter_context(nc.psum_tensor("ps", [P, 8, CH], F32))
        scratch = lambda n, shape, dt: nc.dram_tensor(n, shape, dt, kind="Internal").ap()
        dram = {"qk": scratch("qk_parts", [3, NP3, NB, P, SEQ], BF16), "table": scratch("table_parts", [NP3, HD + 1, NREL], BF16),
                "const": scratch("const_rows", [3, NP3, SEQ], BF16), "rel": scratch("rel_rows", [2, NT_B, P * NREL], F32)}
        for name in ("h_sorted", "y_sorted"):
            dram[name] = scratch(name, [ST * P, D], F32)
        dram["rows"] = [dram["qk"][a].rearrange("k b r t -> k (b r) t") for a in range(3)]
        bc_dram = nc.dram_tensor("bc_parts", [3, NB, 2, NS, SEQ], BF16, kind="Internal").ap()
        constants_and_modulation(nc, core, T, A)
        layernorm(nc, core, T, "ln0", 0, 0, T["hT"])
        for L in range(NL):
            mamba_layer(nc, core, T, A, L, bc_dram)
        core.reuse_semaphores()
        layernorm(nc, core, T, "ln1", 0, 3, T["hT"], residual=(T["hT"], 0, 2))
        route_heads(nc, core, T, A)
        chosen_heads(nc, core, T, A)
        layernorm(nc, core, T, "ln2", 1, 0, T["hT"])
        second_attention(nc, core, T, A, dram)
        layernorm(nc, core, T, "ln3", 1, 3, T["hT"])
        experts(nc, core, T, A, dram, out)


def layout(inputs):
    import numpy as np
    f = lambda n: np.ascontiguousarray(inputs[n])
    t = lambda a: np.ascontiguousarray(np.moveaxis(a, -1, -2))
    a = {
        "xT": t(f("L0_attn_x").reshape(TOK, D)),
        "c0": t(f("L0_c")), "c1": t(f("L1_c")), "wmod0": f("L0_wmod"), "wmod1": f("L1_wmod"),
        "normw": f("L0_attn_norm_w")[:, :, None],
        "win": t(f("L0_attn_Win")), "wx": t(f("L0_attn_Wx")), "wdt": t(f("L0_attn_Wdt")), "wout": t(f("L0_attn_Wout")),
        "chan": np.concatenate([f("L0_attn_conv_w"), f("L0_attn_conv_b")[..., None], f("L0_attn_bdt")[..., None],
                                f("L0_attn_Dp")[..., None], f("L0_attn_A_log")], axis=-1),
    }
    wqkv1 = f("L1_attn_Wqkv").reshape(H1, 3, HD, D).transpose(3, 1, 0, 2).reshape(D, 3, D)
    bqkv1 = f("L1_attn_bqkv").reshape(H1, 3, HD).transpose(1, 0, 2).reshape(3, D)
    table, tbias = f("L1_attn_Wr"), f("L1_attn_br")
    a.update({
        "wqkv1": wqkv1, "bv1": bqkv1[2:3], "brow": tbias[None, [0, NREL - 1]],
        "cols1": np.stack([bqkv1[0], bqkv1[1], np.tile(table[0], H1), np.tile(table[NREL - 1], H1)], axis=-1),
        "table": np.concatenate([table.T, tbias[None, :]], axis=0),
        "table_edge": np.concatenate([table[0], tbias[0:1]])[:, None],
    })
    heads = [f(f"L0_ffn_W{n}").reshape(D, N_HEAD, DH).transpose(1, 0, 2) for n in "qkv"]
    biases = [f(f"L0_ffn_b{n}").reshape(N_HEAD, DH) for n in "qkv"]
    a.update({
        "wr": f("L0_ffn_Wr"), "br": f("L0_ffn_br")[None, :], "bo": f("L0_ffn_bo")[:, None],
        "wqkv_h": np.concatenate(heads, axis=-1), "bqkv_h": np.stack(biases, axis=-1), "bv_h": biases[2],
        "router_w": f("L1_ffn_router_w"), "router_b": f("L1_ffn_router_b")[None, :], "w1": f("L1_ffn_w1"),
        "biases": np.concatenate([f("L1_ffn_b1"), f("L1_ffn_b2")], 1), "w2": f("L1_ffn_w2"),
        "wo_k": f("L0_ffn_Wo").reshape(N_ACT, DH, D),
    })
    return {k: np.ascontiguousarray(v) for k, v in a.items()}


def kernel(**inputs):
    import numpy as _np
    import concourse.bacc as _bacc
    from concourse import mybir as _mybir
    from concourse.bass_utils import run_bass_kernel_spmd as _run

    nc = _bacc.Bacc("TRN2", target_bir_lowering=False, num_devices=1)
    arrays = layout(inputs)
    aps = {n: nc.dram_tensor(f"in_{n}", a.shape, _mybir.dt.from_np(a.dtype), kind="ExternalInput").ap()
           for n, a in arrays.items()}
    out = nc.dram_tensor("out_xT", (D, TOK), _mybir.dt.float32, kind="ExternalOutput").ap()
    build(nc, aps, out)
    r = _run(nc, [{f"in_{n}": a for n, a in arrays.items()}], core_ids=[0])
    return _np.ascontiguousarray(r.results[0]["out_xT"].T).reshape(NB, SEQ, D)
```
